# Optimizing a Trainium2 kernel written in Bass

```python
import numpy as np
import jax
import jax.numpy as jnp

def _softmax(x, axis=-1):
    return jax.nn.softmax(x, axis=axis)
def _gelu(x):
    return jax.nn.gelu(x, approximate=True)
def _silu(x):
    return jax.nn.silu(x)
def _sigmoid(x):
    return jax.nn.sigmoid(x)
def _layernorm(x, axis=-1, eps=1e-5):
    m = jnp.mean(x, axis=axis, keepdims=True)
    v = jnp.var(x, axis=axis, keepdims=True)
    return (x - m) / jnp.sqrt(v + eps)
def _scatter_add(tgt, idx, src, axis=0):
    return tgt.at[idx].add(src)
def _segment_sum(src, seg, n):
    return jax.ops.segment_sum(src, seg, n)

kernel_name = 'mk_conv_preact_d2_conv_nhwc128_1a83eb'

def setup_inputs(seed: int = 0):
    np.random.seed(seed)
    _w = jnp.asarray
    def _rec_inputs():
        import jax
        import jax.numpy as jnp
        _gk = jax.random.key(seed)
        x = -0.0005207 + 1.001 * jax.random.normal(jax.random.fold_in(_gk, 1), (4, 32, 128, 128), jnp.float32)
        return x
    x = _rec_inputs()
    def _L0_conv_setup():
        import jax, jax.numpy as jnp
        import numpy as np
        N_HEADS = 32
        EPS = 1e-05

        def _inorm(x, w=None, b=None):
            mu = jnp.mean(x, axis=(-2, -1), keepdims=True)
            var = jnp.var(x, axis=(-2, -1), keepdims=True)
            y = (x - mu) * jax.lax.rsqrt(var + EPS)
            if w is not None:
                y = y * w[None, :, None, None] + b[None, :, None, None]
            return y

        def _fourier_resize(x, oh, ow):
            B, C, H, W = x.shape
            if (oh, ow) == (H, W):
                return x
            X = jnp.fft.rfft2(x, norm='forward')
            kh = min(H, oh) // 2
            kw = min(W // 2 + 1, ow // 2 + 1)
            out = jnp.zeros((B, C, oh, ow // 2 + 1), dtype=X.dtype)
            out = out.at[:, :, :kh, :kw].set(X[:, :, :kh, :kw])
            out = out.at[:, :, -kh:, :kw].set(X[:, :, -kh:, :kw])
            return jnp.fft.irfft2(out, s=(oh, ow), norm='forward')

        def _spectral_conv(x, w2, oh, ow):
            w = w2[..., 0] + 1j * w2[..., 1]
            mh = w.shape[2] // 2
            mw = w.shape[3]
            X = jnp.fft.rfft2(x, norm='forward')
            Xk = jnp.concatenate([X[:, :, :mh, :mw], X[:, :, -mh:, :mw]], axis=2)
            Yk = jnp.einsum('bixy,ioxy->boxy', Xk, w)
            B = x.shape[0]
            O = w.shape[1]
            out = jnp.zeros((B, O, oh, ow // 2 + 1), dtype=Yk.dtype)
            out = out.at[:, :, :mh, :mw].set(Yk[:, :, :mh])
            out = out.at[:, :, -mh:, :mw].set(Yk[:, :, mh:])
            return jnp.fft.irfft2(out, s=(oh, ow), norm='forward')

        def _fno_layer(x, conv_w, skip_w, oh, ow, inner_norm=False, act=False):
            skip = jnp.einsum('bixy,oi->boxy', x, skip_w)
            skip = _fourier_resize(skip, oh, ow)
            xf = _spectral_conv(x, conv_w, oh, ow)
            if inner_norm:
                xf = _inorm(xf)
            y = xf + skip
            if act:
                y = jax.nn.gelu(y, approximate=False)
            return y
        key = jax.random.key(seed)
        ks = jax.random.split(key, 16)
        B, T, H, W = (4, 32, 128, 128)

        def cw(k, ci, co, mh2, mw):
            scale = 1.0 / (ci * co)
            return scale * jax.random.normal(k, (ci, co, mh2, mw, 2), jnp.float32)

        def sw(k, co, ci):
            return jax.random.normal(k, (co, ci), jnp.float32) / np.float32(np.sqrt(ci))
        one = jnp.ones((1,), jnp.float32)
        zero = jnp.zeros((1,), jnp.float32)
        return dict(x=jax.random.normal(ks[0], (B, T, H, W), jnp.float32), norm1_w=one, norm1_b=zero, Kcw=cw(ks[1], 1, N_HEADS, 32, 17), Ksw=sw(ks[2], N_HEADS, 1), Qcw=cw(ks[3], 1, N_HEADS, 32, 17), Qsw=sw(ks[4], N_HEADS, 1), Vcw=cw(ks[5], 1, N_HEADS, 32, 17), Vsw=sw(ks[6], N_HEADS, 1), Pcw=cw(ks[7], N_HEADS, 1, 64, 33), Psw=sw(ks[8], 1, N_HEADS), attn_w=one, attn_b=zero, norm2_w=one, norm2_b=zero, m0cw=cw(ks[9], 1, 1, 64, 33), m0sw=sw(ks[10], 1, 1), m1cw=cw(ks[11], 1, 1, 64, 33), m1sw=sw(ks[12], 1, 1), mon_w=one, mon_b=zero)
    _L0_conv_all = _L0_conv_setup()
    _L0_conv_in = {k: v for k, v in _L0_conv_all.items() if k in ('norm1_w', 'norm1_b', 'Kcw', 'Ksw', 'Qcw', 'Qsw', 'Vcw', 'Vsw', 'Pcw', 'Psw', 'attn_w', 'attn_b', 'norm2_w', 'norm2_b', 'm0cw', 'm0sw', 'm1cw', 'm1sw', 'mon_w', 'mon_b', )}
    del _L0_conv_all

    def _L1_conv_setup():
        import jax, jax.numpy as jnp
        import numpy as np
        B, CIN, COUT, H, W = (8, 32, 32, 128, 128)

        def rfftshift(x):
            return jnp.conj(jnp.flip(jnp.fft.fftshift(x, axes=-2), axis=-1))

        def irfftshift(x):
            return jnp.conj(jnp.flip(jnp.fft.ifftshift(x, axes=-2), axis=-1))

        def symmetric_padding(xf_old, im_shape_old, im_shape_new):
            Ho, Wo = im_shape_old
            Hn, Wn = im_shape_new
            ft_h_old = Ho + (1 - Ho % 2)
            ft_w_old = Wo // 2 + 1
            ft_h_new = Hn + (1 - Hn % 2)
            ft_w_new = Wn // 2 + 1
            nlead = xf_old.ndim - 2
            xf = jnp.pad(xf_old, [(0, 0)] * nlead + [(0, ft_h_old - Ho), (0, 0)])
            if Ho % 2 == 0:
                xf = xf.at[..., 0, :].multiply(0.5)
                xf = xf.at[..., -1, :].set(xf[..., 0, :])
            if Wo % 2 == 0:
                xf = xf.at[..., :, 0].multiply(0.5)
            ph = (ft_h_new - ft_h_old) // 2
            pw = ft_w_new - ft_w_old
            xf = jnp.pad(xf, [(0, 0)] * nlead + [(ph, ph), (pw, 0)])
            if Hn % 2 == 0:
                xf = xf.at[..., 0, :].multiply(2.0)
            if Wn % 2 == 0:
                xf = xf.at[..., :, 0].multiply(2.0)
            return xf[..., :Hn, :]
        key = jax.random.key(seed)
        k1, k2, k3 = jax.random.split(key, 3)
        x = jax.random.normal(k1, (B, CIN, H, W), dtype=jnp.float32)
        weight_real = jax.random.uniform(k2, (CIN, COUT, H, W // 2 + 1), dtype=jnp.float32)
        weight_imag = jax.random.uniform(k3, (CIN, COUT, H, W // 2 + 1), dtype=jnp.float32)
        weight_imag = weight_imag.at[:, :, 0, 0].set(0.0)
        return {'x': x, 'weight_real': weight_real, 'weight_imag': weight_imag}
    _L1_conv_all = _L1_conv_setup()
    _L1_conv_in = {k: v for k, v in _L1_conv_all.items() if k in ('weight_real', 'weight_imag', )}
    del _L1_conv_all

    return {
        "x": x,
        "L0_conv_norm1_w": _L0_conv_in["norm1_w"],
        "L0_conv_norm1_b": _L0_conv_in["norm1_b"],
        "L0_conv_Kcw": _L0_conv_in["Kcw"],
        "L0_conv_Ksw": _L0_conv_in["Ksw"],
        "L0_conv_Qcw": _L0_conv_in["Qcw"],
        "L0_conv_Qsw": _L0_conv_in["Qsw"],
        "L0_conv_Vcw": _L0_conv_in["Vcw"],
        "L0_conv_Vsw": _L0_conv_in["Vsw"],
        "L0_conv_Pcw": _L0_conv_in["Pcw"],
        "L0_conv_Psw": _L0_conv_in["Psw"],
        "L0_conv_attn_w": _L0_conv_in["attn_w"],
        "L0_conv_attn_b": _L0_conv_in["attn_b"],
        "L0_conv_norm2_w": _L0_conv_in["norm2_w"],
        "L0_conv_norm2_b": _L0_conv_in["norm2_b"],
        "L0_conv_m0cw": _L0_conv_in["m0cw"],
        "L0_conv_m0sw": _L0_conv_in["m0sw"],
        "L0_conv_m1cw": _L0_conv_in["m1cw"],
        "L0_conv_m1sw": _L0_conv_in["m1sw"],
        "L0_conv_mon_w": _L0_conv_in["mon_w"],
        "L0_conv_mon_b": _L0_conv_in["mon_b"],
        "L1_conv_weight_real": _L1_conv_in["weight_real"],
        "L1_conv_weight_imag": _L1_conv_in["weight_imag"],
    }

def reference(x, L0_conv_norm1_w, L0_conv_norm1_b, L0_conv_Kcw, L0_conv_Ksw, L0_conv_Qcw, L0_conv_Qsw, L0_conv_Vcw, L0_conv_Vsw, L0_conv_Pcw, L0_conv_Psw, L0_conv_attn_w, L0_conv_attn_b, L0_conv_norm2_w, L0_conv_norm2_b, L0_conv_m0cw, L0_conv_m0sw, L0_conv_m1cw, L0_conv_m1sw, L0_conv_mon_w, L0_conv_mon_b, L1_conv_weight_real, L1_conv_weight_imag):
    import jax
    import jax.numpy as jnp
    def _L0_conv_ref(x, norm1_w, norm1_b, Kcw, Ksw, Qcw, Qsw, Vcw, Vsw, Pcw, Psw, attn_w, attn_b, norm2_w, norm2_b, m0cw, m0sw, m1cw, m1sw, mon_w, mon_b):
        import jax, jax.numpy as jnp
        import numpy as np
        N_HEADS = 32
        EPS = 1e-05

        def _inorm(x, w=None, b=None):
            mu = jnp.mean(x, axis=(-2, -1), keepdims=True)
            var = jnp.var(x, axis=(-2, -1), keepdims=True)
            y = (x - mu) * jax.lax.rsqrt(var + EPS)
            if w is not None:
                y = y * w[None, :, None, None] + b[None, :, None, None]
            return y

        def _fourier_resize(x, oh, ow):
            B, C, H, W = x.shape
            if (oh, ow) == (H, W):
                return x
            X = jnp.fft.rfft2(x, norm='forward')
            kh = min(H, oh) // 2
            kw = min(W // 2 + 1, ow // 2 + 1)
            out = jnp.zeros((B, C, oh, ow // 2 + 1), dtype=X.dtype)
            out = out.at[:, :, :kh, :kw].set(X[:, :, :kh, :kw])
            out = out.at[:, :, -kh:, :kw].set(X[:, :, -kh:, :kw])
            return jnp.fft.irfft2(out, s=(oh, ow), norm='forward')

        def _spectral_conv(x, w2, oh, ow):
            w = w2[..., 0] + 1j * w2[..., 1]
            mh = w.shape[2] // 2
            mw = w.shape[3]
            X = jnp.fft.rfft2(x, norm='forward')
            Xk = jnp.concatenate([X[:, :, :mh, :mw], X[:, :, -mh:, :mw]], axis=2)
            Yk = jnp.einsum('bixy,ioxy->boxy', Xk, w)
            B = x.shape[0]
            O = w.shape[1]
            out = jnp.zeros((B, O, oh, ow // 2 + 1), dtype=Yk.dtype)
            out = out.at[:, :, :mh, :mw].set(Yk[:, :, :mh])
            out = out.at[:, :, -mh:, :mw].set(Yk[:, :, mh:])
            return jnp.fft.irfft2(out, s=(oh, ow), norm='forward')

        def _fno_layer(x, conv_w, skip_w, oh, ow, inner_norm=False, act=False):
            skip = jnp.einsum('bixy,oi->boxy', x, skip_w)
            skip = _fourier_resize(skip, oh, ow)
            xf = _spectral_conv(x, conv_w, oh, ow)
            if inner_norm:
                xf = _inorm(xf)
            y = xf + skip
            if act:
                y = jax.nn.gelu(y, approximate=False)
            return y
        B, T, H, W = x.shape
        Hs, Ws = (H // 2, W // 2)
        temperature = 1.0
        xa = x.reshape(B * T, 1, H, W)
        xn = _inorm(xa, norm1_w, norm1_b)
        k = _fno_layer(xn, Kcw, Ksw, Hs, Ws)
        q = _fno_layer(xn, Qcw, Qsw, Hs, Ws)
        v = _fno_layer(xn, Vcw, Vsw, H, W)
        nh = k.shape[1]
        kf = k.reshape(B, T, nh, Hs * Ws).transpose(0, 2, 1, 3)
        qf = q.reshape(B, T, nh, Hs * Ws).transpose(0, 2, 1, 3)
        vf = v.reshape(B, T, nh, H * W).transpose(0, 2, 1, 3)
        scores = jnp.einsum('bntk,bnsk->bnts', qf, kf) / (np.float32(np.sqrt(Hs * Ws)) * temperature)
        p_attn = jax.nn.softmax(scores, axis=-1)
        av = jnp.einsum('bnts,bnsk->bntk', p_attn, vf)
        av = av.reshape(B, nh, T, H, W).transpose(0, 2, 1, 3, 4).reshape(B * T, nh, H, W)
        p = _fno_layer(av, Pcw, Psw, H, W)
        a = _inorm(p + xa, attn_w, attn_b)
        an = _inorm(a, norm2_w, norm2_b)
        m = _fno_layer(an, m0cw, m0sw, H, W, inner_norm=True, act=True)
        m = _fno_layer(m, m1cw, m1sw, H, W, inner_norm=True, act=False)
        out = _inorm(m, mon_w, mon_b) + a
        return out.reshape(B, T, H, W)

    def _L1_conv_ref(x, weight_real, weight_imag):
        import jax, jax.numpy as jnp
        import numpy as np
        B, CIN, COUT, H, W = (8, 32, 32, 128, 128)

        def rfftshift(x):
            return jnp.conj(jnp.flip(jnp.fft.fftshift(x, axes=-2), axis=-1))

        def irfftshift(x):
            return jnp.conj(jnp.flip(jnp.fft.ifftshift(x, axes=-2), axis=-1))

        def symmetric_padding(xf_old, im_shape_old, im_shape_new):
            Ho, Wo = im_shape_old
            Hn, Wn = im_shape_new
            ft_h_old = Ho + (1 - Ho % 2)
            ft_w_old = Wo // 2 + 1
            ft_h_new = Hn + (1 - Hn % 2)
            ft_w_new = Wn // 2 + 1
            nlead = xf_old.ndim - 2
            xf = jnp.pad(xf_old, [(0, 0)] * nlead + [(0, ft_h_old - Ho), (0, 0)])
            if Ho % 2 == 0:
                xf = xf.at[..., 0, :].multiply(0.5)
                xf = xf.at[..., -1, :].set(xf[..., 0, :])
            if Wo % 2 == 0:
                xf = xf.at[..., :, 0].multiply(0.5)
            ph = (ft_h_new - ft_h_old) // 2
            pw = ft_w_new - ft_w_old
            xf = jnp.pad(xf, [(0, 0)] * nlead + [(ph, ph), (pw, 0)])
            if Hn % 2 == 0:
                xf = xf.at[..., 0, :].multiply(2.0)
            if Wn % 2 == 0:
                xf = xf.at[..., :, 0].multiply(2.0)
            return xf[..., :Hn, :]
        weight = jax.lax.complex(weight_real, weight_imag)
        im_shape = (H, W)
        multiplier = symmetric_padding(weight, im_shape, im_shape)
        x_ft = symmetric_padding(rfftshift(jnp.fft.rfft2(x, norm='forward')), im_shape, im_shape)
        out_ft = jnp.einsum('bixy,ioxy->boxy', x_ft, multiplier)
        out = jnp.fft.irfft2(irfftshift(out_ft), s=im_shape, norm='forward')
        return out

    def _gn(v, G=32, eps=1e-5):
        B_, H_, W_, C_ = v.shape
        g = v.reshape(B_, H_, W_, G, C_ // G)
        m = jnp.mean(g, axis=(1, 2, 4), keepdims=True)
        s = jnp.var(g, axis=(1, 2, 4), keepdims=True)
        return ((g - m) / jnp.sqrt(s + eps)).reshape(v.shape)

    def _ln_c(v, eps=1e-6):
        m = jnp.mean(v, axis=-1, keepdims=True)
        s = jnp.var(v, axis=-1, keepdims=True)
        return (v - m) / jnp.sqrt(s + eps)

    def _ln_t(v, eps=1e-5):
        m = jnp.mean(v, axis=-1, keepdims=True)
        s = jnp.var(v, axis=-1, keepdims=True)
        return (v - m) / jnp.sqrt(s + eps)

    def _to_tokens(v):
        B_, H_, W_, C_ = v.shape
        return v.reshape(B_, H_ * W_, C_)
    def _from_tokens(t, like):
        return t.reshape(like.shape)

    x = x + _L0_conv_ref(_gn(x), L0_conv_norm1_w, L0_conv_norm1_b, L0_conv_Kcw, L0_conv_Ksw, L0_conv_Qcw, L0_conv_Qsw, L0_conv_Vcw, L0_conv_Vsw, L0_conv_Pcw, L0_conv_Psw, L0_conv_attn_w, L0_conv_attn_b, L0_conv_norm2_w, L0_conv_norm2_b, L0_conv_m0cw, L0_conv_m0sw, L0_conv_m1cw, L0_conv_m1sw, L0_conv_mon_w, L0_conv_mon_b)
    x = x + _L1_conv_ref(_gn(x), L1_conv_weight_real, L1_conv_weight_imag)
    return x


_drawn_inputs = setup_inputs


def setup_inputs(seed=0):
    import zlib

    import numpy as np

    out = dict(_drawn_inputs(seed))
    spreads = {}
    factors = {'L0_conv_Kcw': 64.0, 'L0_conv_Qcw': 39.53, 'L0_conv_Vcw': 7.85, 'L0_conv_Psw': 2.859}
    for name, (base, spread) in spreads.items():
        noise = np.random.default_rng([zlib.crc32(name.encode()), seed]).standard_normal(out[name].shape)
        drawn = base * np.exp(spread * noise) if base else spread * noise
        out[name] = jnp.asarray(drawn.astype(out[name].dtype))
    for name, factor in factors.items():
        out[name] = (out[name] * factor).astype(out[name].dtype)
    return out
```

```python
import math

import numpy as np

import concourse.bass as bass
from concourse import mybir
from contextlib import ExitStack

F32 = mybir.dt.float32
ALU = mybir.AluOpType
ACT = mybir.ActivationFunctionType
AX = mybir.AxisListType

NB, NT, NHD = 4, 32, 32
HH = WW = 128
NI = NB * NT
NG = 32
KW, KH = 33, 64
M2 = KW * KH
RW, RH = 17, 32
NCH = (RW + 1) // 2
GI = 8
NGRP = NI // GI
GPB = NT // GI
EPS = 1e-5
KWF = WW // 2 + 1
NBLK = 12
MB = M2 // NBLK
PB = 4
NCK = NHD // PB
SL = 4
NSLAB = HH // 2 // SL
SM = SL * KWF
SCALARS = ["norm1_w", "norm1_b", "attn_w", "attn_b", "norm2_w", "norm2_b", "m0sw", "m1sw", "mon_w", "mon_b"]


def constants():
    c = {}
    n = np.arange(128)
    k = np.concatenate([np.arange(32), np.arange(-32, 0)])
    j = np.arange(KW)
    ph = 2 * np.pi * np.outer(n, k) / 128
    c["fh"] = np.concatenate([np.cos(ph), -np.sin(ph)], 1) / 128
    th = 2 * np.pi * np.outer(n, j) / 128
    c["fw1"] = np.stack([np.cos(th), -np.sin(th)], 2).reshape(128, -1) / 128
    c["fw2"] = np.stack([np.sin(th), np.cos(th)], 2).reshape(128, -1) / 128
    c["eh"] = np.concatenate([np.cos(ph).T, -np.sin(ph).T], 0)
    wt = np.where(j == 0, 1.0, 2.0)[:, None]
    c["cw"] = np.concatenate([wt * np.cos(th).T, -wt * np.sin(th).T], 0)
    c["ident"] = np.eye(128)
    c["ones"] = np.ones((128, 128))
    b = np.arange(128) // 32
    c["bmean"] = (b[:, None] == b[None, :]) / 32.0
    c["sel"] = (np.arange(128)[:, None] == 32 * np.arange(4)[None, :]) * 1.0
    c["gmean"] = (n[:, None] // 4 == n[None, :] // 4) / 4.0
    def sym(rows_in, rows_out):
        m = np.zeros((2, len(rows_in), 2, len(rows_out)))
        for a, ki in enumerate(rows_in):
            for o, ko in enumerate(rows_out):
                for s in (0, 1):
                    if ki == ko:
                        m[s, a, s, o] += 0.5
                    if ki == -ko:
                        m[s, a, s, o] += 0.5 if s == 0 else -0.5
        return m.reshape(2 * len(rows_in), 2 * len(rows_out))
    c["sym"] = sym(k, k)
    kr = np.concatenate([np.arange(16), np.arange(-16, 0)])
    c["symv"] = sym(kr, k)
    c["symr"] = sym(kr, kr)
    cm = np.zeros((128, NCH))
    for ch in range(NCH):
        for h in range(2):
            kw = 2 * ch + h
            w = np.full(32, 2.0) if kw else np.where(kr == -16, 2.0, 1.0)
            if kw < RW:
                cm[64 * h:64 * h + 64, ch] = 64 * np.concatenate([w, w])
    c["cm"] = cm
    wg = np.zeros((128, KW))
    inside = (k >= -16) & (k < 16)
    for kw in range(KW):
        if kw == 0:
            w = np.where(np.abs(k) <= 16, 0.0, 1.0)
            wg[:, 0] = np.concatenate([w, np.where(k == -32, 0.0, w)])
        elif kw < 32:
            w = np.where(inside, 0.0, 2.0) if kw < RW else np.full(64, 2.0)
            wg[:, kw] = np.concatenate([w, w])
    c["wg"] = 64 * wg
    s = sym(k, k)
    r = list(k).index(-32)
    s[:, r] = 0
    s[:, 64 + r] = 0
    s[r, r] = 1
    c["ny"] = 64 * (s @ s.T)
    ka, kb = np.arange(65), np.arange(1, 64)
    c["qh"] = np.concatenate([np.cos(2 * np.pi * np.outer(n, ka) / 128), np.sin(2 * np.pi * np.outer(n, kb) / 128)], 1) / 128
    kf = np.arange(KWF)
    tf = 2 * np.pi * np.outer(n, kf) / 128
    cc, ss = np.cos(tf) / 128, np.sin(tf) / 128
    c["wa"] = np.concatenate([cc, -ss], 1)
    c["wb8"] = np.concatenate([-ss, -cc], 1)
    slot = np.concatenate([np.arange(64), -np.arange(1, 65)])
    ps = 2 * np.pi * np.outer(slot, n) / 128
    c["e1"] = np.concatenate([np.cos(ps), np.sin(ps)], 1)
    c["e2"] = np.concatenate([-np.sin(ps), np.cos(ps)], 1)
    wf = np.where((kf == 0) | (kf == 64), 1.0, 2.0)[:, None]
    c["cc"] = wf * np.cos(tf).T
    c["cs"] = -wf * np.sin(tf).T
    return {k2: np.ascontiguousarray(v, dtype=np.float32) for k2, v in c.items()}


def bc(ap, dim, n):
    v = ap.unsqueeze(dim)
    shape = list(v.shape)
    shape[dim] = n
    return v.broadcast_to(shape)


class Chain:

    def __init__(self, eng, sem):
        self.eng, self.sem, self.n = eng, sem, 0

    def link(self, ins):
        self.n += 1
        ins.then_inc(self.sem, 1)
        self.eng.wait_ge(self.sem, self.n)


class Root:

    def __init__(self, asked, given):
        self.asked, self.given, self.n, self.m = asked, given, 0, 0

    def rsqrt(self, dve, ch, V, out, var):
        self.n += 1
        V.tensor_scalar(out, var, EPS, None, ALU.add).then_inc(self.asked, 1)
        dve.wait_ge(self.given, self.n)
        ch.link(V.reciprocal(out, out))

    def serve(self, act, A, out):
        self.m += 1
        act.wait_ge(self.asked, self.m)
        A.activation(out, out, ACT.Sqrt).then_inc(self.given, 1)


def nth(b, u):
    return GPB // 2 * b + u // 2


def wait(eng, sem, value):
    if not (isinstance(value, int) and value <= 0):
        eng.wait_ge(sem, value)


def per_batch(eng, body):
    body(0)
    with eng.Fori(1, NB) as b:
        body(b)


def build(nc, a, c, out):
    x = a["x"].rearrange("b t h w -> (b t) h w")
    xf = x.rearrange("i h w -> i (h w)")
    xo = out.rearrange("b t h w -> (b t) h w")

    def dram(name, shape):
        return nc.dram_tensor(name, shape, F32, kind="Internal").ap()

    xs = dram("xs", (NI, 2 * KW, KH))
    xns = dram("xns", (NI, 2, M2))
    wv = dram("wv", (PB, NBLK, NCK, 2, MB))
    mixd = dram("mixd", (NI, HH, WW))
    pspec = dram("pspec", (NI, 2, M2))
    ys = dram("ys", (NI, 2 * KW, KH))
    x1s = dram("x1s", (3, NI, HH, KWF))
    os_ = dram("os_", (NT, NB, 2, HH, KWF))

    top = ExitStack()
    names, held = set(), []

    def sems(name, n):
        return [sem(f"{name}_{i}") for i in range(n)]

    def sem(name):
        assert name not in names
        names.add(name)
        held.append(nc.alloc_semaphore(name=name))
        return held[-1]

    def recycle():
        with nc.Block() as block:
            @block.gpsimd
            def _(pool):
                for h in held:
                    pool.sem_clear(h)
        while held:
            nc.release_semaphore(held.pop())

    with top:
        def keep(name, shape):
            return top.enter_context(nc.sbuf_tensor(name, shape, F32))

        fh = keep("fh", [128, 128])
        fw1 = keep("fw1", [128, 2 * KW])
        fw2 = keep("fw2", [128, 2 * KW])
        eh = keep("eh", [128, 128])
        cw = keep("cw", [2 * KW, 128])
        ident = keep("ident", [128, 128])
        ones = keep("ones", [128, 128])
        bmean = keep("bmean", [128, 128])
        sel = keep("sel", [128, 4])
        sym = keep("sym", [128, 128])
        sc = keep("sc", [128, len(SCALARS)])
        vec = keep("vec", [128, 64])
        kept = [("fh", fh), ("fw1", fw1), ("fw2", fw2), ("eh", eh), ("cw", cw), ("ident", ident),
                ("ones", ones), ("bmean", bmean), ("sel", sel), ("sym", sym)]
        scalar = {n: sc[:, i:i + 1] for i, n in enumerate(SCALARS)}
        vnames = {}
        mt = keep("mt", [128, NI])
        c1b = keep("c1b", [128, NI])
        c2b = keep("c2b", [128, NI])

        def v1(name):
            i = vnames.setdefault(name, len(vnames))
            return vec[:, i:i + 1]

        s_const = sem("const_loaded")
        att = ExitStack()
        xa = att.enter_context(nc.sbuf_tensor("xa", [128, HH * WW], F32))
        gt = att.enter_context(nc.sbuf_tensor("gt", [128, NCH, 2, NHD], F32))
        vpb = att.enter_context(nc.sbuf_tensor("vpb", [128, NHD], F32))
        qkb = att.enter_context(nc.sbuf_tensor("qkb", [128, NHD], F32))

        with ExitStack() as p1:
            def sb(name, shape):
                return p1.enter_context(nc.sbuf_tensor(name, shape, F32))

            def pb(name, shape):
                return p1.enter_context(nc.psum_tensor(name, shape, F32))

            xd = sb("xd", [128, GPB, GI * WW])
            yb = sb("yb", [128, 2, 2, GI, KH])
            xst = sb("xst", [2 * KW, 2, GI, KH])
            st = sb("st", [128, NG, 6])
            mv = sb("mv", [128, NG, 2])
            me = sb("me", [128, 2, NG])
            gs = sb("gs", [128, 4, NG])
            rw = sb("rw", [128, 2, WW])
            rt = sb("rt", [128, 2, NB])
            tmpg = sb("tmpg", [128, 2, NG])
            praw = sb("praw", [NHD, KH, KW, 2])
            pr = sb("pr", [NHD, 2, KW, KH])
            vf = sb("vf", [NHD, 2, KW, KH])
            wt = praw[:, :, :, :].rearrange("n h w r -> n (h w r)").rearrange("n (r w h) -> n r w h", r=2, w=KW)
            kvq = sb("kvq", [NHD, 3, RH * RW * 2])
            kq = sb("kq", [NHD, 2, 2, RW, RH])
            col = sb("col", [NHD, 3, 2, RH])
            colt = sb("colt", [2 * RH, 3, NHD])
            gg = sb("gg", [NHD, 2, RW + 1, 2, RH])
            hs = sb("hs", [NHD, 4])
            rows = sb("rows", [128, 4, NHD])
            symv = sb("symv", [2 * RH, 2 * KH])
            symr = sb("symr", [2 * RH, 2 * RH])
            cm = sb("cm", [128, NCH])
            f1 = [pb(f"f1_{i}", [128, GI * 128]) for i in range(2)]
            f2 = [pb(f"f2_{i}", [2 * KW, GI * KH]) for i in range(2)]
            pg = pb("pg", [128, 512])
            pw = pb("pw", [128, 512])

            s_x = sem("image_rows_loaded")
            s_xd = sems("row_group_loaded", GPB)
            s_w = sem("weights_loaded")
            s_f1 = sem("h_transform_done")
            s_e1 = sem("h_transform_copied")
            s_f2 = sem("w_transform_done")
            s_e2 = sem("w_transform_copied")
            s_xs = sems("spectrum_stored", 2)
            s_c1 = sem("p1_vector_steps")
            s_me = sem("local_moments_ready")
            s_gm = sem("group_moments_ready")
            s_rw = sem("scale_rows_ready")
            s_rt = sem("scales_by_column_ready")
            s_rts = sem("scales_copied")
            s_dc = sem("p1_scalar_steps")
            s_col = sem("weight_columns_ready")
            s_ct = sem("weight_columns_transposed")
            s_cts = sem("weight_columns_copied")
            s_sy = sem("weight_columns_symmetrised")
            s_gg = sem("score_weights_ready")
            s_gt = sem("score_weights_transposed")
            s_gts = sem("score_weights_copied")
            s_wt = sem("value_weights_ready")
            s_wv = sem("value_weights_stored")
            root = Root(sem("p1_root_asked"), sem("p1_root_given"))
            NW = 3 + 4 + 4 + 4
            block = p1.enter_context(nc.Block())

            @block.sync
            def _(sp):
                for i in range(4):
                    n = HH * WW // 4
                    sp.dma_start(xa[:, i * n:(i + 1) * n], xf[:, i * n:(i + 1) * n]).then_inc(s_x, 16)

                def load(b):
                    for u in range(GPB):
                        wait(sp, s_f1, GPB * b + u + 1 - GPB)
                        sp.dma_start(xd[:, u, :].rearrange("h (g w) -> h g w", g=GI),
                                     x[bass.ds((b * GPB + u) * GI, GI)].rearrange("g h w -> h g w")).then_inc(s_xd[u], 16)
                per_batch(sp, load)
                sp.wait_ge(s_wt, 1)
                wf = wt.rearrange("n r w h -> n r (w h)").rearrange("n r (q m) -> n r q m", m=MB)
                for k in range(NCK):
                    for r in range(2):
                        sp.dma_start(wv[:, :, k, r], wf[PB * k:PB * k + PB, r]).then_inc(s_wv, 16)
                sp.wait_ge(s_wv, 16 * 2 * NCK)

            @block.gpsimd
            def _(pool):
                def store(b):
                    for u in range(GPB):
                        g = GPB * b + u
                        pool.wait_ge(s_e2, g + 1)
                        pool.dma_start(xs[bass.ds(g * GI, GI)].rearrange("i m k -> m i k"),
                                       xst[:, u % 2]).then_inc(s_xs[u % 2], 16)
                per_batch(pool, store)
                for q in s_xs:
                    pool.wait_ge(q, 16 * NGRP // 2)

            @block.scalar
            def _(act):
                for n, t in kept:
                    act.dma_start(t[:, :], c[n]).then_inc(s_const, 16)
                for i, n in enumerate(SCALARS):
                    src = a["L0_conv_" + n]
                    act.dma_start(sc[:, i:i + 1], bass.AP(src.tensor, 0, [[0, 128], [1, 1]])).then_inc(s_const, 16)
                for t, n in ((symv, "symv"), (symr, "symr"), (cm, "cm")):
                    act.dma_start(t[:, :], c[n]).then_inc(s_w, 16)
                for i, n in enumerate(("Ksw", "Qsw", "Vsw", "Psw")):
                    src = a["L0_conv_" + n]
                    act.dma_start(hs[:, i:i + 1], bass.AP(src.tensor, 0, [[1, NHD], [1, 1]])).then_inc(s_w, 16)
                    act.dma_start(rows[:, i, :], bass.AP(src.tensor, 0, [[0, 128], [1, NHD]])).then_inc(s_w, 16)
                for i, n in enumerate(("Kcw", "Qcw", "Vcw")):
                    act.dma_start(kvq[:, i, :], a["L0_conv_" + n].rearrange("a n h w r -> (a n) (h w r)")).then_inc(s_w, 16)
                act.dma_start(praw[:, :, :, :], a["L0_conv_Pcw"].rearrange("n a h w r -> (n a) h w r")).then_inc(s_w, 16)
                root.serve(act, nc.scalar, gs[:, 2, :])
                act.wait_ge(s_rts, 1)
                root.serve(act, nc.scalar, v1("alpha"))
                dc = [0]

                def copy_w(b, u):
                    g = GPB * b + u
                    act.wait_ge(s_f2, g + 1)
                    wait(act, s_xs[u % 2], 16 * nth(b, u))
                    act.activation(xst[:, u % 2], f2[u % 2][:, :].rearrange("m (i k) -> m i k", i=GI),
                                   ACT.Copy).then_inc(s_e2, 1)

                def copy(b):
                    for u in range(GPB):
                        g = GPB * b + u
                        act.wait_ge(s_f1, g + 1)
                        wait(act, s_f2, g - 1)
                        act.activation(yb[:, u % 2], f1[u % 2][:, :].rearrange("w (i r k) -> w r i k", i=GI, r=2),
                                       ACT.Copy, scale=rt[:, 0, b:b + 1]).then_inc(s_dc, 1)
                        act.wait_ge(s_dc, g + 1)
                        act.activation(yb[:, u % 2, 0, :, 0:1], yb[:, u % 2, 0, :, 0:1],
                                       ACT.Identity, bias=rt[:, 1, b:b + 1]).then_inc(s_e1, 1)
                        if u:
                            copy_w(b, u - 1)
                        elif not (isinstance(b, int) and b == 0):
                            copy_w(b - 1, GPB - 1)
                for b in range(NB):
                    copy(b)
                copy_w(NB - 1, GPB - 1)

            @block.tensor
            def _(pe):
                pe.wait_ge(s_const, 16 * (len(kept) + len(SCALARS)))
                pe.wait_ge(s_me, 1)
                nc.tensor.matmul(pg[:, 0:2 * NG], bmean[:, :], me[:, :, :].rearrange("p a g -> p (a g)"),
                                 start=True, stop=True).then_inc(s_gm, 1)
                pe.wait_ge(s_rw, 1)
                for i in range(2):
                    m = nc.tensor.matmul(pg[:, 128 + 4 * i:132 + 4 * i], rw[:, i, :], sel[:, :],
                                         start=True, stop=True)
                m.then_inc(s_rt, 1)

                def w_transform(b, u):
                    g = GPB * b + u
                    pe.wait_ge(s_e1, g + 1)
                    wait(pe, s_e2, g - 1)
                    for r, f in enumerate((fw1, fw2)):
                        m = nc.tensor.matmul(f2[u % 2][:, :], f[:, :],
                                             yb[:, u % 2, r].rearrange("w i k -> w (i k)"),
                                             start=(r == 0), stop=(r == 1))
                    m.then_inc(s_f2, 1)

                def transform(b):
                    for u in range(GPB):
                        g = GPB * b + u
                        pe.wait_ge(s_xd[u], 16 * (b + 1))
                        wait(pe, s_e1, g - 1)
                        for i in range(GI):
                            m = nc.tensor.matmul(f1[u % 2][:, 128 * i:128 * i + 128],
                                                 xd[:, u, WW * i:WW * i + WW], fh[:, :], start=True, stop=True)
                        m.then_inc(s_f1, 1)
                        if u:
                            w_transform(b, u - 1)
                        elif not (isinstance(b, int) and b == 0):
                            w_transform(b - 1, GPB - 1)
                per_batch(pe, transform)
                w_transform(NB - 1, GPB - 1)
                pe.wait_ge(s_col, 1)
                for i in range(3):
                    m = nc.tensor.transpose(pw[0:2 * RH, 32 * i:32 * i + 32],
                                            col[:, i].rearrange("n r h -> n (r h)"), ident[0:NHD, 0:NHD])
                m.then_inc(s_ct, 1)
                pe.wait_ge(s_cts, 1)
                nc.tensor.matmul(pw[0:NHD, 128:192], colt[:, 0, :], symr[:, :], start=True, stop=True)
                nc.tensor.matmul(pw[0:NHD, 192:256], colt[:, 1, :], symr[:, :], start=True, stop=True)
                nc.tensor.matmul(pw[0:NHD, 256:384], colt[:, 2, :], symv[:, :], start=True, stop=True).then_inc(s_sy, 1)
                pe.wait_ge(s_gg, 1)
                for ch in range(NCH):
                    for r in range(2):
                        m = nc.tensor.transpose(f1[r][:, 32 * ch:32 * ch + 32],
                                                gg[:, r, 2 * ch:2 * ch + 2].rearrange("n w d h -> n (w d h)"),
                                                ident[0:NHD, 0:NHD])
                m.then_inc(s_gt, 1)

            @block.vector
            def _(dve):
                ch = Chain(dve, s_c1)
                V = nc.vector
                dve.wait_ge(s_x, 64)
                xv = xa[:, :].rearrange("p (h g q) -> p g h q", g=NG, q=4)
                for g in range(NG):
                    s = V.bn_stats(st[:, g, :], xv[:, g])
                ch.link(s)
                for g in range(NG):
                    s = V.bn_aggr(mv[:, g, :], st[:, g, :])
                ch.link(s)
                ch.link(V.tensor_copy(me[:, 0, :], mv[:, :, 0]))
                ch.link(V.tensor_tensor(me[:, 1, :], mv[:, :, 0], mv[:, :, 0], ALU.mult))
                V.tensor_tensor(me[:, 1, :], me[:, 1, :], mv[:, :, 1], ALU.add).then_inc(s_me, 1)
                dve.wait_ge(s_gm, 1)
                ch.link(V.tensor_copy(gs[:, 0:2, :], pg[:, 0:2 * NG].rearrange("p (a g) -> p a g", a=2)))
                ch.link(V.tensor_tensor(gs[:, 2, :], gs[:, 0, :], gs[:, 0, :], ALU.mult))
                ch.link(V.tensor_tensor(gs[:, 2, :], gs[:, 1, :], gs[:, 2, :], ALU.subtract))
                root.rsqrt(dve, ch, V, gs[:, 2, :], gs[:, 2, :])
                ch.link(V.tensor_tensor(gs[:, 3, :], gs[:, 0, :], gs[:, 2, :], ALU.mult))
                ch.link(V.tensor_scalar(gs[:, 3, :], gs[:, 3, :], -1.0, None, ALU.mult))
                ch.link(V.tensor_copy(rw[:, 0, :].rearrange("p (g q) -> p g q", q=4), bc(gs[:, 2, :], 2, 4)))
                V.tensor_copy(rw[:, 1, :].rearrange("p (g q) -> p g q", q=4), bc(gs[:, 3, :], 2, 4)).then_inc(s_rw, 1)
                dve.wait_ge(s_rt, 1)
                V.tensor_copy(rt[:, :, :], pg[:, 128:136].rearrange("p (a b) -> p a b", a=2)).then_inc(s_rts, 1)
                ch.link(V.tensor_tensor(tmpg[:, 0, :], me[:, 0, :], gs[:, 2, :], ALU.mult))
                ch.link(V.tensor_tensor(tmpg[:, 0, :], tmpg[:, 0, :], gs[:, 3, :], ALU.add))
                ch.link(V.reduce_sum(v1("mean"), tmpg[:, 0, :], axis=AX.X))
                ch.link(V.tensor_scalar(v1("mean"), v1("mean"), 1.0 / NG, None, ALU.mult))
                ch.link(V.tensor_scalar(tmpg[:, 0, :], tmpg[:, 0, :], v1("mean"), None, ALU.subtract))
                ch.link(V.tensor_tensor(tmpg[:, 0, :], tmpg[:, 0, :], tmpg[:, 0, :], ALU.mult))
                ch.link(V.tensor_tensor(tmpg[:, 1, :], gs[:, 2, :], gs[:, 2, :], ALU.mult))
                ch.link(V.tensor_tensor(tmpg[:, 1, :], tmpg[:, 1, :], mv[:, :, 1], ALU.mult))
                ch.link(V.tensor_tensor(tmpg[:, 0, :], tmpg[:, 0, :], tmpg[:, 1, :], ALU.add))
                ch.link(V.reduce_sum(v1("alpha"), tmpg[:, 0, :], axis=AX.X))
                ch.link(V.tensor_scalar(v1("alpha"), v1("alpha"), 1.0 / NG, None, ALU.mult))
                root.rsqrt(dve, ch, V, v1("alpha"), v1("alpha"))
                dve.wait_ge(s_const, 16 * (len(kept) + len(SCALARS)))
                ch.link(V.tensor_tensor(v1("alpha"), v1("alpha"), scalar["norm1_w"], ALU.mult))
                ch.link(V.tensor_tensor(v1("beta"), v1("alpha"), v1("mean"), ALU.mult))
                ch.link(V.tensor_tensor(v1("beta"), scalar["norm1_b"], v1("beta"), ALU.subtract))
                xg = xa[:, :].rearrange("p (h w) -> p h w", w=WW)
                for i in range(4):
                    q = xg[:, 32 * i:32 * i + 32, :]
                    ch.link(V.tensor_tensor(q, q, bc(rw[:, 0, :], 1, 32), ALU.mult))
                    ch.link(V.tensor_tensor(q, q, bc(rw[:, 1, :], 1, 32), ALU.add))
                dve.wait_ge(s_w, 16 * NW)
                kv = [kvq[:, i, :].rearrange("n (h w r) -> n r w h", h=RH, w=RW) for i in range(3)]
                for i in range(3):
                    s = V.tensor_copy(col[:, i], kv[i][:, :, 0, :])
                s.then_inc(s_col, 1)
                for i in range(2):
                    for r in range(2):
                        s = V.tensor_copy(kq[:, i, r], kv[i][:, r])
                V.memset(vf[:, :, :, :], 0.0)
                for r in range(2):
                    s = V.tensor_copy(pr[:, r], praw[:, :, :, r].rearrange("n h w -> n w h"))
                ch.link(s)
                V.tensor_copy(vf[:, :, 1:RW, 0:16], kv[2][:, :, 1:RW, 0:16])
                V.tensor_copy(vf[:, :, 1:RW, 48:64], kv[2][:, :, 1:RW, 16:32])
                dve.wait_ge(s_ct, 1)
                V.tensor_copy(colt[:, :, :], pw[0:2 * RH, 0:96].rearrange("m (i n) -> m i n", i=3)).then_inc(s_cts, 1)
                dve.wait_ge(s_sy, 1)
                for i in range(2):
                    s = V.tensor_copy(kq[:, i, :, 0, :], pw[0:NHD, 128 + 64 * i:192 + 64 * i].rearrange("n (r h) -> n r h", r=2))
                ch.link(V.tensor_copy(vf[:, :, 0, :], pw[0:NHD, 256:384].rearrange("n (r h) -> n r h", r=2)))
                for i in range(2):
                    ch.link(V.tensor_scalar(kq[:, i, 0], kq[:, i, 0], hs[:, i:i + 1], None, ALU.add))
                K, Q = kq[:, 0], kq[:, 1]
                ch.link(V.memset(gg[:, :, RW:RW + 1], 0.0))
                t0, t1 = kvq[:, 0, 0:RW * RH].rearrange("n (w h) -> n w h", w=RW), kvq[:, 1, 0:RW * RH].rearrange("n (w h) -> n w h", w=RW)
                ch.link(V.tensor_tensor(t0, Q[:, 0], K[:, 0], ALU.mult))
                ch.link(V.tensor_tensor(t1, Q[:, 1], K[:, 1], ALU.mult))
                ch.link(V.tensor_tensor(gg[:, 0, 0:RW, 0], t0, t1, ALU.add))
                ch.link(V.tensor_tensor(t0, Q[:, 1], K[:, 0], ALU.mult))
                ch.link(V.tensor_tensor(t1, Q[:, 0], K[:, 1], ALU.mult))
                ch.link(V.tensor_tensor(gg[:, 1, 0:RW, 0], t0, t1, ALU.subtract))
                V.tensor_copy(gg[:, :, 0:RW, 1], gg[:, :, 0:RW, 0]).then_inc(s_gg, 1)
                vs, psk = hs[:, 2:3], hs[:, 3:4]
                ch.link(V.tensor_scalar(wt[:, 0], vf[:, 0], vs, None, ALU.add))
                ch.link(V.tensor_tensor(wt[:, 1], pr[:, 1], wt[:, 0], ALU.mult))
                ch.link(V.tensor_tensor(wt[:, 0], pr[:, 0], wt[:, 0], ALU.mult))
                ch.link(V.tensor_tensor(pr[:, 0], pr[:, 0], vf[:, 1], ALU.mult))
                ch.link(V.tensor_tensor(pr[:, 1], pr[:, 1], vf[:, 1], ALU.mult))
                ch.link(V.tensor_tensor(wt[:, 0], wt[:, 0], pr[:, 1], ALU.subtract))
                ch.link(V.tensor_tensor(wt[:, 1], wt[:, 1], pr[:, 0], ALU.add))
                ch.link(V.tensor_scalar(vf[:, :, :, :], vf[:, :, :, :], psk, None, ALU.mult))
                V.tensor_tensor(wt, wt, vf[:, :, :, :], ALU.add).then_inc(s_wt, 1)
                ch.link(V.tensor_tensor(qkb[:, :], rows[:, 0, :], rows[:, 1, :], ALU.mult))
                ch.link(V.tensor_tensor(vpb[:, :], rows[:, 2, :], rows[:, 3, :], ALU.mult))
                dve.wait_ge(s_gt, 1)
                for k in range(NCH):
                    for r in range(2):
                        s = V.tensor_scalar(gt[:, k, r, :], f1[r][:, 32 * k:32 * k + 32], cm[:, k:k + 1], None, ALU.mult)
                ch.link(s)

        pt = att.enter_context(nc.sbuf_tensor("pt", [128, NCK, NI], F32))
        npt = att.enter_context(nc.sbuf_tensor("npt", [128, NCK, NI], F32))
        with ExitStack() as p2:
            def sb(name, shape):
                return p2.enter_context(nc.sbuf_tensor(name, shape, F32))

            def pb(name, shape):
                return p2.enter_context(nc.psum_tensor(name, shape, F32))

            xt = sb("xt", [128, KW, 2, KH])
            xr = sb("xr", [128, 2, RW, 2, RH])
            xrm = sb("xrm", [128, 2, NCH, NI])
            xg = sb("xg", [128, 2, 2, NI])
            z = sb("z", [128, 2, NB, 16, NT])
            gram = sb("gram", [128, NT])
            wg = sb("wg", [128, KW])
            ny = sb("ny", [128, 128])
            sco = sb("sco", [128, NHD, NT])
            ex = sb("ex", [128, NHD, NT])
            mx = sb("mx", [128, NHD])
            am = sb("am", [128, NT])
            ad = sb("ad", [128, NI])
            at = sb("at", [128, NI])
            tp = [pb(f"tp{i}", [128, 512]) for i in range(2)]
            pgr = pb("pgr", [128, 512])
            psc = pb("psc", [128, 1024])
            pny = pb("pny", [128, 512])

            s_xt = sem("spectrum_loaded")
            s_wg = sem("gram_weights_loaded")
            s_xn = sem("spectrum_normed")
            s_xns = sem("normed_spectrum_stored")
            s_c2 = sem("p2_vector_steps")
            s_t = sem("gram_chunk_transposed")
            s_tc = sem("gram_chunk_copied")
            s_tw = sem("gram_chunk_weighted")
            s_ny = sem("nyquist_chunk_weighted")
            s_gr = sem("gram_done")
            s_r = sem("region_chunk_transposed")
            s_rc = sem("region_chunk_copied")
            s_z = sem("score_products_ready")
            s_zu = sem("score_products_used")
            s_mx = sem("scores_less_maximum")
            s_ex = sem("exponentials_ready")
            s_p = sem("probabilities_ready")
            s_pt = sem("probabilities_transposed")
            s_ptc = sem("probabilities_copied")
            s_a = sem("skip_mixing_ready")
            s_at = sem("skip_mixing_transposed")
            s_atc = sem("skip_mixing_copied")
            s_cb = sem("mixed_offset_ready")
            block = p2.enter_context(nc.Block())
            NZ = 4 * NCH

            @block.sync
            def _(sp):
                sp.dma_start(xt[:, :, :, :].rearrange("p w r h -> p (w r h)"), xs.rearrange("i m k -> i (m k)")).then_inc(s_xt, 16)
                sp.dma_start(wg[:, :], c["wg"]).then_inc(s_wg, 16)
                sp.dma_start(ny[:, :], c["ny"]).then_inc(s_wg, 16)
                sp.wait_ge(s_xn, 1)
                for r in range(2):
                    sp.dma_start(xns[:, r].rearrange("i (w h) -> i w h", w=KW), xt[:, :, r, :]).then_inc(s_xns, 16)
                sp.wait_ge(s_xns, 32)

            @block.scalar
            def _(act):
                act.wait_ge(s_wg, 32)
                for kw in range(KW):
                    act.wait_ge(s_tc, kw + 1)
                    wait(act, s_gr, kw - 1)
                    if kw < KW - 1:
                        act.activation(xg[:, kw % 2, 1, :], xg[:, kw % 2, 0, :], ACT.Copy, scale=wg[:, kw:kw + 1]).then_inc(s_tw, 1)
                    else:
                        act.wait_ge(s_ny, 1)
                        act.activation(xg[:, kw % 2, 1, :], pny[:, 0:NI], ACT.Copy).then_inc(s_tw, 1)
                act.wait_ge(s_mx, 1)
                act.activation(ex[:, :, :], sco[:, :, :], ACT.Exp).then_inc(s_ex, 1)
                act.wait_ge(s_ptc, 1)
                act.activation(npt[:, :, :], pt[:, :, :], ACT.Copy, scale=-1.0).then_inc(s_ex, 1)
                act.wait_ge(s_ex, 2)

            @block.tensor
            def _(pe):
                pe.wait_ge(s_xn, 1)
                def gram_step(kw):
                    pe.wait_ge(s_tc, kw + 1)
                    if kw == KW - 1:
                        nc.tensor.matmul(pny[:, 0:NI], ny[:, :], xg[:, kw % 2, 0, :], start=True, stop=True).then_inc(s_ny, 1)
                    pe.wait_ge(s_tw, kw + 1)
                    nc.tensor.matmul(pgr[:, 0:NI], xg[:, kw % 2, 0, :], xg[:, kw % 2, 1, :],
                                     start=(kw == 0), stop=(kw == KW - 1)).then_inc(s_gr, 1)
                for kw in range(KW):
                    if kw >= 2:
                        pe.wait_ge(s_tc, kw - 1)
                        pe.wait_ge(s_tw, kw - 1)
                    nc.tensor.transpose(tp[kw % 2][:, 0:NI], xt[:, kw].rearrange("p r h -> p (r h)"), ident[:, :]).then_inc(s_t, 1)
                    if kw:
                        gram_step(kw - 1)
                gram_step(KW - 1)
                for i in range(2 * NCH):
                    v, k = i // NCH, i % NCH
                    n = 64 * min(2, RW - 2 * k)
                    wait(pe, s_rc, i - 1)
                    nc.tensor.transpose(tp[i % 2][0:n, 0:NI], xr[:, v, 2 * k:2 * k + n // 64].rearrange("p w r h -> p (w r h)"),
                                        ident[:, :]).then_inc(s_r, 1)
                for j in range(NZ):
                    k, half, v = j // 4, (j // 2) % 2, j % 2
                    n = 64 * min(2, RW - 2 * k)
                    pe.wait_ge(s_z, j + 1)
                    for b in range(NB):
                        m = nc.tensor.matmul(psc[32 * b:32 * b + 32, 512 * half:512 * half + 512],
                                             xrm[0:n, 0, k, 32 * b:32 * b + 32],
                                             z[0:n, j % 2, b].rearrange("p n s -> p (n s)"),
                                             start=(j < 4 and v == 0), stop=(k == NCH - 1 and v == 1))
                    m.then_inc(s_zu, 1)
                pe.wait_ge(s_p, 1)
                for k in range(NCK):
                    m = nc.tensor.transpose(psc[:, 128 * k:128 * k + 128],
                                            ex[:, PB * k:PB * k + PB, :].rearrange("p n s -> p (n s)"), ident[:, :])
                m.then_inc(s_pt, 1)
                pe.wait_ge(s_a, 1)
                nc.tensor.transpose(tp[0][:, 0:NI], ad[:, :], ident[:, :]).then_inc(s_at, 1)
                pe.wait_ge(s_atc, 1)
                nc.tensor.matmul(tp[1][:, 0:1], at[:, :], v1("beta"), start=True, stop=True).then_inc(s_cb, 1)

            @block.vector
            def _(dve):
                ch = Chain(dve, s_c2)
                V = nc.vector
                dve.wait_ge(s_xt, 16)
                ch.link(V.tensor_scalar(xt[:, :, :, :], xt[:, :, :, :], v1("alpha"), None, ALU.mult))
                V.tensor_scalar(xt[:, 0, 0, 0:1], xt[:, 0, 0, 0:1], v1("beta"), None, ALU.add).then_inc(s_xn, 1)
                dve.wait_ge(s_xn, 1)
                for kw in range(KW):
                    dve.wait_ge(s_t, kw + 1)
                    wait(dve, s_gr, kw - 1)
                    V.tensor_copy(xg[:, kw % 2, 0, :], tp[kw % 2][:, 0:NI]).then_inc(s_tc, 1)
                    if kw == 0:
                        for r in range(2):
                            for q in range(2):
                                s = V.tensor_copy(xr[:, 0, :, r, 16 * q:16 * q + 16], xt[:, 0:RW, r, 48 * q:48 * q + 16])
                        ch.link(s)
                        V.tensor_copy(xr[:, 1, :, 0, :], xr[:, 0, :, 1, :])
                        ch.link(V.tensor_scalar(xr[:, 1, :, 1, :], xr[:, 0, :, 0, :], -1.0, None, ALU.mult))
                dve.wait_ge(s_gr, KW)
                for b in range(NB):
                    s = V.tensor_copy(gram[32 * b:32 * b + 32, :], pgr[32 * b:32 * b + 32, 32 * b:32 * b + 32])
                ch.link(s)
                for i in range(2 * NCH):
                    n = 64 * min(2, RW - 2 * (i % NCH))
                    dve.wait_ge(s_r, i + 1)
                    V.tensor_copy(xrm[0:n, i // NCH, i % NCH, :], tp[i % 2][0:n, 0:NI]).then_inc(s_rc, 1)
                dve.wait_ge(s_rc, 2 * NCH)
                for j in range(NZ):
                    k, half, v = j // 4, (j // 2) % 2, j % 2
                    n = 64 * min(2, RW - 2 * k)
                    wait(dve, s_zu, j - 1)
                    w = gt[0:n, k, v, 16 * half:16 * half + 16]
                    xx = xrm[0:n, v, k, :].rearrange("p (b s) -> p b s", b=NB)
                    V.tensor_tensor(z[0:n, j % 2], bc(bc(w, 1, NB), 3, NT), bc(xx, 2, 16), ALU.mult).then_inc(s_z, 1)
                ch.link(V.tensor_tensor(sco[:, :, :], bc(qkb[:, :], 2, NT), bc(gram[:, :], 1, NHD), ALU.mult))
                dve.wait_ge(s_zu, NZ)
                ch.link(V.tensor_tensor(sco[:, :, :], sco[:, :, :], psc[:, :].rearrange("p (n s) -> p n s", n=NHD), ALU.add))
                ch.link(V.reduce_max(mx[:, :], sco[:, :, :], axis=AX.X))
                V.tensor_tensor(sco[:, :, :], sco[:, :, :], bc(mx[:, :], 2, NT), ALU.subtract).then_inc(s_mx, 1)
                dve.wait_ge(s_ex, 1)
                ch.link(V.reduce_sum(mx[:, :], ex[:, :, :], axis=AX.X))
                ch.link(V.reciprocal(mx[:, :], mx[:, :]))
                V.tensor_tensor(ex[:, :, :], ex[:, :, :], bc(mx[:, :], 2, NT), ALU.mult).then_inc(s_p, 1)
                dve.wait_ge(s_p, 1)
                ch.link(V.tensor_tensor(sco[:, :, :], ex[:, :, :], bc(vpb[:, :], 2, NT), ALU.mult))
                ch.link(V.reduce_sum(am[:, :], sco[:, :, :].rearrange("p n s -> p s n"), axis=AX.X))
                ch.link(V.memset(ad[:, :], 0.0))
                for b in range(NB):
                    s = V.tensor_copy(ad[32 * b:32 * b + 32, 32 * b:32 * b + 32], am[32 * b:32 * b + 32, :])
                s.then_inc(s_a, 1)
                dve.wait_ge(s_pt, 1)
                V.tensor_copy(pt[:, :, :], psc[:, :].rearrange("p (k i) -> p k i", k=NCK)).then_inc(s_ptc, 1)
                dve.wait_ge(s_at, 1)
                V.tensor_copy(at[:, :], tp[0][:, 0:NI]).then_inc(s_atc, 1)
                dve.wait_ge(s_atc, 1)
                ch.link(V.scalar_tensor_tensor(mt[:, :], at[:, :], v1("alpha"), ident[:, :], ALU.mult, ALU.add))
                dve.wait_ge(s_cb, 1)
                ch.link(V.tensor_copy(v1("cbeta"), tp[1][:, 0:1]))

        with ExitStack() as p3:
            def sb(name, shape):
                return p3.enter_context(nc.sbuf_tensor(name, shape, F32))

            def pb(name, shape):
                return p3.enter_context(nc.psum_tensor(name, shape, F32))

            pa = sb("pa3", [128, 2, M2])
            wb = sb("wb", [128, 2, NCK, 2, MB])
            xb = sb("xb", [128, 2, NB, 2, MB])
            q1 = sb("q1", [128, 2, NB, 2, MB])
            q2 = sb("q2", [128, 2, NB, 2, MB])
            ms = sb("ms", [128, 2, 512])
            sq = sb("sq", [128, 512])
            ssq = sb("ssq", [128, 32])
            acc = [pb(f"acc{i}", [128, 2, MB]) for i in range(2)]
            pm = [pb(f"pm{i}", [128, 512]) for i in range(2)]
            s_blk = sems("block_loaded", 2)
            s_q = sem("value_products_ready")
            s_qu = sem("value_products_used")
            s_ac = sem("block_copied")
            s_mm = sem("images_mixed")
            s_mc = sem("mixed_images_copied")
            s_ms = sems("mixed_images_stored", 2)
            s_sq = sem("squares_summed")
            s_c3 = sem("p3_vector_steps")
            s_pa = sem("projected_spectrum_stored")
            NMX = HH * WW // 512
            block = p3.enter_context(nc.Block())

            @block.sync
            def _(sp):
                def load(blk, u):
                    wait(sp, s_qu, NCK * (blk - 1))
                    for j in range(PB):
                        n = NCK * 2 * MB
                        sp.dma_start(wb[32 * j:32 * j + 32, u].rearrange("p k r m -> p (k r m)"),
                                     bass.AP(wv.tensor, (blk + j * NBLK) * n, [[0, 32], [1, n]])).then_inc(s_blk[u], 16)
                        for r in range(2):
                            sp.dma_start(xb[32 * j:32 * j + 32, u, :, r],
                                         bass.AP(xns.tensor, r * M2 + blk * MB, [[2 * M2, NT], [NT * 2 * M2, NB], [1, MB]])).then_inc(s_blk[u], 16)
                load(0, 0)
                load(1, 1)
                with sp.Fori(1, NBLK // 2) as i:
                    for u in range(2):
                        load(2 * i + u, u)
                sp.wait_ge(s_ac, NBLK)
                sp.dma_start(pspec, pa[:, :, :]).then_inc(s_pa, 16)
                sp.wait_ge(s_pa, 16)

            @block.gpsimd
            def _(pool):
                mo = mixd.rearrange("i h w -> i (h w)")
                def store(i, u):
                    t = 2 * i + u
                    pool.wait_ge(s_mc, t + 1)
                    pool.dma_start(mo[:, bass.ds(t * 512, 512)], ms[:, u]).then_inc(s_ms[u], 16)
                with pool.Fori(0, NMX // 2) as i:
                    for u in range(2):
                        store(i, u)
                for q in s_ms:
                    pool.wait_ge(q, 16 * NMX // 2)

            @block.scalar
            def _(act):
                def mixed(i, u):
                    t = 2 * i + u
                    act.wait_ge(s_mm, t + 1)
                    wait(act, s_ms[u], 16 * i)
                    act.activation(ms[:, u], pm[u][:, :], ACT.Identity, bias=v1("cbeta")).then_inc(s_mc, 1)
                    act.wait_ge(s_mc, t + 1)
                    wait(act, s_sq, t)
                    act.activation(sq[:, :], ms[:, u], ACT.Square,
                                   accum_out=ssq[:, bass.ds(t, 1)]).then_inc(s_sq, 1)
                mixed(0, 0)
                mixed(0, 1)
                with act.Fori(1, NMX // 2) as i:
                    for u in range(2):
                        mixed(i, u)
                with act.Fori(0, NBLK // 2) as i:
                    for u in range(2):
                        blk = 2 * i + u
                        act.wait_ge(s_qu, NCK * (blk + 1))
                        act.activation(pa[:, :, bass.ds(blk * MB, MB)], acc[u][:, :, :], ACT.Copy).then_inc(s_ac, 1)
                act.wait_ge(s_ac, NBLK)

            @block.tensor
            def _(pe):
                def mix(i, u):
                    t = 2 * i + u
                    wait(pe, s_mc, t - 1)
                    nc.tensor.matmul(pm[u][:, :], mt[:, :], xa[:, bass.ds(t * 512, 512)], start=True, stop=True).then_inc(s_mm, 1)
                mix(0, 0)
                mix(0, 1)
                with pe.Fori(1, NMX // 2) as i:
                    for u in range(2):
                        mix(i, u)

                def contract(blk, u):
                    wait(pe, s_ac, blk - 1)
                    for k in range(NCK):
                        pe.wait_ge(s_q, NCK * blk + k + 1)
                        for p in range(3):
                            for b in range(NB):
                                rows = slice(32 * b, 32 * b + 32)
                                P, N = pt[:, k, rows], npt[:, k, rows]
                                if p == 0:
                                    m = nc.tensor.matmul(acc[u][rows, :, :].rearrange("p r m -> p (r m)"), P,
                                                         q1[:, k % 2, b].rearrange("p r m -> p (r m)"),
                                                         start=(k == 0), stop=False)
                                elif p == 1:
                                    m = nc.tensor.matmul(acc[u][rows, 1, :], P, q2[:, k % 2, b, 0], start=False, stop=False)
                                else:
                                    m = nc.tensor.matmul(acc[u][rows, 0, :], N, q2[:, k % 2, b, 1], start=False, stop=(k == NCK - 1))
                        m.then_inc(s_qu, 1)
                contract(0, 0)
                contract(1, 1)
                with pe.Fori(1, NBLK // 2) as i:
                    for u in range(2):
                        contract(2 * i + u, u)

            @block.vector
            def _(dve):
                V = nc.vector
                def products(i, u):
                    blk = 2 * i + u
                    dve.wait_ge(s_blk[u], 16 * 3 * PB * (i + 1))
                    for k in range(NCK):
                        wait(dve, s_qu, NCK * blk + k - 1)
                        X = xb[:, u].rearrange("p b r m -> p (b r) m")
                        V.tensor_tensor(q1[:, k % 2].rearrange("p b r m -> p (b r) m"), bc(wb[:, u, k, 0], 1, 2 * NB), X, ALU.mult)
                        V.tensor_tensor(q2[:, k % 2].rearrange("p b r m -> p (b r) m"), bc(wb[:, u, k, 1], 1, 2 * NB), X, ALU.mult).then_inc(s_q, 1)
                products(0, 0)
                products(0, 1)
                with dve.Fori(1, NBLK // 2) as i:
                    for u in range(2):
                        products(i, u)
                dve.wait_ge(s_sq, NMX)
                ch = Chain(dve, s_c3)
                ch.link(V.reduce_sum(v1("mixsq"), ssq[:, :], axis=AX.X))
                ch.link(V.tensor_scalar(v1("mixsq"), v1("mixsq"), 1.0 / (HH * WW), None, ALU.mult))

        att.close()
        yall = keep("yall", [128, NI, WW])
        spec = ExitStack()
        tt = spec.enter_context(nc.sbuf_tensor("tt", [128, 2 * KW, NI], F32))
        DC = (slice(None), 0, 0, slice(0, 1))

        def complex_product(ch, V, dst, w, src, t):
            wr, wi = (w[:, :, :, r].rearrange("p h w -> p w h") for r in (0, 1))
            V.tensor_tensor(dst[:, :, 0], wr, src[:, :, 0], ALU.mult)
            V.tensor_tensor(dst[:, :, 1], wr, src[:, :, 1], ALU.mult)
            ch.link(V.tensor_tensor(t, wi, src[:, :, 1], ALU.mult))
            ch.link(V.tensor_tensor(dst[:, :, 0], dst[:, :, 0], t, ALU.subtract))
            ch.link(V.tensor_tensor(t, wi, src[:, :, 0], ALU.mult))
            ch.link(V.tensor_tensor(dst[:, :, 1], dst[:, :, 1], t, ALU.add))

        def energy(ch, act, src, col0, t, en):
            for r in range(2):
                ch.link(act.activation(t[:, 0:(KW - 1) * KH].rearrange("p (w h) -> p w h", w=KW - 1), src[:, 1:KW, r, :], ACT.Square, accum_out=en[:, r:r + 1]))
            ch.link(act.activation(t[:, 0:2 * KH].rearrange("p (r h) -> p r h", r=2), col0, ACT.Square, accum_out=en[:, 2:3]))
            ch.link(act.activation(t[:, 0:2], col0[:, :, 32], ACT.Square, accum_out=en[:, 3:4]))

        def energy_sum(ch, V, out, en):
            ch.link(V.tensor_tensor(out, en[:, 0:1], en[:, 1:2], ALU.add))
            ch.link(V.tensor_scalar(out, out, 2.0, None, ALU.mult))
            ch.link(V.tensor_tensor(out, out, en[:, 2:3], ALU.add))
            ch.link(V.tensor_tensor(out, out, en[:, 3:4], ALU.add))

        def mulv(ch, V, out, x_, y_):
            ch.link(V.tensor_tensor(out, x_, y_, ALU.mult))

        def to_rows_pe(pe, zp, ps, s_zp, s_tr, s_trc):
            pe.wait_ge(s_zp, 1)
            for q in range(0, 2 * KW, 4):
                if q // 4 >= 2:
                    pe.wait_ge(s_trc, q // 4 - 1)
                for j in range(q, min(q + 4, 2 * KW)):
                    v, kw = j // KW, j % KW
                    m = nc.tensor.transpose(ps[(q // 4) % 2][:, 128 * (j - q):128 * (j - q) + 128], zp[:, kw, v:v + 2].rearrange("p r h -> p (r h)"), ident[:, :])
                m.then_inc(s_tr, 1)

        def to_rows_copy(act, ps, s_tr, s_trc):
            for q in range(0, 2 * KW, 4):
                n = min(4, 2 * KW - q)
                act.wait_ge(s_tr, q // 4 + 1)
                act.activation(tt[:, q:q + n, :], ps[(q // 4) % 2][:, 0:128 * n].rearrange("p (j i) -> p j i", j=n), ACT.Copy).then_inc(s_trc, 1)
            act.wait_ge(s_trc, (2 * KW + 3) // 4)

        def symmetrise(pe, src, ps, cs, s_a, s_b, s_c, n):
            nc.tensor.transpose(ps[:, 0:128], src[:, 0, 0:2].rearrange("p r h -> p (r h)"), ident[:, :]).then_inc(s_a, 1)
            pe.wait_ge(s_b, n)
            nc.tensor.matmul(ps[:, 128:256], cs[:, :], sym[:, :], start=True, stop=True).then_inc(s_c, 1)


        with ExitStack() as p4:
            def sb(name, shape):
                return p4.enter_context(nc.sbuf_tensor(name, shape, F32))

            def pb(name, shape):
                return p4.enter_context(nc.psum_tensor(name, shape, F32))

            zp = sb("zp4", [128, KW, 3, KH])
            pa = sb("pa4", [128, KW, 2, KH])
            fs = sb("fs4", [128, KW, 2, KH])
            t4 = sb("t4", [128, M2])
            ta = sb("t4a", [128, M2])
            cs = sb("cs4", [128, 128])
            s0 = sb("s04", [128, 2, KH])
            en = sb("en4", [128, 12])
            dg = sb("dg4", [128, NI])
            flat = tt[:, :, :].rearrange("p j i -> p (j i)")
            xt4 = flat[:, 0:2 * M2]
            mraw = flat[:, 2 * M2:4 * M2].rearrange("p (h w r) -> p h w r", h=KH, w=KW)
            mxs = sb("mx4", [128, KW, 2, KH])
            pmx = [pb(f"pmx{i}", [128, 512]) for i in range(2)]
            psy = pb("psy4", [128, 512])
            ps = [pb(f"ptr4_{i}", [128, 512]) for i in range(2)]
            pbc = pb("pbc4", [128, 512])
            s_ld = sem("p4_spectra_loaded")
            s_mr = sem("m0_weights_loaded")
            s_mm4 = sem("mixed_spectrum_done")
            s_mc4 = sem("mixed_spectrum_copied")
            s_y0 = sem("p4_products_ready")
            s_sa, s_sbb, s_sc = sem("p4_column0_transposed"), sem("p4_column0_copied"), sem("p4_column0_symmetrised")
            s_v4, s_a4 = sem("p4_vector_steps"), sem("p4_energy_steps")
            s_f = sem("p4_spectrum_for_energy")
            s_zp, s_tr, s_trc = sem("p4_spectrum_ready"), sem("p4_rows_transposed"), sem("p4_rows_copied")
            s_dg, s_bc = sem("p4_factors_ready"), sem("p4_factors_spread")
            root = Root(sem("p4_root_asked"), sem("p4_root_given"))
            block = p4.enter_context(nc.Block())
            NC4 = (2 * M2 + 511) // 512

            @block.sync
            def _(sp):
                sp.dma_start(xt4, xs.rearrange("i m k -> i (m k)")).then_inc(s_ld, 16)
                for r in range(2):
                    sp.dma_start(pa[:, :, r, :], pspec[:, r].rearrange("i (w h) -> i w h", w=KW)).then_inc(s_ld, 16)
                src = a["L0_conv_m0cw"]
                sp.dma_start(mraw.rearrange("p h w r -> p (h w r)"), bass.AP(src.tensor, 0, [[0, 128], [1, 2 * M2]])).then_inc(s_mr, 16)

            @block.tensor
            def _(pe):
                pe.wait_ge(s_ld, 48)
                for j in range(NC4):
                    n = min(512, 2 * M2 - 512 * j)
                    if j >= 2:
                        pe.wait_ge(s_mc4, j - 1)
                    nc.tensor.matmul(pmx[j % 2][:, 0:n], mt[:, :], xt4[:, 512 * j:512 * j + n], start=True, stop=True).then_inc(s_mm4, 1)
                symmetrise(pe, pa, psy, cs, s_sa, s_sbb, s_sc, 1)
                pe.wait_ge(s_y0, 1)
                symmetrise(pe, zp, psy, cs, s_sa, s_sbb, s_sc, 2)
                to_rows_pe(pe, zp, ps, s_zp, s_tr, s_trc)
                for i in range(2):
                    pe.wait_ge(s_dg, i + 1)
                    nc.tensor.matmul(pbc[:, 128 * i:128 * i + 128], ones[:, :], dg[:, :], start=True, stop=True).then_inc(s_bc, 1)

            @block.scalar
            def _(act):
                ch = Chain(act, s_a4)
                act.wait_ge(s_f, 1)
                energy(ch, nc.scalar, mxs, mxs[:, 0], ta, en[:, 0:4])
                energy(ch, nc.scalar, fs, fs[:, 0], ta, en[:, 4:8])
                root.serve(act, nc.scalar, v1("r"))
                root.serve(act, nc.scalar, v1("r"))
                act.wait_ge(s_f, 2)
                energy(ch, nc.scalar, zp, s0[:, :, :], ta, en[:, 8:12])
                root.serve(act, nc.scalar, v1("r"))
                act.wait_ge(s_zp, 1)
                to_rows_copy(act, ps, s_tr, s_trc)

            @block.vector
            def _(dve):
                ch = Chain(dve, s_v4)
                V = nc.vector
                mflat = mxs[:, :, :, :].rearrange("p w r h -> p (w r h)")
                for j in range(NC4):
                    n = min(512, 2 * M2 - 512 * j)
                    dve.wait_ge(s_mm4, j + 1)
                    V.tensor_copy(mflat[:, 512 * j:512 * j + n], pmx[j % 2][:, 0:n]).then_inc(s_mc4, 1)
                dve.wait_ge(s_mc4, NC4)
                ch.link(V.tensor_scalar(mxs[DC], mxs[DC], v1("cbeta"), None, ALU.add))
                dve.wait_ge(s_sa, 1)
                V.tensor_copy(cs[:, :], psy[:, 0:128]).then_inc(s_sbb, 1)
                ch.link(V.tensor_tensor(fs[:, 1:KW], mxs[:, 1:KW], pa[:, 1:KW], ALU.add))
                dve.wait_ge(s_sc, 1)
                V.tensor_tensor(fs[:, 0], mxs[:, 0], psy[:, 128:256].rearrange("p (r h) -> p r h", r=2), ALU.add).then_inc(s_f, 1)
                dve.wait_ge(s_a4, 8)
                e1, e2 = v1("e1"), v1("e2")
                energy_sum(ch, V, e1, en[:, 0:4])
                energy_sum(ch, V, e2, en[:, 4:8])
                var, r, t = v1("var"), v1("r"), v1("t")
                ch.link(V.tensor_tensor(var, e2, e1, ALU.subtract))
                ch.link(V.tensor_tensor(var, var, v1("mixsq"), ALU.add))
                ch.link(V.tensor_copy(v1("mu"), fs[DC]))
                mulv(ch, V, t, v1("mu"), v1("mu"))
                ch.link(V.tensor_tensor(var, var, t, ALU.subtract))
                root.rsqrt(dve, ch, V, r, var)
                mulv(ch, V, v1("g"), r, scalar["attn_w"])
                mulv(ch, V, t, v1("g"), v1("g"))
                mulv(ch, V, t, t, var)
                root.rsqrt(dve, ch, V, r, t)
                mulv(ch, V, v1("kappa"), r, scalar["norm2_w"])
                mulv(ch, V, v1("kg"), v1("kappa"), v1("g"))
                ch.link(V.tensor_scalar(fs[:, :, :, :], fs[:, :, :, :], v1("kg"), None, ALU.mult))
                ch.link(V.tensor_copy(fs[DC], scalar["norm2_b"]))
                dve.wait_ge(s_mr, 16)
                complex_product(ch, V, zp[:, :, 0:2], mraw, fs, t4[:, :].rearrange("p (w h) -> p w h", w=KW))
                ch.link(V.memset(zp[:, 0, 0:2, 0:1], 0.0))
                V.tensor_scalar(t4[:, 0:1], zp[DC], 1.0, None, ALU.mult).then_inc(s_y0, 1)
                dve.wait_ge(s_sa, 2)
                V.tensor_copy(cs[:, :], psy[:, 0:128]).then_inc(s_sbb, 1)
                dve.wait_ge(s_sc, 2)
                V.tensor_copy(s0[:, :, :], psy[:, 128:256].rearrange("p (r h) -> p r h", r=2)).then_inc(s_f, 1)
                dve.wait_ge(s_a4, 12)
                energy_sum(ch, V, e1, en[:, 8:12])
                root.rsqrt(dve, ch, V, r, e1)
                mulv(ch, V, v1("skg"), v1("kg"), scalar["m0sw"])
                ch.link(V.tensor_scalar(zp[:, :, 0:2], zp[:, :, 0:2], r, None, ALU.mult))
                ch.link(V.scalar_tensor_tensor(zp[:, :, 0:2], pa[:, :, :, :], v1("skg"), zp[:, :, 0:2], ALU.mult, ALU.add))
                mulv(ch, V, t, v1("skg"), v1("mu"))
                ch.link(V.tensor_tensor(zp[DC], zp[DC], t, ALU.subtract))
                mulv(ch, V, t, scalar["m0sw"], scalar["norm2_b"])
                ch.link(V.tensor_tensor(zp[DC], zp[DC], t, ALU.add))
                V.tensor_scalar(zp[:, :, 2], zp[:, :, 0], -1.0, None, ALU.mult).then_inc(s_zp, 1)
                for i, (n, dst) in enumerate((("skg", c1b), ("g", c2b))):
                    V.tensor_scalar(dg[:, :], ident[:, :], v1(n), None, ALU.mult).then_inc(s_dg, 1)
                    dve.wait_ge(s_bc, i + 1)
                    ch.link(V.tensor_copy(dst[:, :], pbc[:, 128 * i:128 * i + 128]))

        recycle()

        def lagged(b, u, k, body, *args):
            if k > u:
                if not (isinstance(b, int) and b == 0):
                    body(b - 1, u - k + GPB, *args)
            else:
                body(b, u - k, *args)

        def inverse_h(pe, b, u, ts, pz, s_ts, s_s1, s_z):
            g = GPB * b + u
            pe.wait_ge(s_ts, g + 1)
            wait(pe, s_z, g)
            for i in range(GI):
                m = nc.tensor.matmul(pz[:, 128 * i:128 * i + 128], ts[:, u % 2, :, i], eh[:, :], start=True, stop=True)
            m.then_inc(s_s1, 1)

        def inverse_w(pe, b, u, zs, pi, s_z, s_s2, s_add):
            g = GPB * b + u
            pe.wait_ge(s_z, g + 1)
            wait(pe, s_add, g)
            for i in range(GI):
                m = nc.tensor.matmul(pi[:, 128 * i:128 * i + 128], zs[:, u % 2, i, :], cw[:, :], start=True, stop=True)
            m.then_inc(s_s2, 1)

        with ExitStack() as p5:
            def sb(name, shape):
                return p5.enter_context(nc.sbuf_tensor(name, shape, F32))

            def pb(name, shape):
                return p5.enter_context(nc.psum_tensor(name, shape, F32))

            mg = sb("mg5", [128, GPB, GI, WW])
            ts = sb("ts5", [128, 2, 2 * KW, GI])
            zs = sb("zs5", [2 * KW, 2, GI, 128])
            pre = sb("pre5", [128, 2, GI, WW])
            yst = sb("yst5", [128, 2, GI, WW])
            sq = sb("sq5", [128, 2, GI, WW])
            yf = sb("yf5", [128, 2, 2, GI, KH])
            yo = sb("yo5", [2 * KW, GPB, GI, KH])
            ysq = sb("ysq5", [128, NI])
            pz = pb("pz5", [2 * KW, GI * 128])
            pi = pb("pi5", [128, GI * 128])
            pf = pb("pf5", [128, GI * 128])
            pw = pb("pw5", [2 * KW, GI * KH])
            pq = pb("pq5", [128, 512])
            s_mg = sems("p5_mixed_loaded", GPB)
            s_ts, s_s1, s_z, s_s2 = sem("p5_spectra_staged"), sem("p5_rows_done"), sem("p5_rows_copied_back"), sem("p5_pixels_done")
            s_m5 = sem("p5_mixed_scaled")
            s_add, s_y, s_sqd, s_rd = sem("p5_preactivation_ready"), sem("hidden_ready"), sem("hidden_squared"), sem("hidden_squares_summed")
            s_yd = sems("hidden_kept", 2)
            s_f1, s_e1, s_f2, s_e2, s_yo = sem("p5_h_transform_done"), sem("p5_h_transform_copied"), sem("p5_w_transform_done"), sem("p5_w_transform_copied"), sems("hidden_spectrum_stored", GPB)
            s_q5, s_v5 = sem("hidden_energy_done"), sem("p5_vector_steps")
            block = p5.enter_context(nc.Block())
            mixr = mixd.rearrange("i h w -> h i w")

            @block.sync
            def _(sp):
                def load(b):
                    for u in range(GPB):
                        g = GPB * b + u
                        wait(sp, s_m5, g + 1 - GPB)
                        sp.dma_start(mg[:, u], mixr[:, bass.ds(g * GI, GI), :]).then_inc(s_mg[u], 16)
                per_batch(sp, load)

            @block.gpsimd
            def _(pool):
                def stage(b, u):
                    g = GPB * b + u
                    wait(pool, s_s1, g - 1)
                    nc.gpsimd.tensor_copy(ts[:, u % 2], tt[:, :, bass.ds(g * GI, GI)]).then_inc(s_ts, 1)

                def keep_hidden(b, u):
                    g = GPB * b + u
                    pool.wait_ge(s_y, g + 1)
                    pool.dma_start(yall[:, bass.ds(g * GI, GI), :], yst[:, u % 2]).then_inc(s_yd[u % 2], 16)

                def store(b, u):
                    g = GPB * b + u
                    pool.wait_ge(s_e2, g + 1)
                    pool.dma_start(ys[bass.ds(g * GI, GI)].rearrange("i m k -> m i k"), yo[:, u]).then_inc(s_yo[u], 16)

                def body(b):
                    for u in range(GPB):
                        lagged(b, u, 0, stage)
                        lagged(b, u, 1, keep_hidden)
                        lagged(b, u, 2, store)
                per_batch(pool, body)
                keep_hidden(NB - 1, GPB - 1)
                store(NB - 1, GPB - 2)
                store(NB - 1, GPB - 1)
                for q in s_yo:
                    pool.wait_ge(q, 16 * NGRP // GPB)
                for q in s_yd:
                    pool.wait_ge(q, 16 * NGRP // 2)

            @block.tensor
            def _(pe):
                def forward_h(b, u):
                    g = GPB * b + u
                    pe.wait_ge(s_y, g + 1)
                    wait(pe, s_e1, g)
                    for i in range(GI):
                        m = nc.tensor.matmul(pf[:, 128 * i:128 * i + 128], yst[:, u % 2, i, :], fh[:, :], start=True, stop=True)
                    m.then_inc(s_f1, 1)

                def forward_w(b, u):
                    g = GPB * b + u
                    pe.wait_ge(s_e1, g + 1)
                    wait(pe, s_e2, g)
                    for r, f in enumerate((fw1, fw2)):
                        m = nc.tensor.matmul(pw[:, :], f[:, :], yf[:, u % 2, r].rearrange("w i k -> w (i k)"), start=(r == 0), stop=(r == 1))
                    m.then_inc(s_f2, 1)

                def body(b):
                    for u in range(GPB):
                        lagged(b, u, 0, lambda c_, v: inverse_h(pe, c_, v, ts, pz, s_ts, s_s1, s_z))
                        lagged(b, u, 1, forward_h)
                        lagged(b, u, 0, lambda c_, v: inverse_w(pe, c_, v, zs, pi, s_z, s_s2, s_add))
                        lagged(b, u, 1, forward_w)
                per_batch(pe, body)
                forward_h(NB - 1, GPB - 1)
                forward_w(NB - 1, GPB - 1)
                pe.wait_ge(s_rd, NGRP)
                nc.tensor.matmul(pq[:, 0:1], ysq[:, :], ones[:, 0:1], start=True, stop=True).then_inc(s_q5, 1)

            @block.scalar
            def _(act):
                def rows_back(b, u):
                    g = GPB * b + u
                    act.wait_ge(s_s1, g + 1)
                    wait(act, s_s2, g - 1)
                    act.activation(zs[:, u % 2], pz[:, :].rearrange("m (i h) -> m i h", i=GI), ACT.Copy).then_inc(s_z, 1)

                def forward_copy(b, u):
                    g = GPB * b + u
                    act.wait_ge(s_f1, g + 1)
                    wait(act, s_f2, g - 1)
                    act.activation(yf[:, u % 2], pf[:, :].rearrange("w (i r k) -> w r i k", i=GI, r=2), ACT.Copy).then_inc(s_e1, 1)

                def gelu(b, u):
                    g = GPB * b + u
                    act.wait_ge(s_add, g + 1)
                    wait(act, s_f1, g - 1)
                    wait(act, s_yd[u % 2], 16 * nth(b, u))
                    act.activation(yst[:, u % 2], pre[:, u % 2], ACT.Gelu).then_inc(s_y, 1)
                    act.wait_ge(s_y, g + 1)
                    wait(act, s_rd, g - 1)
                    act.activation(sq[:, u % 2], yst[:, u % 2], ACT.Square).then_inc(s_sqd, 1)

                def body(b):
                    for u in range(GPB):
                        lagged(b, u, 0, rows_back)
                        lagged(b, u, 1, forward_copy)
                        lagged(b, u, 0, gelu)
                per_batch(act, body)
                forward_copy(NB - 1, GPB - 1)

            @block.vector
            def _(dve):
                V = nc.vector

                def scale(b, u):
                    g = GPB * b + u
                    dve.wait_ge(s_mg[u], 16 * (b + 1))
                    wait(dve, s_y, g - 1)
                    V.tensor_tensor(pre[:, u % 2], mg[:, u], bc(c1b[:, bass.ds(g * GI, GI)], 2, WW), ALU.mult).then_inc(s_m5, 1)

                def add(b, u):
                    g = GPB * b + u
                    dve.wait_ge(s_s2, g + 1)
                    dve.wait_ge(s_m5, g + 1)
                    V.tensor_tensor(pre[:, u % 2], pre[:, u % 2], pi[:, :].rearrange("h (i w) -> h i w", i=GI), ALU.add).then_inc(s_add, 1)

                def sum_squares(b, u):
                    g = GPB * b + u
                    dve.wait_ge(s_sqd, g + 1)
                    V.reduce_sum(ysq[:, bass.ds(g * GI, GI)], sq[:, u % 2], axis=AX.X).then_inc(s_rd, 1)

                def copy_out(b, u):
                    g = GPB * b + u
                    dve.wait_ge(s_f2, g + 1)
                    wait(dve, s_yo[u], 16 * b)
                    V.tensor_copy(yo[:, u], pw[:, :].rearrange("m (i k) -> m i k", i=GI)).then_inc(s_e2, 1)

                def body(b):
                    for u in range(GPB):
                        lagged(b, u, 0, scale)
                        lagged(b, u, 1, sum_squares)
                        lagged(b, u, 0, add)
                        lagged(b, u, 1, copy_out)
                per_batch(dve, body)
                sum_squares(NB - 1, GPB - 1)
                copy_out(NB - 1, GPB - 1)
                dve.wait_ge(s_q5, 1)
                ch = Chain(dve, s_v5)
                ch.link(V.tensor_scalar(v1("ysq"), pq[:, 0:1], 1.0 / (HH * WW), None, ALU.mult))

        with ExitStack() as p6:
            def sb(name, shape):
                return p6.enter_context(nc.sbuf_tensor(name, shape, F32))

            def pb(name, shape):
                return p6.enter_context(nc.psum_tensor(name, shape, F32))

            zp = sb("zp6", [128, KW, 3, KH])
            pa = sb("pa6", [128, KW, 2, KH])
            t6 = sb("t6", [128, M2])
            ta = sb("t6a", [128, M2])
            cs = sb("cs6", [128, 128])
            s0 = sb("s06", [128, 2, KH])
            en = sb("en6", [128, 4])
            cr = sb("cr6", [128, 4])
            dg = sb("dg6", [128, NI])
            flat = tt[:, :, :].rearrange("p j i -> p (j i)")
            yt = flat[:, 0:2 * M2].rearrange("p (w r h) -> p w r h", r=2, w=KW)
            mraw = flat[:, 2 * M2:4 * M2].rearrange("p (h w r) -> p h w r", h=KH, w=KW)
            psy = pb("psy6", [128, 512])
            ps = [pb(f"ptr6_{i}", [128, 512]) for i in range(2)]
            pbc = pb("pbc6", [128, 512])
            s_ld = sem("p6_loaded")
            s_y1 = sem("p6_products_ready")
            s_sa, s_sbb, s_sc = sem("p6_column0_transposed"), sem("p6_column0_copied"), sem("p6_column0_symmetrised")
            s_v6, s_a6 = sem("p6_vector_steps"), sem("p6_energy_steps")
            s_f = sem("p6_spectrum_for_energy")
            s_zp, s_tr, s_trc = sem("p6_spectrum_ready"), sem("p6_rows_transposed"), sem("p6_rows_copied")
            s_dg, s_bc = sem("p6_factors_ready"), sem("p6_factors_spread")
            root = Root(sem("p6_root_asked"), sem("p6_root_given"))
            block = p6.enter_context(nc.Block())

            @block.sync
            def _(sp):
                sp.dma_start(flat[:, 0:2 * M2], ys.rearrange("i m k -> i (m k)")).then_inc(s_ld, 16)
                for r in range(2):
                    sp.dma_start(pa[:, :, r, :], pspec[:, r].rearrange("i (w h) -> i w h", w=KW)).then_inc(s_ld, 16)
                src = a["L0_conv_m1cw"]
                sp.dma_start(mraw.rearrange("p h w r -> p (h w r)"), bass.AP(src.tensor, 0, [[0, 128], [1, 2 * M2]])).then_inc(s_ld, 16)

            @block.tensor
            def _(pe):
                pe.wait_ge(s_y1, 1)
                symmetrise(pe, zp, psy, cs, s_sa, s_sbb, s_sc, 1)
                to_rows_pe(pe, zp, ps, s_zp, s_tr, s_trc)
                pe.wait_ge(s_dg, 1)
                nc.tensor.matmul(pbc[:, 0:128], ones[:, :], dg[:, :], start=True, stop=True).then_inc(s_bc, 1)

            @block.scalar
            def _(act):
                ch = Chain(act, s_a6)
                act.wait_ge(s_f, 1)
                energy(ch, nc.scalar, zp, s0[:, :, :], ta, en[:, 0:4])
                root.serve(act, nc.scalar, v1("r"))
                root.serve(act, nc.scalar, v1("t"))
                act.wait_ge(s_zp, 1)
                to_rows_copy(act, ps, s_tr, s_trc)

            @block.vector
            def _(dve):
                ch = Chain(dve, s_v6)
                V = nc.vector
                r, t, var = v1("r"), v1("t"), v1("var")
                dve.wait_ge(s_ld, 64)
                tv = t6[:, :].rearrange("p (w h) -> p w h", w=KW)
                complex_product(ch, V, zp[:, :, 0:2], mraw, yt, tv)
                ch.link(V.memset(zp[:, 0, 0:2, 0:1], 0.0))
                V.tensor_scalar(t6[:, 0:1], zp[DC], 1.0, None, ALU.mult).then_inc(s_y1, 1)
                dve.wait_ge(s_sa, 1)
                V.tensor_copy(cs[:, :], psy[:, 0:128]).then_inc(s_sbb, 1)
                dve.wait_ge(s_sc, 1)
                V.tensor_copy(s0[:, :, :], psy[:, 128:256].rearrange("p (r h) -> p r h", r=2)).then_inc(s_f, 1)
                for q in range(2):
                    ch.link(V.tensor_tensor(tv, zp[:, :, q], yt[:, :, q], ALU.mult))
                    ch.link(V.reduce_sum(cr[:, 2 * q:2 * q + 1], t6[:, KH:M2], axis=AX.X))
                    ch.link(V.reduce_sum(cr[:, 2 * q + 1:2 * q + 2], t6[:, 0:KH], axis=AX.X))
                cross = v1("cross")
                ch.link(V.tensor_tensor(cross, cr[:, 0:1], cr[:, 2:3], ALU.add))
                ch.link(V.tensor_scalar(cross, cross, 2.0, None, ALU.mult))
                ch.link(V.tensor_tensor(cross, cross, cr[:, 1:2], ALU.add))
                ch.link(V.tensor_tensor(cross, cross, cr[:, 3:4], ALU.add))
                dve.wait_ge(s_a6, 4)
                e1, w1, yb_ = v1("e1"), scalar["m1sw"], v1("ybar")
                energy_sum(ch, V, e1, en[:, 0:4])
                root.rsqrt(dve, ch, V, r, e1)
                mulv(ch, V, var, r, e1)
                mulv(ch, V, t, w1, cross)
                ch.link(V.tensor_scalar(t, t, 2.0, None, ALU.mult))
                ch.link(V.tensor_tensor(var, var, t, ALU.add))
                mulv(ch, V, var, var, r)
                ch.link(V.tensor_copy(yb_, yt[DC]))
                mulv(ch, V, t, yb_, yb_)
                ch.link(V.tensor_tensor(t, v1("ysq"), t, ALU.subtract))
                mulv(ch, V, t, t, w1)
                mulv(ch, V, t, t, w1)
                ch.link(V.tensor_tensor(var, var, t, ALU.add))
                root.rsqrt(dve, ch, V, t, var)
                gm = v1("gm")
                mulv(ch, V, gm, t, scalar["mon_w"])
                mulv(ch, V, r, r, gm)
                ch.link(V.tensor_scalar(zp[:, :, 0:2], zp[:, :, 0:2], r, None, ALU.mult))
                ch.link(V.scalar_tensor_tensor(zp[:, :, 0:2], pa[:, :, :, :], v1("g"), zp[:, :, 0:2], ALU.mult, ALU.add))
                c2 = v1("c2")
                mulv(ch, V, c2, gm, w1)
                mulv(ch, V, t, c2, yb_)
                ch.link(V.tensor_tensor(zp[DC], zp[DC], t, ALU.subtract))
                mulv(ch, V, t, v1("g"), v1("mu"))
                ch.link(V.tensor_tensor(zp[DC], zp[DC], t, ALU.subtract))
                ch.link(V.tensor_tensor(zp[DC], zp[DC], scalar["mon_b"], ALU.add))
                ch.link(V.tensor_tensor(zp[DC], zp[DC], scalar["attn_b"], ALU.add))
                V.tensor_scalar(zp[:, :, 2], zp[:, :, 0], -1.0, None, ALU.mult).then_inc(s_zp, 1)
                V.tensor_scalar(dg[:, :], ident[:, :], c2, None, ALU.mult).then_inc(s_dg, 1)
                dve.wait_ge(s_bc, 1)
                ch.link(V.tensor_copy(c1b[:, :], pbc[:, 0:128]))

        fwd = ExitStack()
        y1 = fwd.enter_context(nc.sbuf_tensor("y1", [128, NI, 130], F32))
        with ExitStack() as p7:
            def sb(name, shape):
                return p7.enter_context(nc.sbuf_tensor(name, shape, F32))

            def pb(name, shape):
                return p7.enter_context(nc.psum_tensor(name, shape, F32))

            mg = sb("mg7", [128, 2, GI, WW])
            xg = sb("xg7", [128, 2, GI, WW])
            ts = sb("ts7", [128, 2, 2 * KW, GI])
            zs = sb("zs7", [2 * KW, 2, GI, 128])
            xn = sb("xn7", [128, 2, GI, WW])
            qh = sb("qh", [128, 128])
            pz = pb("pz7", [2 * KW, GI * 128])
            pi = pb("pi7", [128, GI * 128])
            pf = pb("pf7", [128, GI * 128])
            s_qh = sem("p7_matrix_loaded")
            s_mg = sems("p7_images_loaded", 2)
            s_ts, s_s1, s_z, s_s2 = sem("p7_spectra_staged"), sem("p7_rows_done"), sem("p7_rows_copied_back"), sem("p7_pixels_done")
            s_m7, s_p7 = sem("p7_mixed_scaled"), sem("p7_input_added")
            s_h7, s_q7 = sem("p7_hidden_scaled"), sem("p7_parts_added")
            s_add, s_k = sem("layer0_output_ready"), sems("layer0_output_kept", 2)
            s_f1, s_e1 = sem("p7_h_transform_done"), sem("p7_h_transform_copied")
            block = p7.enter_context(nc.Block())
            xr7 = x.rearrange("i h w -> h i w")

            @block.sync
            def _(sp):
                sp.dma_start(qh[:, :], c["qh"]).then_inc(s_qh, 16)

                def load(b, u):
                    g = GPB * b + u
                    wait(sp, s_q7, g - 1)
                    sp.dma_start(mg[:, u % 2], mixr[:, bass.ds(g * GI, GI), :]).then_inc(s_mg[u % 2], 16)
                    sp.dma_start(xg[:, u % 2], xr7[:, bass.ds(g * GI, GI), :]).then_inc(s_mg[u % 2], 16)

                def body(b):
                    for u in range(GPB):
                        load(b, u)
                per_batch(sp, body)

            @block.gpsimd
            def _(pool):
                V = nc.gpsimd

                def stage(b, u):
                    g = GPB * b + u
                    wait(pool, s_s1, g - 1)
                    V.tensor_copy(ts[:, u % 2], tt[:, :, bass.ds(g * GI, GI)]).then_inc(s_ts, 1)

                def scale(b, u):
                    g = GPB * b + u
                    pool.wait_ge(s_mg[u % 2], 32 * (nth(b, u) + 1))
                    V.tensor_tensor(mg[:, u % 2], mg[:, u % 2], bc(c2b[:, bass.ds(g * GI, GI)], 2, WW), ALU.mult).then_inc(s_m7, 1)
                    pool.wait_ge(s_m7, g + 1)
                    V.tensor_tensor(mg[:, u % 2], mg[:, u % 2], xg[:, u % 2], ALU.add).then_inc(s_p7, 1)

                def keep_output(b, u):
                    g = GPB * b + u
                    pool.wait_ge(s_add, g + 1)
                    pool.dma_start(yall[:, bass.ds(g * GI, GI), :], xn[:, u % 2]).then_inc(s_k[u % 2], 16)

                def body(b):
                    for u in range(GPB):
                        lagged(b, u, 0, stage)
                        lagged(b, u, 0, scale)
                        lagged(b, u, 1, keep_output)
                per_batch(pool, body)
                keep_output(NB - 1, GPB - 1)
                for q in s_k:
                    pool.wait_ge(q, 16 * NGRP // 2)

            @block.tensor
            def _(pe):
                pe.wait_ge(s_qh, 16)

                def forward_h(b, u):
                    g = GPB * b + u
                    pe.wait_ge(s_add, g + 1)
                    wait(pe, s_e1, g)
                    for i in range(GI):
                        m = nc.tensor.matmul(pf[:, 128 * i:128 * i + 128], xn[:, u % 2, i, :], qh[:, :], start=True, stop=True)
                    m.then_inc(s_f1, 1)

                def body(b):
                    for u in range(GPB):
                        lagged(b, u, 0, lambda c_, v: inverse_h(pe, c_, v, ts, pz, s_ts, s_s1, s_z))
                        lagged(b, u, 1, forward_h)
                        lagged(b, u, 0, lambda c_, v: inverse_w(pe, c_, v, zs, pi, s_z, s_s2, s_add))
                per_batch(pe, body)
                forward_h(NB - 1, GPB - 1)

            @block.scalar
            def _(act):
                def rows_back(b, u):
                    g = GPB * b + u
                    act.wait_ge(s_s1, g + 1)
                    wait(act, s_s2, g - 1)
                    act.activation(zs[:, u % 2], pz[:, :].rearrange("m (i h) -> m i h", i=GI), ACT.Copy).then_inc(s_z, 1)

                def forward_copy(b, u):
                    g = GPB * b + u
                    act.wait_ge(s_f1, g + 1)
                    v = pf[:, :].rearrange("w (i k) -> w i k", i=GI)
                    act.activation(y1[:, bass.ds(g * GI, GI), 0:65], v[:, :, 0:65], ACT.Copy)
                    act.activation(y1[:, bass.ds(g * GI, GI), 66:129], v[:, :, 65:128], ACT.Copy).then_inc(s_e1, 1)

                def body(b):
                    for u in range(GPB):
                        lagged(b, u, 0, rows_back)
                        lagged(b, u, 1, forward_copy)
                per_batch(act, body)
                forward_copy(NB - 1, GPB - 1)
                act.wait_ge(s_e1, NGRP)

            @block.vector
            def _(dve):
                V = nc.vector
                V.memset(y1[:, :, 65:130:64], 0.0)

                def hidden(b, u):
                    g = GPB * b + u
                    wait(dve, s_f1, g - 1)
                    wait(dve, s_k[u % 2], 16 * nth(b, u))
                    V.tensor_tensor(xn[:, u % 2], yall[:, bass.ds(g * GI, GI), :], bc(c1b[:, bass.ds(g * GI, GI)], 2, WW), ALU.mult).then_inc(s_h7, 1)
                    dve.wait_ge(s_h7, g + 1)
                    dve.wait_ge(s_p7, g + 1)
                    V.tensor_tensor(xn[:, u % 2], xn[:, u % 2], mg[:, u % 2], ALU.add).then_inc(s_q7, 1)
                    dve.wait_ge(s_q7, g + 1)
                    dve.wait_ge(s_s2, g + 1)
                    V.tensor_tensor(xn[:, u % 2], xn[:, u % 2], pi[:, :].rearrange("h (i w) -> h i w", i=GI), ALU.add).then_inc(s_add, 1)

                def body(b):
                    for u in range(GPB):
                        hidden(b, u)
                per_batch(dve, body)

        with ExitStack() as p8:
            def sb(name, shape):
                return p8.enter_context(nc.sbuf_tensor(name, shape, F32))

            def pb(name, shape):
                return p8.enter_context(nc.psum_tensor(name, shape, F32))

            yg = sb("yg8", [128, 2, GI, 256])
            sq = sb("sq8", [128, GI * 130])
            en = sb("en8", [128, NB, GPB])
            en2 = sb("en8b", [128, NB])
            mo = sb("mo8", [128, 2, NB])
            gs = sb("gs8", [128, 5, NB])
            xst = sb("xst8", [128, 2, 3, GI, KWF])
            wa, wb8 = (sb(n, [128, 2 * KWF]) for n in ("wa", "wb8"))
            gmean = sb("gmean", [128, 128])
            px = [pb(f"px8_{i}", [128, 3 * 512]) for i in range(2)]
            pg = pb("pg8", [128, 512])
            s_ld = sem("p8_matrices_loaded")
            s_sq8 = sem("p8_squares_summed")
            s_v8, s_mo8, s_gm8, s_rt8 = sem("p8_vector_steps"), sem("p8_moments_ready"), sem("p8_group_moments_ready"), sem("p8_scales_ready")
            s_sc8, s_yg = sem("p8_group_scaled"), sem("p8_group_normed")
            root = Root(sem("p8_root_asked"), sem("p8_root_given"))
            s_w8, s_p8, s_n8, s_st8 = sem("p8_w_transform_done"), sem("p8_planes_copied"), sem("p8_negative_plane_ready"), sems("layer1_spectrum_stored", 2)
            block = p8.enter_context(nc.Block())

            @block.sync
            def _(sp):
                for t, n in ((wa, "wa"), (wb8, "wb8"), (gmean, "gmean")):
                    sp.dma_start(t[:, :], c[n]).then_inc(s_ld, 16)

                def store(b):
                    for u in range(GPB):
                        g = GPB * b + u
                        sp.wait_ge(s_n8, g + 1)
                        for p in range(3):
                            sp.dma_start(x1s[p, bass.ds(g * GI, GI)].rearrange("i s w -> s i w"), xst[:, u % 2, p]).then_inc(s_st8[u % 2], 16)
                per_batch(sp, store)
                for q in s_st8:
                    sp.wait_ge(q, 48 * NGRP // 2)

            @block.tensor
            def _(pe):
                pe.wait_ge(s_ld, 48)
                pe.wait_ge(s_mo8, 1)
                nc.tensor.matmul(pg[:, 0:2 * NB], gmean[:, :], mo[:, :, :].rearrange("p a b -> p (a b)"), start=True, stop=True).then_inc(s_gm8, 1)

                def transform(b):
                    for u in range(GPB):
                        g = GPB * b + u
                        pe.wait_ge(s_yg, g + 1)
                        wait(pe, s_p8, g - 1)
                        for i in range(GI):
                            o = 512 * (i // 3) + 130 * (i % 3)
                            dst = px[u % 2][:, o:o + 130]
                            src = yg[:, u % 2, i]
                            nc.tensor.matmul(dst, src[:, 0:128], wa[:, :], start=True, stop=False)
                            m = nc.tensor.matmul(dst, src[:, 128:256], wb8[:, :], start=False, stop=True)
                        m.then_inc(s_w8, 1)
                per_batch(pe, transform)

            @block.scalar
            def _(act):
                ch = [0]
                for b in range(NB):
                    for q in range(GPB):
                        i = (b * GPB + q) * GI
                        act.wait_ge(s_sq8, ch[0])
                        act.activation(sq[:, :], y1[:, i:i + GI, :].rearrange("w i k -> w (i k)"), ACT.Square, accum_out=en[:, b, q:q + 1]).then_inc(s_sq8, 1)
                        ch[0] += 1
                    act.wait_ge(s_sq8, ch[0])
                    act.activation(sq[:, 0:2 * NT].rearrange("w (i k) -> w i k", k=2), y1[:, NT * b:NT * b + NT, 0:65:64], ACT.Square, accum_out=en2[:, b:b + 1]).then_inc(s_sq8, 1)
                    ch[0] += 1
                root.serve(act, nc.scalar, gs[:, 2, :])
                act.wait_ge(s_rt8, 1)

                def norm(b):
                    for u in range(GPB):
                        g = GPB * b + u
                        wait(act, s_w8, g - 1)
                        for at, first, row in ((0, 0, 2), (64, 1, 2), (128, 65, 2), (192, 66, 4)):
                            m = act.activation(yg[:, u % 2, :, at:at + 64], y1[:, bass.ds(g * GI, GI), first:first + 64], ACT.Copy, scale=gs[:, row, b:b + 1])
                        m.then_inc(s_sc8, 1)
                        act.wait_ge(s_sc8, g + 1)
                        act.activation(yg[:, u % 2, :, 0:1], yg[:, u % 2, :, 0:1], ACT.Identity, bias=gs[:, 3, b:b + 1]).then_inc(s_yg, 1)
                for b in range(NB):
                    norm(b)

            @block.vector
            def _(dve):
                ch = Chain(dve, s_v8)
                V = nc.vector
                ch.link(V.reduce_sum(mo[:, 0, :], y1[:, :, 0].rearrange("w (b i) -> w b i", b=NB), axis=AX.X))
                dve.wait_ge(s_sq8, NB * (GPB + 1))
                ch.link(V.reduce_sum(mo[:, 1, :], en[:, :, :], axis=AX.X))
                ch.link(V.tensor_scalar(mo[:, 1, :], mo[:, 1, :], 2.0, None, ALU.mult))
                ch.link(V.tensor_tensor(mo[:, 1, :], mo[:, 1, :], en2[:, :], ALU.subtract))
                V.tensor_scalar(mo[:, :, :], mo[:, :, :], 1.0 / NT, None, ALU.mult).then_inc(s_mo8, 1)
                dve.wait_ge(s_gm8, 1)
                ch.link(V.tensor_copy(gs[:, 0:2, :], pg[:, 0:2 * NB].rearrange("p (a b) -> p a b", a=2)))
                ch.link(V.tensor_tensor(gs[:, 2, :], gs[:, 0, :], gs[:, 0, :], ALU.mult))
                ch.link(V.tensor_tensor(gs[:, 2, :], gs[:, 1, :], gs[:, 2, :], ALU.subtract))
                root.rsqrt(dve, ch, V, gs[:, 2, :], gs[:, 2, :])
                ch.link(V.tensor_scalar(gs[:, 4, :], gs[:, 2, :], -1.0, None, ALU.mult))
                ch.link(V.tensor_tensor(gs[:, 3, :], gs[:, 0, :], gs[:, 2, :], ALU.mult))
                V.tensor_scalar(gs[:, 3, :], gs[:, 3, :], -1.0, None, ALU.mult).then_inc(s_rt8, 1)

                def copy(b):
                    for u in range(GPB):
                        g = GPB * b + u
                        dve.wait_ge(s_w8, g + 1)
                        wait(dve, s_st8[u % 2], 48 * nth(b, u))
                        for q in range(3):
                            n = min(3, GI - 3 * q)
                            m = V.tensor_copy(xst[:, u % 2, 0:2, 3 * q:3 * q + n, :],
                                              px[u % 2][:, 512 * q:512 * q + 130 * n].rearrange("s (i r w) -> s r i w", i=n, r=2))
                        m.then_inc(s_p8, 1)
                        dve.wait_ge(s_p8, g + 1)
                        V.tensor_scalar(xst[:, u % 2, 2], xst[:, u % 2, 0], -1.0, None, ALU.mult).then_inc(s_n8, 1)
                per_batch(dve, copy)
        fwd.close()
        spec.close()

        with ExitStack() as p9:
            def sb(name, shape):
                return p9.enter_context(nc.sbuf_tensor(name, shape, F32))

            def pb(name, shape):
                return p9.enter_context(nc.psum_tensor(name, shape, F32))

            wsl = [sb(f"wsl{i}", [128, NT, SM]) for i in range(2)]
            xsl = [sb(f"xsl{i}", [128, 2, NB, 2, SM]) for i in range(2)]
            osl = [sb(f"osl{i}", [128, 2, NB, 2, KWF]) for i in range(2)]
            po = [pb(f"po9_{i}", [128, 3 * 512]) for i in range(2)]
            s_ws, s_os = sems("slab_loaded", 2), sems("mixed_slab_stored", 2)
            s_ms, s_oc = sem("slab_mixed"), sem("mixed_slab_copied")
            s_free = sem("slab_buffers_cleared")
            block = p9.enter_context(nc.Block())
            SLOT, IMG, PLANE = KWF, HH * KWF, NI * HH * KWF

            @block.sync
            def _(sp):
                wdr = (a["L1_conv_weight_real"].tensor, a["L1_conv_weight_imag"].tensor)
                sp.wait_ge(s_free, 2)

                def load(s, u):
                    wait(sp, s_ms, s - 1)
                    for p in range(2):
                        row0 = 64 + SL * s if p == 0 else SL * s
                        slot0 = SL * s if p == 0 else HH - SL - SL * s
                        for r in range(2):
                            q = slice(64 * p + 32 * r, 64 * p + 32 * r + 32)
                            sp.dma_start(wsl[u][q], bass.AP(wdr[r], row0 * KWF, [[NT * HH * KWF, NT], [HH * KWF, NT], [1, SM]])).then_inc(s_ws[u], 16)
                            for b in range(NB):
                                sp.dma_start(xsl[u][q, p, b], bass.AP(x1s.tensor, r * PLANE + b * NT * IMG + slot0 * SLOT,
                                                                      [[IMG, NT], [PLANE, 2], [1, SM]])).then_inc(s_ws[u], 16)
                load(0, 0)
                load(1, 1)
                with sp.Fori(1, NSLAB // 2) as i:
                    for u in range(2):
                        load(2 * i + u, u)

            @block.tensor
            def _(pe):
                with pe.Fori(0, NSLAB // 2) as i:
                    for u in range(2):
                        s = 2 * i + u
                        pe.wait_ge(s_ws[u], 16 * 20 * (i + 1))
                        pe.wait_ge(s_oc, s + 1)
                        for kw in range(KWF):
                            for q in range(SL):
                                v = xsl[u][:, 0, 0, 0, q * KWF + kw:q * KWF + kw + 1]
                                mov = bass.AP(v.tensor, v.offset, [list(v.ap[0]), [2 * NB * SM + (SL - 1 - 2 * q) * KWF, 2], [SM, 2 * NB]])
                                m = nc.tensor.matmul(po[u][32 * q:32 * q + 32, 16 * kw:16 * kw + 16],
                                                     wsl[u][:, :, q * KWF + KWF - 1 - kw], mov, start=True, stop=True)
                        m.then_inc(s_ms, 1)

            @block.vector
            def _(dve):
                V = nc.vector
                for u in range(2):
                    V.memset(xsl[u][0:64, 1], 0.0)
                    V.memset(xsl[u][64:128, 0], 0.0).then_inc(s_free, 1)
                V.memset(osl[0][:, :, :, :, 0:1], 0.0).then_inc(s_oc, 1)
                V.memset(osl[1][:, :, :, :, 0:1], 0.0).then_inc(s_oc, 1)

                def copy(i, u):
                    s = 2 * i + u
                    dve.wait_ge(s_ms, s + 1)
                    wait(dve, s_os[u], 16 * 8 * i)
                    V.tensor_copy(osl[u][:, :, :, :, :].rearrange("p h b r w -> p (h b r) w"),
                                  po[u][:, 0:16 * KWF].rearrange("p (w c) -> p c w", w=KWF)).then_inc(s_oc, 1)
                copy(0, 0)
                copy(0, 1)
                with dve.Fori(1, NSLAB // 2) as i:
                    for u in range(2):
                        copy(i, u)

            @block.scalar
            def _(act):
                def store(s, u):
                    act.wait_ge(s_oc, s + 3)
                    for q in range(SL):
                        for p in range(2):
                            slot = SL * s + q if p == 0 else HH - 1 - SL * s - q
                            act.dma_start(bass.AP(os_.tensor, slot * SLOT, [[2 * NB * IMG, NT], [IMG, 2 * NB], [1, KWF]]),
                                          osl[u][32 * q:32 * q + 32, p].rearrange("o b r w -> o (b r) w")).then_inc(s_os[u], 16)
                with act.Fori(0, NSLAB // 2) as i:
                    for u in range(2):
                        store(2 * i + u, u)
                for q in s_os:
                    act.wait_ge(q, 16 * 8 * NSLAB // 2)

        with ExitStack() as p10:
            def sb(name, shape):
                return p10.enter_context(nc.sbuf_tensor(name, shape, F32))

            def pb(name, shape):
                return p10.enter_context(nc.psum_tensor(name, shape, F32))

            od = sb("od", [128, GPB, 2, GI, KWF])
            zz = [sb(f"zz{i}", [KWF, 4, 256]) for i in range(2)]
            e1t, e2t = sb("e1t", [128, 256]), sb("e2t", [128, 256])
            cct, cst = sb("cct", [KWF, 128]), sb("cst", [KWF, 128])
            pz = [pb(f"pz10_{i}", [KWF, 1024]) for i in range(2)]
            pi = [pb(f"pi10_{i}", [128, 512]) for i in range(2)]
            s_cl = sem("p10_matrices_loaded")
            s_od, s_h, s_hc = sems("p10_spectra_loaded", GPB), sem("p10_rows_done"), sem("p10_rows_copied")
            s_w, s_fin, s_st = sem("p10_pixels_done"), sem("output_ready"), sem("output_stored")
            block = p10.enter_context(nc.Block())
            HALF = GI // 2

            @block.sync
            def _(sp):
                for t, n in ((e1t, "e1"), (e2t, "e2"), (cct, "cc"), (cst, "cs")):
                    sp.dma_start(t[:, :], c[n]).then_inc(s_cl, 16)

                def load(b):
                    for u in range(GPB):
                        g = GPB * b + u
                        wait(sp, s_h, 2 * (g + 1 - GPB))
                        for r in range(2):
                            sp.dma_start(od[:, u, r], os_[u * GI:(u + 1) * GI, bass.ds(b, 1), r].rearrange("i b s w -> s (i b) w")).then_inc(s_od[u], 16)
                per_batch(sp, load)

            @block.tensor
            def _(pe):
                pe.wait_ge(s_cl, 64)

                def rows_back(b, u, h):
                    g = GPB * b + u
                    pe.wait_ge(s_od[u], 32 * (b + 1))
                    t = 2 * g + h
                    wait(pe, s_hc, t - 1)
                    for j in range(HALF):
                        for r, e in enumerate((e1t, e2t)):
                            m = nc.tensor.matmul(pz[h][:, 256 * j:256 * j + 256], od[:, u, r, HALF * h + j, :], e[:, :], start=(r == 0), stop=(r == 1))
                    m.then_inc(s_h, 1)

                def pixels(b, u, h):
                    g = GPB * b + u
                    t = 2 * g + h
                    pe.wait_ge(s_hc, t + 1)
                    wait(pe, s_fin, t - 1)
                    for j in range(HALF):
                        for r, e in enumerate((cct, cst)):
                            m = nc.tensor.matmul(pi[h][:, 128 * j:128 * j + 128], zz[h][:, j, 128 * r:128 * r + 128], e[:, :], start=(r == 0), stop=(r == 1))
                    m.then_inc(s_w, 1)

                def body(b):
                    for u in range(GPB):
                        g = GPB * b + u
                        rows_back(b, u, 0)
                        lagged(b, u, 1, pixels, 1)
                        rows_back(b, u, 1)
                        pixels(b, u, 0)
                per_batch(pe, body)
                pixels(NB - 1, GPB - 1, 1)

            @block.scalar
            def _(act):
                def body(b):
                    for u in range(GPB):
                        for h in range(2):
                            t = 2 * (GPB * b + u) + h
                            act.wait_ge(s_h, t + 1)
                            wait(act, s_w, t - 1)
                            act.activation(zz[h][:, :, :], pz[h][:, :].rearrange("k (j e) -> k j e", j=HALF), ACT.Copy).then_inc(s_hc, 1)
                per_batch(act, body)

            @block.vector
            def _(dve):
                V = nc.vector

                def body(b):
                    for u in range(GPB):
                        for h in range(2):
                            t = 2 * (GPB * b + u) + h
                            dve.wait_ge(s_w, t + 1)
                            y = yall[:, bass.ds(t * HALF, HALF), :]
                            V.tensor_tensor(y, y, pi[h][:, :].rearrange("h (i w) -> h i w", i=HALF), ALU.add).then_inc(s_fin, 1)
                per_batch(dve, body)

            @block.gpsimd
            def _(pool):
                def store(b):
                    for u in range(GPB):
                        g = GPB * b + u
                        pool.wait_ge(s_fin, 2 * (g + 1))
                        pool.dma_start(xo.rearrange("i h w -> h i w")[:, bass.ds(g * GI, GI), :], yall[:, bass.ds(g * GI, GI), :]).then_inc(s_st, 16)
                per_batch(pool, store)
                pool.wait_ge(s_st, 16 * NGRP)


_INS = ["x"] + ["L0_conv_" + n for n in (
    "norm1_w", "norm1_b", "Kcw", "Ksw", "Qcw", "Qsw", "Vcw", "Vsw", "Pcw", "Psw", "attn_w", "attn_b",
    "norm2_w", "norm2_b", "m0cw", "m0sw", "m1cw", "m1sw", "mon_w", "mon_b")] + ["L1_conv_weight_real", "L1_conv_weight_imag"]


def kernel(**inputs):
    import numpy as _np
    import concourse.bacc as _bacc
    from concourse import mybir as _mybir
    from concourse.bass_utils import run_bass_kernel_spmd as _run

    nc = _bacc.Bacc("TRN2", target_bir_lowering=False, num_devices=1)
    arrays, a, c = {}, {}, {}
    for name in _INS:
        v = _np.ascontiguousarray(inputs[name])
        arrays[f"in_{name}_dram"] = v
        a[name] = nc.dram_tensor(f"in_{name}_dram", v.shape, _mybir.dt.from_np(v.dtype), kind="ExternalInput").ap()
    for name, v in constants().items():
        arrays[f"const_{name}_dram"] = v
        c[name] = nc.dram_tensor(f"const_{name}_dram", v.shape, _mybir.dt.float32, kind="ExternalInput").ap()
    out = nc.dram_tensor("out_0_dram", (NB, NT, HH, WW), _mybir.dt.float32, kind="ExternalOutput").ap()
    build(nc, a, c, out)
    r = _run(nc, [arrays], core_ids=[0])
    return r.results[0]["out_0_dram"]
```

```python
import math

import numpy as np

import concourse.bass as bass
from concourse import mybir
from contextlib import ExitStack

F32 = mybir.dt.float32
ALU = mybir.AluOpType
ACT = mybir.ActivationFunctionType
AX = mybir.AxisListType

NB, NT, NHD = 4, 32, 32
HH = WW = 128
NI = NB * NT
NG = 32
KW, KH = 33, 64
M2 = KW * KH
RW, RH = 17, 32
NUN = 3 * RW + 1
NCH = NUN // 4
GI = 8
NGRP = NI // GI
GPB = NT // GI
EPS = 1e-5
KWF = WW // 2 + 1
CB = 3
NBLK = KW // CB
MB = CB * KH
PB = 4
NCK = NHD // PB
SL = 4
NSLAB = HH // 2 // SL
SM = SL * KWF
SCALARS = ["norm1_w", "norm1_b", "attn_w", "attn_b", "norm2_w", "norm2_b", "m0sw", "m1sw", "mon_w", "mon_b"]


def constants():
    c = {}
    n = np.arange(128)
    k = np.concatenate([np.arange(32), np.arange(-32, 0)])
    j = np.arange(KW)
    ph = 2 * np.pi * np.outer(n, k) / 128
    c["fh"] = np.concatenate([np.cos(ph), -np.sin(ph)], 1) / 128
    th = 2 * np.pi * np.outer(n, j) / 128
    c["fw1"] = np.stack([np.cos(th), -np.sin(th)], 2).reshape(128, -1) / 128
    c["fw2"] = np.stack([np.sin(th), np.cos(th)], 2).reshape(128, -1) / 128
    c["eh"] = np.concatenate([np.cos(ph).T, -np.sin(ph).T], 0)
    wt = np.where(j == 0, 1.0, 2.0)[:, None]
    c["cw"] = np.concatenate([wt * np.cos(th).T, -wt * np.sin(th).T], 0)
    c["ident"] = np.eye(128)
    c["ones"] = np.ones((128, 128))
    b = np.arange(128) // 32
    c["bmean"] = (b[:, None] == b[None, :]) / 32.0
    c["sel"] = (np.arange(128)[:, None] == 32 * np.arange(4)[None, :]) * 1.0
    c["gmean"] = (n[:, None] // 4 == n[None, :] // 4) / 4.0
    def sym(rows_in, rows_out):
        m = np.zeros((2, len(rows_in), 2, len(rows_out)))
        for a, ki in enumerate(rows_in):
            for o, ko in enumerate(rows_out):
                for s in (0, 1):
                    if ki == ko:
                        m[s, a, s, o] += 0.5
                    if ki == -ko:
                        m[s, a, s, o] += 0.5 if s == 0 else -0.5
        return m.reshape(2 * len(rows_in), 2 * len(rows_out))
    c["sym"] = sym(k, k)
    kr = np.concatenate([np.arange(16), np.arange(-16, 0)])
    c["symv"] = sym(kr, k)
    c["symr"] = sym(kr, kr)
    cm = np.zeros((NUN, RH))
    for f in range(3):
        cm[f * RW:f * RW + RW] = 64 * 2.0
        cm[f * RW] = 64 * np.where(kr == -16, 2.0, 1.0)
    cm = cm.reshape(NCH, 128).T
    c["cm"] = cm
    wg = np.zeros((128, KW))
    inside = (k >= -16) & (k < 16)
    for kw in range(KW):
        if kw == 0:
            w = np.where(np.abs(k) <= 16, 0.0, 1.0)
            wg[:, 0] = np.concatenate([w, np.where(k == -32, 0.0, w)])
        elif kw < 32:
            w = np.where(inside, 0.0, 2.0) if kw < RW else np.full(64, 2.0)
            wg[:, kw] = np.concatenate([w, w])
    c["wg"] = 64 * wg
    s = sym(k, k)
    r = list(k).index(-32)
    s[:, r] = 0
    s[:, 64 + r] = 0
    s[r, r] = 1
    c["ny"] = 64 * (s @ s.T)
    ka, kb = np.arange(65), np.arange(1, 64)
    c["qh"] = np.concatenate([np.cos(2 * np.pi * np.outer(n, ka) / 128), np.sin(2 * np.pi * np.outer(n, kb) / 128)], 1) / 128
    kf = np.arange(KWF)
    tf = 2 * np.pi * np.outer(n, kf) / 128
    cc, ss = np.cos(tf) / 128, np.sin(tf) / 128
    c["wa"] = np.concatenate([cc, -ss], 1)
    c["wb8"] = np.concatenate([-ss, -cc], 1)
    slot = np.concatenate([np.arange(64), -np.arange(1, 65)])
    ps = 2 * np.pi * np.outer(slot, n) / 128
    c["ec"] = np.cos(ps)
    c["es"] = -np.sin(ps)
    wf = np.where((kf == 0) | (kf == 64), 1.0, 2.0)[:, None]
    c["cf"] = np.concatenate([wf * np.cos(tf).T, -wf[1:64] * np.sin(tf).T[1:64]], 0)
    return {k2: np.ascontiguousarray(v, dtype=np.float32) for k2, v in c.items()}


def bc(ap, dim, n):
    v = ap.unsqueeze(dim)
    shape = list(v.shape)
    shape[dim] = n
    return v.broadcast_to(shape)


class Chain:

    def __init__(self, eng, sem):
        self.eng, self.sem, self.n = eng, sem, 0

    def link(self, ins):
        self.n += 1
        ins.then_inc(self.sem, 1)
        self.eng.wait_ge(self.sem, self.n)


class Root:

    def __init__(self, asked, given):
        self.asked, self.given, self.n, self.m = asked, given, 0, 0

    def rsqrt(self, dve, ch, V, out, var):
        self.n += 1
        V.tensor_scalar(out, var, EPS, None, ALU.add).then_inc(self.asked, 1)
        dve.wait_ge(self.given, self.n)
        ch.link(V.reciprocal(out, out))

    def serve(self, act, A, out):
        self.m += 1
        act.wait_ge(self.asked, self.m)
        A.activation(out, out, ACT.Sqrt).then_inc(self.given, 1)


def nth(b, u):
    return GPB // 2 * b + u // 2


def wait(eng, sem, value):
    if not (isinstance(value, int) and value <= 0):
        eng.wait_ge(sem, value)


def per_batch(eng, body):
    body(0)
    with eng.Fori(1, NB) as b:
        body(b)


def build(nc, a, c, out):
    x = a["x"].rearrange("b t h w -> (b t) h w")
    xf = x.rearrange("i h w -> i (h w)")
    xo = out.rearrange("b t h w -> (b t) h w")

    def dram(name, shape):
        return nc.dram_tensor(name, shape, F32, kind="Internal").ap()

    xs = dram("xs", (NI, 2 * KW, KH))
    xns = dram("xns", (NI, 3, M2))
    wv = dram("wv", (PB, NBLK, NCK, 3, MB))
    mixd = dram("mixd", (NI, HH, WW))
    ys = dram("ys", (NI, 2 * KW, KH))
    x1s = dram("x1s", (NT, NB, HH, 2 * KWF))
    os_ = dram("os_", (NT, NB, HH, 2 * KWF))

    top = ExitStack()
    names, held = set(), []
    POOL_TRANSFERS = ("mixed_images_stored_0", "mixed_images_stored_1", "spectrum_stored_0", "spectrum_stored_1")

    def sems(name, n):
        return [sem(f"{name}_{i}") for i in range(n)]

    def sem(name):
        assert name not in names
        names.add(name)
        h = nc.alloc_semaphore(name=name)
        if name not in POOL_TRANSFERS:
            held.append(h)
        return h

    def recycle():
        with nc.Block() as block:
            @block.gpsimd
            def _(pool):
                for h in held:
                    pool.sem_clear(h)
        while held:
            nc.release_semaphore(held.pop())

    with top:
        def keep(name, shape):
            return top.enter_context(nc.sbuf_tensor(name, shape, F32))

        fh = keep("fh", [128, 128])
        fw1 = keep("fw1", [128, 2 * KW])
        fw2 = keep("fw2", [128, 2 * KW])
        eh = keep("eh", [128, 128])
        cw = keep("cw", [2 * KW, 128])
        ident = keep("ident", [128, 128])
        ones = keep("ones", [128, 128])
        bmean = keep("bmean", [128, 128])
        sel = keep("sel", [128, 4])
        sym = keep("sym", [128, 128])
        sc = keep("sc", [128, len(SCALARS)])
        vec = keep("vec", [128, 64])
        kept = [("fh", fh), ("fw1", fw1), ("fw2", fw2), ("eh", eh), ("cw", cw), ("ident", ident),
                ("ones", ones), ("bmean", bmean), ("sel", sel), ("sym", sym)]
        scalar = {n: sc[:, i:i + 1] for i, n in enumerate(SCALARS)}
        vnames = {}
        mt = keep("mt", [128, NI])
        pa = keep("pa", [128, KW, 2, KH])

        def v1(name):
            i = vnames.setdefault(name, len(vnames))
            return vec[:, i:i + 1]

        s_const = sem("const_loaded")
        att = ExitStack()
        xa = att.enter_context(nc.sbuf_tensor("xa", [128, HH * WW], F32))
        gt = att.enter_context(nc.sbuf_tensor("gt", [128, NCH, NHD], F32))
        vpb = att.enter_context(nc.sbuf_tensor("vpb", [128, NHD], F32))
        qkb = att.enter_context(nc.sbuf_tensor("qkb", [128, NHD], F32))

        with ExitStack() as p1:
            def sb(name, shape):
                return p1.enter_context(nc.sbuf_tensor(name, shape, F32))

            def pb(name, shape):
                return p1.enter_context(nc.psum_tensor(name, shape, F32))

            xd = sb("xd", [128, GPB, GI * WW])
            yb = sb("yb", [128, 2, 2, GI, KH])
            xst = sb("xst", [2 * KW, 2, GI, KH])
            st = sb("st", [128, NG, 2, 6])
            mv = sb("mv", [128, NG, 2])
            me = sb("me", [128, 2, NG])
            gs = sb("gs", [128, 4, NG])
            rw = sb("rw", [128, 2, WW])
            rt = sb("rt", [128, 2, NB])
            tmpg = sb("tmpg", [128, 2, NG])
            praw = sb("praw", [NHD, KH, KW, 2])
            pr = sb("pr", [NHD, 2, KW, KH])
            vf = sb("vf", [NHD, 2, KW, KH])
            wt = praw[:, :, :, :].rearrange("n h w r -> n (h w r)").rearrange("n (z w h) -> n z w h", z=2, w=KW)
            kvq = sb("kvq", [NHD, 3, RH * RW * 2])
            kq = sb("kq", [NHD, 2, 2, RW, RH])
            col = sb("col", [NHD, 3, 2, RH])
            colt = sb("colt", [2 * RH, 3, NHD])
            gg = sb("gg", [NHD, NUN, RH])
            hs = sb("hs", [NHD, 4])
            rows = sb("rows", [128, 4, NHD])
            symv = sb("symv", [2 * RH, 2 * KH])
            symr = sb("symr", [2 * RH, 2 * RH])
            cm = sb("cm", [128, NCH])
            f1 = [pb(f"f1_{i}", [128, GI * 128]) for i in range(2)]
            f2 = [pb(f"f2_{i}", [2 * KW, GI * KH]) for i in range(2)]
            pg = pb("pg", [128, 512])
            pw = pb("pw", [128, 512])

            s_x = sems("image_rows_loaded", 2)
            s_xd = sems("row_group_loaded", GPB)
            s_w = sem("weights_loaded")
            s_f1 = sem("h_transform_done")
            s_e1 = sem("h_transform_copied")
            s_f2 = sem("w_transform_done")
            s_e2 = sem("w_transform_copied")
            s_xs = sems("spectrum_stored", 2)
            s_c1 = sem("p1_vector_steps")
            s_me = sem("local_moments_ready")
            s_gm = sem("group_moments_ready")
            s_rw = sem("scale_rows_ready")
            s_rt = sem("scales_by_column_ready")
            s_rts = sem("scales_copied")
            s_dc = sem("p1_scalar_steps")
            s_col = sem("weight_columns_ready")
            s_ct = sem("weight_columns_transposed")
            s_cts = sem("weight_columns_copied")
            s_sy = sem("weight_columns_symmetrised")
            s_gg = sem("score_weights_ready")
            s_gt = sem("score_weights_transposed")
            s_gts = sem("score_weights_copied")
            s_wt = sem("value_weights_ready")
            s_wv = sem("value_weights_stored")
            root = Root(sem("p1_root_asked"), sem("p1_root_given"))
            NW = 3 + 4 + 4 + 4
            block = p1.enter_context(nc.Block())

            @block.sync
            def _(sp):
                for i in range(4):
                    n = HH * WW // 4
                    sp.dma_start(xa[:, i * n:(i + 1) * n], xf[:, i * n:(i + 1) * n]).then_inc(s_x[i // 2], 16)

                def load(b):
                    for u in range(GPB):
                        wait(sp, s_f1, GPB * b + u + 1 - GPB)
                        sp.dma_start(xd[:, u, :].rearrange("h (g w) -> h g w", g=GI),
                                     x[bass.ds((b * GPB + u) * GI, GI)].rearrange("g h w -> h g w")).then_inc(s_xd[u], 16)
                per_batch(sp, load)
                sp.wait_ge(s_wt, 1)
                for k in range(NCK):
                    for r, v in enumerate((wt[:, 0], vf[:, 0], vf[:, 1])):
                        v = v.rearrange("n w h -> n (w h)").rearrange("n (q m) -> n q m", m=MB)
                        sp.dma_start(wv[:, :, k, r], v[PB * k:PB * k + PB]).then_inc(s_wv, 16)
                sp.wait_ge(s_wv, 16 * 3 * NCK)

            @block.gpsimd
            def _(pool):
                def store(b):
                    for u in range(GPB):
                        g = GPB * b + u
                        pool.wait_ge(s_e2, g + 1)
                        pool.dma_start(xs[bass.ds(g * GI, GI)].rearrange("i m k -> m i k"),
                                       xst[:, u % 2]).then_inc(s_xs[u % 2], 16)
                per_batch(pool, store)
                for q in s_xs:
                    pool.wait_ge(q, 16 * NGRP // 2)

            @block.scalar
            def _(act):
                for n, t in kept:
                    act.dma_start(t[:, :], c[n]).then_inc(s_const, 16)
                for i, n in enumerate(SCALARS):
                    src = a["L0_conv_" + n]
                    act.dma_start(sc[:, i:i + 1], bass.AP(src.tensor, 0, [[0, 128], [1, 1]])).then_inc(s_const, 16)
                for t, n in ((symv, "symv"), (symr, "symr"), (cm, "cm")):
                    act.dma_start(t[:, :], c[n]).then_inc(s_w, 16)
                for i, n in enumerate(("Ksw", "Qsw", "Vsw", "Psw")):
                    src = a["L0_conv_" + n]
                    act.dma_start(hs[:, i:i + 1], bass.AP(src.tensor, 0, [[1, NHD], [1, 1]])).then_inc(s_w, 16)
                    act.dma_start(rows[:, i, :], bass.AP(src.tensor, 0, [[0, 128], [1, NHD]])).then_inc(s_w, 16)
                for i, n in enumerate(("Kcw", "Qcw", "Vcw")):
                    act.dma_start(kvq[:, i, :], a["L0_conv_" + n].rearrange("a n h w r -> (a n) (h w r)")).then_inc(s_w, 16)
                act.dma_start(praw[:, :, :, :], a["L0_conv_Pcw"].rearrange("n a h w r -> (n a) h w r")).then_inc(s_w, 16)
                root.serve(act, nc.scalar, gs[:, 2, :])
                act.wait_ge(s_rts, 1)
                root.serve(act, nc.scalar, v1("alpha"))
                dc = [0]

                def copy_w(b, u):
                    g = GPB * b + u
                    act.wait_ge(s_f2, g + 1)
                    wait(act, s_xs[u % 2], 16 * nth(b, u))
                    act.activation(xst[:, u % 2], f2[u % 2][:, :].rearrange("m (i k) -> m i k", i=GI),
                                   ACT.Copy).then_inc(s_e2, 1)

                def copy(b):
                    for u in range(GPB):
                        g = GPB * b + u
                        act.wait_ge(s_f1, g + 1)
                        wait(act, s_f2, g - 1)
                        act.activation(yb[:, u % 2], f1[u % 2][:, :].rearrange("w (i r k) -> w r i k", i=GI, r=2),
                                       ACT.Copy, scale=rt[:, 0, b:b + 1]).then_inc(s_dc, 1)
                        act.wait_ge(s_dc, g + 1)
                        act.activation(yb[:, u % 2, 0, :, 0:1], yb[:, u % 2, 0, :, 0:1],
                                       ACT.Identity, bias=rt[:, 1, b:b + 1]).then_inc(s_e1, 1)
                        if u:
                            copy_w(b, u - 1)
                        elif not (isinstance(b, int) and b == 0):
                            copy_w(b - 1, GPB - 1)
                for b in range(NB):
                    copy(b)
                copy_w(NB - 1, GPB - 1)

            @block.tensor
            def _(pe):
                pe.wait_ge(s_const, 16 * (len(kept) + len(SCALARS)))
                pe.wait_ge(s_me, 1)
                nc.tensor.matmul(pg[:, 0:2 * NG], bmean[:, :], me[:, :, :].rearrange("p a g -> p (a g)"),
                                 start=True, stop=True).then_inc(s_gm, 1)
                pe.wait_ge(s_rw, 1)
                for i in range(2):
                    m = nc.tensor.matmul(pg[:, 128 + 4 * i:132 + 4 * i], rw[:, i, :], sel[:, :],
                                         start=True, stop=True)
                m.then_inc(s_rt, 1)
                pe.wait_ge(s_col, 1)
                for i in range(3):
                    m = nc.tensor.transpose(pw[0:2 * RH, 32 * i:32 * i + 32],
                                            col[:, i].rearrange("n r h -> n (r h)"), ident[0:NHD, 0:NHD])
                m.then_inc(s_ct, 1)
                pe.wait_ge(s_cts, 1)
                nc.tensor.matmul(pw[0:NHD, 128:192], colt[:, 0, :], symr[:, :], start=True, stop=True)
                nc.tensor.matmul(pw[0:NHD, 192:256], colt[:, 1, :], symr[:, :], start=True, stop=True)
                nc.tensor.matmul(pw[0:NHD, 256:384], colt[:, 2, :], symv[:, :], start=True, stop=True).then_inc(s_sy, 1)

                def w_transform(b, u):
                    g = GPB * b + u
                    pe.wait_ge(s_e1, g + 1)
                    wait(pe, s_e2, g - 1)
                    for r, f in enumerate((fw1, fw2)):
                        m = nc.tensor.matmul(f2[u % 2][:, :], f[:, :],
                                             yb[:, u % 2, r].rearrange("w i k -> w (i k)"),
                                             start=(r == 0), stop=(r == 1))
                    m.then_inc(s_f2, 1)

                def transform(b):
                    for u in range(GPB):
                        g = GPB * b + u
                        pe.wait_ge(s_xd[u], 16 * (b + 1))
                        wait(pe, s_e1, g - 1)
                        for i in range(GI):
                            m = nc.tensor.matmul(f1[u % 2][:, 128 * i:128 * i + 128],
                                                 xd[:, u, WW * i:WW * i + WW], fh[:, :], start=True, stop=True)
                        m.then_inc(s_f1, 1)
                        if u:
                            w_transform(b, u - 1)
                        elif not (isinstance(b, int) and b == 0):
                            w_transform(b - 1, GPB - 1)
                per_batch(pe, transform)
                w_transform(NB - 1, GPB - 1)
                pe.wait_ge(s_gg, 1)
                for ch in range(NCH):
                    m = nc.tensor.transpose(f1[0][:, 32 * ch:32 * ch + 32],
                                            gg[:, 4 * ch:4 * ch + 4].rearrange("n c h -> n (c h)"), ident[0:NHD, 0:NHD])
                m.then_inc(s_gt, 1)

            @block.vector
            def _(dve):
                ch = Chain(dve, s_c1)
                V = nc.vector
                xv = xa[:, :].rearrange("p (h g q) -> p g h q", g=NG, q=4)
                for i in range(2):
                    dve.wait_ge(s_x[i], 32)
                    for g in range(NG):
                        s = V.bn_stats(st[:, g, i, :], xv[:, g, 64 * i:64 * i + 64])
                ch.link(s)
                for g in range(NG):
                    s = V.bn_aggr(mv[:, g, :], st[:, g].rearrange("p i s -> p (i s)"))
                ch.link(s)
                ch.link(V.tensor_copy(me[:, 0, :], mv[:, :, 0]))
                ch.link(V.tensor_tensor(me[:, 1, :], mv[:, :, 0], mv[:, :, 0], ALU.mult))
                V.tensor_tensor(me[:, 1, :], me[:, 1, :], mv[:, :, 1], ALU.add).then_inc(s_me, 1)
                dve.wait_ge(s_gm, 1)
                ch.link(V.tensor_copy(gs[:, 0:2, :], pg[:, 0:2 * NG].rearrange("p (a g) -> p a g", a=2)))
                ch.link(V.tensor_tensor(gs[:, 2, :], gs[:, 0, :], gs[:, 0, :], ALU.mult))
                ch.link(V.tensor_tensor(gs[:, 2, :], gs[:, 1, :], gs[:, 2, :], ALU.subtract))
                root.rsqrt(dve, ch, V, gs[:, 2, :], gs[:, 2, :])
                ch.link(V.tensor_tensor(gs[:, 3, :], gs[:, 0, :], gs[:, 2, :], ALU.mult))
                ch.link(V.tensor_scalar(gs[:, 3, :], gs[:, 3, :], -1.0, None, ALU.mult))
                ch.link(V.tensor_copy(rw[:, 0, :].rearrange("p (g q) -> p g q", q=4), bc(gs[:, 2, :], 2, 4)))
                V.tensor_copy(rw[:, 1, :].rearrange("p (g q) -> p g q", q=4), bc(gs[:, 3, :], 2, 4)).then_inc(s_rw, 1)
                dve.wait_ge(s_rt, 1)
                V.tensor_copy(rt[:, :, :], pg[:, 128:136].rearrange("p (a b) -> p a b", a=2)).then_inc(s_rts, 1)
                dve.wait_ge(s_w, 16 * NW)
                kv = [kvq[:, i, :].rearrange("n (h w r) -> n r w h", h=RH, w=RW) for i in range(3)]
                for i in range(3):
                    s = V.tensor_copy(col[:, i], kv[i][:, :, 0, :])
                s.then_inc(s_col, 1)
                dve.wait_ge(s_ct, 1)
                V.tensor_copy(colt[:, :, :], pw[0:2 * RH, 0:96].rearrange("m (i n) -> m i n", i=3)).then_inc(s_cts, 1)
                ch.link(V.tensor_tensor(tmpg[:, 0, :], me[:, 0, :], gs[:, 2, :], ALU.mult))
                ch.link(V.tensor_tensor(tmpg[:, 0, :], tmpg[:, 0, :], gs[:, 3, :], ALU.add))
                ch.link(V.reduce_sum(v1("mean"), tmpg[:, 0, :], axis=AX.X))
                ch.link(V.tensor_scalar(v1("mean"), v1("mean"), 1.0 / NG, None, ALU.mult))
                ch.link(V.tensor_scalar(tmpg[:, 0, :], tmpg[:, 0, :], v1("mean"), None, ALU.subtract))
                ch.link(V.tensor_tensor(tmpg[:, 0, :], tmpg[:, 0, :], tmpg[:, 0, :], ALU.mult))
                ch.link(V.tensor_tensor(tmpg[:, 1, :], gs[:, 2, :], gs[:, 2, :], ALU.mult))
                ch.link(V.tensor_tensor(tmpg[:, 1, :], tmpg[:, 1, :], mv[:, :, 1], ALU.mult))
                ch.link(V.tensor_tensor(tmpg[:, 0, :], tmpg[:, 0, :], tmpg[:, 1, :], ALU.add))
                ch.link(V.reduce_sum(v1("alpha"), tmpg[:, 0, :], axis=AX.X))
                ch.link(V.tensor_scalar(v1("alpha"), v1("alpha"), 1.0 / NG, None, ALU.mult))
                root.rsqrt(dve, ch, V, v1("alpha"), v1("alpha"))
                dve.wait_ge(s_const, 16 * (len(kept) + len(SCALARS)))
                ch.link(V.tensor_tensor(v1("alpha"), v1("alpha"), scalar["norm1_w"], ALU.mult))
                ch.link(V.tensor_tensor(v1("beta"), v1("alpha"), v1("mean"), ALU.mult))
                ch.link(V.tensor_tensor(v1("beta"), scalar["norm1_b"], v1("beta"), ALU.subtract))
                for i in range(2):
                    for r in range(2):
                        s = V.tensor_copy(kq[:, i, r], kv[i][:, r])
                V.memset(vf[:, :, :, :], 0.0)
                for r in range(2):
                    s = V.tensor_copy(pr[:, r], praw[:, :, :, r].rearrange("n h w -> n w h"))
                ch.link(s)
                V.tensor_copy(vf[:, :, 1:RW, 0:16], kv[2][:, :, 1:RW, 0:16])
                V.tensor_copy(vf[:, :, 1:RW, 48:64], kv[2][:, :, 1:RW, 16:32])
                dve.wait_ge(s_sy, 1)
                for i in range(2):
                    s = V.tensor_copy(kq[:, i, :, 0, :], pw[0:NHD, 128 + 64 * i:192 + 64 * i].rearrange("n (r h) -> n r h", r=2))
                ch.link(V.tensor_copy(vf[:, :, 0, :], pw[0:NHD, 256:384].rearrange("n (r h) -> n r h", r=2)))
                for i in range(2):
                    ch.link(V.tensor_scalar(kq[:, i, 0], kq[:, i, 0], hs[:, i:i + 1], None, ALU.add))
                K, Q = kq[:, 0], kq[:, 1]
                ch.link(V.memset(gg[:, 3 * RW:NUN], 0.0))
                t0, t1 = kvq[:, 0, 0:RW * RH].rearrange("n (w h) -> n w h", w=RW), kvq[:, 1, 0:RW * RH].rearrange("n (w h) -> n w h", w=RW)
                ch.link(V.tensor_tensor(t0, Q[:, 0], K[:, 0], ALU.mult))
                ch.link(V.tensor_tensor(t1, Q[:, 1], K[:, 1], ALU.mult))
                gr = gg[:, 0:RW]
                ch.link(V.tensor_tensor(gr, t0, t1, ALU.add))
                ch.link(V.tensor_tensor(t0, Q[:, 1], K[:, 0], ALU.mult))
                ch.link(V.tensor_tensor(t1, Q[:, 0], K[:, 1], ALU.mult))
                ch.link(V.tensor_tensor(t0, t0, t1, ALU.subtract))
                V.tensor_tensor(gg[:, RW:2 * RW], gr, t0, ALU.subtract)
                V.tensor_tensor(gg[:, 2 * RW:3 * RW], gr, t0, ALU.add).then_inc(s_gg, 1)
                vs, psk = hs[:, 2:3], hs[:, 3:4]
                ch.link(V.tensor_scalar(wt[:, 0], vf[:, 0], vs, None, ALU.add))
                ch.link(V.tensor_tensor(wt[:, 1], pr[:, 1], wt[:, 0], ALU.mult))
                ch.link(V.tensor_tensor(wt[:, 0], pr[:, 0], wt[:, 0], ALU.mult))
                ch.link(V.tensor_tensor(pr[:, 0], pr[:, 0], vf[:, 1], ALU.mult))
                ch.link(V.tensor_tensor(pr[:, 1], pr[:, 1], vf[:, 1], ALU.mult))
                ch.link(V.tensor_tensor(wt[:, 0], wt[:, 0], pr[:, 1], ALU.subtract))
                ch.link(V.tensor_tensor(wt[:, 1], wt[:, 1], pr[:, 0], ALU.add))
                ch.link(V.tensor_scalar(vf[:, :, :, :], vf[:, :, :, :], psk, None, ALU.mult))
                ch.link(V.tensor_tensor(wt, wt, vf[:, :, :, :], ALU.add))
                V.tensor_tensor(vf[:, 0], wt[:, 1], wt[:, 0], ALU.subtract)
                V.tensor_tensor(vf[:, 1], wt[:, 0], wt[:, 1], ALU.add).then_inc(s_wt, 1)
                ch.link(V.tensor_tensor(qkb[:, :], rows[:, 0, :], rows[:, 1, :], ALU.mult))
                ch.link(V.tensor_tensor(vpb[:, :], rows[:, 2, :], rows[:, 3, :], ALU.mult))
                xg = xa[:, :].rearrange("p (h w) -> p h w", w=WW)
                for i in range(4):
                    q = xg[:, 32 * i:32 * i + 32, :]
                    ch.link(V.tensor_tensor(q, q, bc(rw[:, 0, :], 1, 32), ALU.mult))
                    ch.link(V.tensor_tensor(q, q, bc(rw[:, 1, :], 1, 32), ALU.add))
                dve.wait_ge(s_gt, 1)
                s = V.tensor_tensor(gt[:, :, :], f1[0][:, 0:32 * NCH].rearrange("p (k n) -> p k n", k=NCH), bc(cm[:, :], 2, NHD), ALU.mult)
                ch.link(s)

        pt = att.enter_context(nc.sbuf_tensor("pt", [128, NCK, NI], F32))
        npt = att.enter_context(nc.sbuf_tensor("npt", [128, NCK, NI], F32))
        with ExitStack() as p2:
            def sb(name, shape):
                return p2.enter_context(nc.sbuf_tensor(name, shape, F32))

            def pb(name, shape):
                return p2.enter_context(nc.psum_tensor(name, shape, F32))

            xt = sb("xt", [128, KW, 2, KH])
            xr = sb("xr", [128, 2, NUN, RH])
            xrm = sb("xrm", [128, 2, NCH, NI])
            xg = sb("xg", [128, 2, 2, NI])
            z = sb("z", [128, 2, NB, 16, NT])
            gram = sb("gram", [128, NT])
            wg = sb("wg", [128, KW])
            ny = sb("ny", [128, 128])
            sco = sb("sco", [128, NHD, NT])
            ex = sb("ex", [128, NHD, NT])
            mx = sb("mx", [128, NHD])
            am = sb("am", [128, NT])
            ad = sb("ad", [128, NI])
            at = sb("at", [128, NI])
            tp = [pb(f"tp{i}", [128, 512]) for i in range(2)]
            tg = [pb(f"tg{i}", [128, 512]) for i in range(2)]
            pgr = pb("pgr", [128, 512])
            psc = pb("psc", [128, 1024])
            pny = pb("pny", [128, 512])

            s_xt = sem("spectrum_loaded")
            s_wg = sem("gram_weights_loaded")
            s_xn = sem("region_columns_normed")
            s_xh = sem("other_columns_normed")
            s_fac = sem("region_factors_ready")
            s_fac2 = sem("negative_factors_ready")
            s_sum = sem("parts_summed")
            xsum = sb("xsum", [128, KW, KH])
            s_xns = sem("normed_spectrum_stored")
            s_c2 = sem("p2_vector_steps")
            s_t = sem("gram_chunk_transposed")
            s_tc = sem("gram_chunk_copied")
            s_tw = sem("gram_chunk_weighted")
            s_ny = sem("nyquist_chunk_weighted")
            s_gr = sem("gram_done")
            s_r = sem("region_chunk_transposed")
            s_rc = sem("region_chunk_copied")
            s_z = sem("score_products_ready")
            s_zu = sem("score_products_used")
            s_mx = sem("scores_less_maximum")
            s_ex = sem("exponentials_ready")
            s_p = sem("probabilities_ready")
            s_pt = sem("probabilities_transposed")
            s_ptc = sem("probabilities_copied")
            s_a = sem("skip_mixing_ready")
            s_at = sem("skip_mixing_transposed")
            s_atc = sem("skip_mixing_copied")
            s_cb = sem("mixed_offset_ready")
            block = p2.enter_context(nc.Block())
            NZ = 2 * NCH
            BESIDE = [2 if j < KW - NZ else 1 for j in range(NZ)]

            def beside(j):
                first = sum(BESIDE[:j])
                return range(first, first + BESIDE[j])

            @block.sync
            def _(sp):
                sp.dma_start(xt[:, :, :, :].rearrange("p w r h -> p (w r h)"), xs.rearrange("i m k -> i (m k)")).then_inc(s_xt, 16)
                sp.dma_start(wg[:, :], c["wg"]).then_inc(s_wg, 16)
                sp.dma_start(ny[:, :], c["ny"]).then_inc(s_wg, 16)
                sp.wait_ge(s_xn, 1)
                sp.wait_ge(s_xh, 1)
                for r in range(2):
                    sp.dma_start(xns[:, r + 1].rearrange("i (w h) -> i w h", w=KW), xt[:, :, r, :]).then_inc(s_xns, 16)
                sp.wait_ge(s_sum, 1)
                sp.dma_start(xns[:, 0], xsum[:, :, :].rearrange("p w h -> p (w h)")).then_inc(s_xns, 16)
                sp.wait_ge(s_xns, 48)

            @block.gpsimd
            def _(pool):
                pool.wait_ge(s_xn, 1)
                pool.wait_ge(s_xh, 1)
                nc.gpsimd.tensor_tensor(xsum[:, :, :], xt[:, :, 0, :], xt[:, :, 1, :], ALU.add).then_inc(s_sum, 1)

            @block.scalar
            def _(act):
                act.wait_ge(s_xt, 16)
                act.activation(xt[:, RW:KW], xt[:, RW:KW], ACT.Copy, scale=v1("alpha")).then_inc(s_xh, 1)
                act.wait_ge(s_fac, 1)
                act.activation(xr[:, 1, 0:RW], xr[:, 0, 0:RW], ACT.Copy)
                act.activation(xr[:, 1, RW:2 * RW], xr[:, 0, 2 * RW:3 * RW], ACT.Copy, scale=-1.0)
                act.activation(xr[:, 1, 2 * RW:3 * RW], xr[:, 0, RW:2 * RW], ACT.Copy, scale=-1.0).then_inc(s_fac2, 1)

                def region(k):
                    for v in range(2):
                        i = 2 * k + v
                        act.wait_ge(s_r, i + 1)
                        act.activation(xrm[:, v, k, :], tp[v][:, 0:NI], ACT.Copy).then_inc(s_rc, 1)

                def gram_copies(kw):
                    act.wait_ge(s_t, kw + 1)
                    wait(act, s_gr, kw - 1)
                    act.activation(xg[:, kw % 2, 0, :], tg[kw % 2][:, 0:NI], ACT.Copy).then_inc(s_tc, 1)
                    if kw < KW - 1:
                        act.activation(xg[:, kw % 2, 1, :], tg[kw % 2][:, 0:NI], ACT.Copy, scale=wg[:, kw:kw + 1]).then_inc(s_tw, 1)
                    else:
                        act.wait_ge(s_ny, 1)
                        act.activation(xg[:, kw % 2, 1, :], pny[:, 0:NI], ACT.Copy).then_inc(s_tw, 1)
                region(0)
                act.wait_ge(s_wg, 32)
                for j in range(NZ):
                    if j % 2 == 0 and j // 2 + 1 < NCH:
                        region(j // 2 + 1)
                    for kw in beside(j):
                        gram_copies(kw)
                act.wait_ge(s_mx, 1)
                act.activation(ex[:, :, :], sco[:, :, :], ACT.Exp).then_inc(s_ex, 1)
                act.wait_ge(s_ptc, 1)
                act.activation(npt[:, :, :], pt[:, :, :], ACT.Copy, scale=-1.0).then_inc(s_ex, 1)
                act.wait_ge(s_ex, 2)

            @block.tensor
            def _(pe):
                def region(k):
                    for v in range(2):
                        wait(pe, s_rc, 2 * k + v - 1)
                        nc.tensor.transpose(tp[v][:, 0:NI], xr[:, v, 4 * k:4 * k + 4].rearrange("p c h -> p (c h)"), ident[:, :]).then_inc(s_r, 1)

                def gram_transpose(kw):
                    wait(pe, s_tc, kw - 1)
                    wait(pe, s_tw, kw - 1)
                    nc.tensor.transpose(tg[kw % 2][:, 0:NI], xt[:, kw].rearrange("p r h -> p (r h)"), ident[:, :]).then_inc(s_t, 1)

                def gram_step(kw):
                    pe.wait_ge(s_tc, kw + 1)
                    if kw == KW - 1:
                        nc.tensor.matmul(pny[:, 0:NI], ny[:, :], xg[:, kw % 2, 0, :], start=True, stop=True).then_inc(s_ny, 1)
                    pe.wait_ge(s_tw, kw + 1)
                    nc.tensor.matmul(pgr[:, 0:NI], xg[:, kw % 2, 0, :], xg[:, kw % 2, 1, :],
                                     start=(kw == 0), stop=(kw == KW - 1)).then_inc(s_gr, 1)

                def scores(j):
                    k, half = j // 2, j % 2
                    pe.wait_ge(s_rc, 2 * k + 2)
                    pe.wait_ge(s_z, j + 1)
                    for b in range(NB):
                        m = nc.tensor.matmul(psc[32 * b:32 * b + 32, 512 * half:512 * half + 512],
                                             xrm[:, 1, k, 32 * b:32 * b + 32],
                                             z[:, j % 2, b].rearrange("p n s -> p (n s)"), start=(k == 0), stop=(k == NCH - 1))
                    m.then_inc(s_zu, 1)
                pe.wait_ge(s_fac, 1)
                pe.wait_ge(s_fac2, 1)
                region(0)
                pe.wait_ge(s_xn, 1)
                pe.wait_ge(s_xh, 1)
                for j in range(NZ):
                    if j % 2 == 0 and j // 2 + 1 < NCH:
                        region(j // 2 + 1)
                    for kw in beside(j):
                        gram_transpose(kw)
                    scores(j)
                    for kw in beside(j):
                        gram_step(kw)
                pe.wait_ge(s_p, 1)
                for k in range(NCK):
                    m = nc.tensor.transpose(psc[:, 128 * k:128 * k + 128],
                                            ex[:, PB * k:PB * k + PB, :].rearrange("p n s -> p (n s)"), ident[:, :])
                m.then_inc(s_pt, 1)
                pe.wait_ge(s_a, 1)
                nc.tensor.transpose(tp[0][:, 0:NI], ad[:, :], ident[:, :]).then_inc(s_at, 1)
                pe.wait_ge(s_atc, 1)
                nc.tensor.matmul(tp[1][:, 0:1], at[:, :], v1("beta"), start=True, stop=True).then_inc(s_cb, 1)

            @block.vector
            def _(dve):
                ch = Chain(dve, s_c2)
                V = nc.vector
                dve.wait_ge(s_xt, 16)
                ch.link(V.tensor_scalar(xt[:, 0:RW], xt[:, 0:RW], v1("alpha"), None, ALU.mult))
                V.tensor_scalar(xt[:, 0, 0, 0:1], xt[:, 0, 0, 0:1], v1("beta"), None, ALU.add).then_inc(s_xn, 1)
                V.memset(xr[:, :, 3 * RW:NUN], 0.0)
                dve.wait_ge(s_xn, 1)
                re, im = (xt[:, 0:RW, r].rearrange("p w (z h) -> p w z h", z=4)[:, :, 0:4:3] for r in range(2))
                so, io, ro = (xr[:, 0, f * RW:f * RW + RW].rearrange("p w (z h) -> p w z h", z=2) for f in range(3))
                V.tensor_tensor(so, re, im, ALU.add)
                V.tensor_copy(io, im)
                V.tensor_copy(ro, re).then_inc(s_fac, 1)
                for j in range(NZ):
                    k, half = j // 2, j % 2
                    dve.wait_ge(s_rc, 2 * k + 1)
                    wait(dve, s_zu, j - 1)
                    w = gt[:, k, 16 * half:16 * half + 16]
                    xx = xrm[:, 0, k, :].rearrange("p (b s) -> p b s", b=NB)
                    V.tensor_tensor(z[:, j % 2], bc(bc(w, 1, NB), 3, NT), bc(xx, 2, 16), ALU.mult).then_inc(s_z, 1)
                dve.wait_ge(s_gr, KW)
                for b in range(NB):
                    s = V.tensor_copy(gram[32 * b:32 * b + 32, :], pgr[32 * b:32 * b + 32, 32 * b:32 * b + 32])
                ch.link(s)
                ch.link(V.tensor_tensor(sco[:, :, :], bc(qkb[:, :], 2, NT), bc(gram[:, :], 1, NHD), ALU.mult))
                dve.wait_ge(s_zu, NZ)
                ch.link(V.tensor_tensor(sco[:, :, :], sco[:, :, :], psc[:, :].rearrange("p (n s) -> p n s", n=NHD), ALU.add))
                ch.link(V.reduce_max(mx[:, :], sco[:, :, :], axis=AX.X))
                V.tensor_tensor(sco[:, :, :], sco[:, :, :], bc(mx[:, :], 2, NT), ALU.subtract).then_inc(s_mx, 1)
                dve.wait_ge(s_ex, 1)
                ch.link(V.reduce_sum(mx[:, :], ex[:, :, :], axis=AX.X))
                ch.link(V.reciprocal(mx[:, :], mx[:, :]))
                V.tensor_tensor(ex[:, :, :], ex[:, :, :], bc(mx[:, :], 2, NT), ALU.mult).then_inc(s_p, 1)
                dve.wait_ge(s_p, 1)
                ch.link(V.tensor_tensor(sco[:, :, :], ex[:, :, :], bc(vpb[:, :], 2, NT), ALU.mult))
                ch.link(V.reduce_sum(am[:, :], sco[:, :, :].rearrange("p n s -> p s n"), axis=AX.X))
                ch.link(V.memset(ad[:, :], 0.0))
                for b in range(NB):
                    s = V.tensor_copy(ad[32 * b:32 * b + 32, 32 * b:32 * b + 32], am[32 * b:32 * b + 32, :])
                s.then_inc(s_a, 1)
                dve.wait_ge(s_pt, 1)
                V.tensor_copy(pt[:, :, :], psc[:, :].rearrange("p (k i) -> p k i", k=NCK)).then_inc(s_ptc, 1)
                dve.wait_ge(s_at, 1)
                V.tensor_copy(at[:, :], tp[0][:, 0:NI]).then_inc(s_atc, 1)
                dve.wait_ge(s_atc, 1)
                ch.link(V.scalar_tensor_tensor(mt[:, :], at[:, :], v1("alpha"), ident[:, :], ALU.mult, ALU.add))
                dve.wait_ge(s_cb, 1)
                ch.link(V.tensor_copy(v1("cbeta"), tp[1][:, 0:1]))

        with ExitStack() as p3:
            def sb(name, shape):
                return p3.enter_context(nc.sbuf_tensor(name, shape, F32))

            def pb(name, shape):
                return p3.enter_context(nc.psum_tensor(name, shape, F32))

            wb = sb("wb", [128, 2, NCK, 3, MB])
            xb = sb("xb", [128, 2, 3, NB, MB])
            q1 = sb("q1", [128, 2, 3, NB, MB])
            ms = sb("ms", [128, 2, 512])
            sq = sb("sq", [128, 512])
            ssq = sb("ssq", [128, 32])
            acc = [pb(f"acc{i}", [128, 2, MB]) for i in range(2)]
            pm = [pb(f"pm{i}", [128, 512]) for i in range(2)]
            s_blk = sems("block_loaded", 2)
            s_q = sem("value_products_ready")
            s_qu = sem("value_products_used")
            s_ac = sem("block_copied")
            s_mm = sem("images_mixed")
            s_mc = sem("mixed_images_copied")
            s_ms = sems("mixed_images_stored", 2)
            s_sq = sem("squares_summed")
            s_c3 = sem("p3_vector_steps")
            NMX = HH * WW // 512
            MPB = (NMX - 2) // (NBLK - 1)
            block = p3.enter_context(nc.Block())

            def blocks(eng, body):
                body(0, 0, 0)
                body(1, 1, 0)
                with eng.Fori(1, NBLK // 2) as i:
                    body(2 * i, 0, i)
                    body(2 * i + 1, 1, i)
                body(NBLK - 1, 0, NBLK // 2)

            @block.sync
            def _(sp):
                def load(blk, u, turn):
                    wait(sp, s_qu, NCK * (blk - 1))
                    for j in range(PB):
                        n = NCK * 3 * MB
                        sp.dma_start(wb[32 * j:32 * j + 32, u].rearrange("p k r m -> p (k r m)"),
                                     bass.AP(wv.tensor, (blk + j * NBLK) * n, [[0, 32], [1, n]])).then_inc(s_blk[u], 16)
                        for r in range(3):
                            sp.dma_start(xb[32 * j:32 * j + 32, u, r],
                                         bass.AP(xns.tensor, r * M2 + blk * MB, [[3 * M2, NT], [NT * 3 * M2, NB], [1, MB]])).then_inc(s_blk[u], 16)
                blocks(sp, load)

            @block.gpsimd
            def _(pool):
                mo = mixd.rearrange("i h w -> i (h w)")
                with pool.Fori(0, NMX // 2) as i:
                    for u in range(2):
                        t = 2 * i + u
                        pool.wait_ge(s_mc, t + 1)
                        pool.dma_start(mo[:, bass.ds(t * 512, 512)], ms[:, u]).then_inc(s_ms[u], 16)
                for q in s_ms:
                    pool.wait_ge(q, 16 * NMX // 2)

            def mix_blocks(eng, mixed, block_copy):
                mixed(0, 0, 0)
                mixed(1, 1, 0)
                block_copy(0, 0)
                with eng.Fori(0, NBLK // 2) as i:
                    for v in range(2):
                        for j in range(MPB):
                            m = MPB * v + j
                            mixed(2 * MPB * i + 2 + m, m % 2, MPB * i + 1 + m // 2)
                        block_copy(2 * i + 1 + v, 1 - v)

            @block.scalar
            def _(act):
                def mixed(t, u, turn):
                    act.wait_ge(s_mm, t + 1)
                    wait(act, s_ms[u], 16 * turn)
                    act.activation(ms[:, u], pm[u][:, :], ACT.Identity, bias=v1("cbeta")).then_inc(s_mc, 1)
                    act.wait_ge(s_mc, t + 1)
                    wait(act, s_sq, t)
                    act.activation(sq[:, :], ms[:, u], ACT.Square,
                                   accum_out=ssq[:, bass.ds(t, 1)]).then_inc(s_sq, 1)

                def block_copy(blk, u):
                    act.wait_ge(s_qu, NCK * (blk + 1))
                    act.activation(pa[:, bass.ds(blk * CB, CB)].rearrange("p w r h -> p r w h"),
                                   acc[u][:, :, :].rearrange("p r (w h) -> p r w h", w=CB), ACT.Copy).then_inc(s_ac, 1)
                mix_blocks(act, mixed, block_copy)
                act.wait_ge(s_ac, NBLK)

            @block.tensor
            def _(pe):
                def mix(t, u, turn):
                    wait(pe, s_mc, t - 1)
                    nc.tensor.matmul(pm[u][:, :], mt[:, :], xa[:, bass.ds(t * 512, 512)], start=True, stop=True).then_inc(s_mm, 1)

                def contract(blk, u):
                    wait(pe, s_ac, blk - 1)
                    for k in range(NCK):
                        pe.wait_ge(s_q, NCK * blk + k + 1)
                        for p in range(3):
                            for b in range(NB):
                                rows = slice(32 * b, 32 * b + 32)
                                P, N = pt[:, k, rows], npt[:, k, rows]
                                if p == 0:
                                    m = nc.tensor.matmul(acc[u][rows, :, :], P, bc(q1[:, k % 2, 0, b], 1, 2), start=(k == 0), stop=False)
                                elif p == 1:
                                    m = nc.tensor.matmul(acc[u][rows, 1, :], P, q1[:, k % 2, 1, b], start=False, stop=False)
                                else:
                                    m = nc.tensor.matmul(acc[u][rows, 0, :], N, q1[:, k % 2, 2, b], start=False, stop=(k == NCK - 1))
                        m.then_inc(s_qu, 1)
                mix_blocks(pe, mix, contract)

            @block.vector
            def _(dve):
                V = nc.vector

                def products(blk, u, turn):
                    dve.wait_ge(s_blk[u], 16 * 4 * PB * (turn + 1))
                    for k in range(NCK):
                        wait(dve, s_qu, NCK * blk + k - 1)
                        V.tensor_tensor(q1[:, k % 2], bc(wb[:, u, k], 2, NB), xb[:, u], ALU.mult).then_inc(s_q, 1)
                blocks(dve, products)
                dve.wait_ge(s_sq, NMX)
                ch = Chain(dve, s_c3)
                ch.link(V.reduce_sum(v1("mixsq"), ssq[:, :], axis=AX.X))
                ch.link(V.tensor_scalar(v1("mixsq"), v1("mixsq"), 1.0 / (HH * WW), None, ALU.mult))

        att.close()
        yall = keep("yall", [128, NI, WW])
        spec = ExitStack()
        tt = spec.enter_context(nc.sbuf_tensor("tt", [128, 2 * KW, NI], F32))
        fac = ExitStack()
        c1b, c2b = (fac.enter_context(nc.sbuf_tensor(n, [128, NI], F32)) for n in ("c1b", "c2b"))
        DC = (slice(None), 0, 0, slice(0, 1))

        def complex_product(ch, V, dst, w, src, t):
            wr, wi = (w[:, :, :, r].rearrange("p h w -> p w h") for r in (0, 1))
            V.tensor_tensor(dst[:, :, 0], wr, src[:, :, 0], ALU.mult)
            V.tensor_tensor(dst[:, :, 1], wr, src[:, :, 1], ALU.mult)
            ch.link(V.tensor_tensor(t, wi, src[:, :, 1], ALU.mult))
            ch.link(V.tensor_tensor(dst[:, :, 0], dst[:, :, 0], t, ALU.subtract))
            ch.link(V.tensor_tensor(t, wi, src[:, :, 0], ALU.mult))
            ch.link(V.tensor_tensor(dst[:, :, 1], dst[:, :, 1], t, ALU.add))

        def energy(ch, act, src, col0, t, en):
            for r in range(2):
                ch.link(act.activation(t[:, 0:(KW - 1) * KH].rearrange("p (w h) -> p w h", w=KW - 1), src[:, 1:KW, r, :], ACT.Square, accum_out=en[:, r:r + 1]))
            ch.link(act.activation(t[:, 0:2 * KH].rearrange("p (r h) -> p r h", r=2), col0, ACT.Square, accum_out=en[:, 2:3]))
            ch.link(act.activation(t[:, 0:2], col0[:, :, 32], ACT.Square, accum_out=en[:, 3:4]))

        def energy_sum(ch, V, out, en):
            ch.link(V.tensor_tensor(out, en[:, 0:1], en[:, 1:2], ALU.add))
            ch.link(V.tensor_scalar(out, out, 2.0, None, ALU.mult))
            ch.link(V.tensor_tensor(out, out, en[:, 2:3], ALU.add))
            ch.link(V.tensor_tensor(out, out, en[:, 3:4], ALU.add))

        def mulv(ch, V, out, x_, y_):
            ch.link(V.tensor_tensor(out, x_, y_, ALU.mult))

        def to_rows_pe(pe, zp, ps, s_zp, s_tr, s_trc):
            pe.wait_ge(s_zp, 1)
            for q in range(0, 2 * KW, 4):
                if q // 4 >= 2:
                    pe.wait_ge(s_trc, q // 4 - 1)
                for j in range(q, min(q + 4, 2 * KW)):
                    v, kw = j // KW, j % KW
                    m = nc.tensor.transpose(ps[(q // 4) % 2][:, 128 * (j - q):128 * (j - q) + 128], zp[:, kw, v:v + 2].rearrange("p r h -> p (r h)"), ident[:, :])
                m.then_inc(s_tr, 1)

        def to_rows_copy(act, ps, s_tr, s_trc):
            for q in range(0, 2 * KW, 4):
                n = min(4, 2 * KW - q)
                act.wait_ge(s_tr, q // 4 + 1)
                act.activation(tt[:, q:q + n, :], ps[(q // 4) % 2][:, 0:128 * n].rearrange("p (j i) -> p j i", j=n), ACT.Copy).then_inc(s_trc, 1)
            act.wait_ge(s_trc, (2 * KW + 3) // 4)

        def symmetrise(pe, src, ps, cs, s_a, s_b, s_c, n):
            nc.tensor.transpose(ps[:, 0:128], src[:, 0, 0:2].rearrange("p r h -> p (r h)"), ident[:, :]).then_inc(s_a, 1)
            pe.wait_ge(s_b, n)
            nc.tensor.matmul(ps[:, 128:256], cs[:, :], sym[:, :], start=True, stop=True).then_inc(s_c, 1)


        with ExitStack() as p4:
            def sb(name, shape):
                return p4.enter_context(nc.sbuf_tensor(name, shape, F32))

            def pb(name, shape):
                return p4.enter_context(nc.psum_tensor(name, shape, F32))

            zp = sb("zp4", [128, KW, 3, KH])
            fs = sb("fs4", [128, KW, 2, KH])
            t4 = sb("t4", [128, M2])
            ta = sb("t4a", [128, M2])
            cs = sb("cs4", [128, 128])
            s0 = sb("s04", [128, 2, KH])
            en = sb("en4", [128, 12])
            dg = sb("dg4", [128, NI])
            flat = tt[:, :, :].rearrange("p j i -> p (j i)")
            xt4 = flat[:, 0:2 * M2]
            mraw = flat[:, 2 * M2:4 * M2].rearrange("p (h w r) -> p h w r", h=KH, w=KW)
            mxs = sb("mx4", [128, KW, 2, KH])
            pmx = [pb(f"pmx{i}", [128, 512]) for i in range(2)]
            psy = pb("psy4", [128, 512])
            ps = [pb(f"ptr4_{i}", [128, 512]) for i in range(2)]
            pbc = pb("pbc4", [128, 512])
            s_ld = sem("p4_spectra_loaded")
            s_mr = sem("m0_weights_loaded")
            s_mm4 = sem("mixed_spectrum_done")
            s_mc4 = sem("mixed_spectrum_copied")
            s_y0 = sem("p4_products_ready")
            s_sa, s_sbb, s_sc = sem("p4_column0_transposed"), sem("p4_column0_copied"), sem("p4_column0_symmetrised")
            s_v4, s_a4 = sem("p4_vector_steps"), sem("p4_energy_steps")
            s_f = sem("p4_spectrum_for_energy")
            s_zp, s_tr, s_trc = sem("p4_spectrum_ready"), sem("p4_rows_transposed"), sem("p4_rows_copied")
            s_dg, s_bc = sem("p4_factors_ready"), sem("p4_factors_spread")
            root = Root(sem("p4_root_asked"), sem("p4_root_given"))
            block = p4.enter_context(nc.Block())
            NC4 = (2 * M2 + 511) // 512

            @block.sync
            def _(sp):
                sp.dma_start(xt4, xs.rearrange("i m k -> i (m k)")).then_inc(s_ld, 16)
                src = a["L0_conv_m0cw"]
                sp.dma_start(mraw.rearrange("p h w r -> p (h w r)"), bass.AP(src.tensor, 0, [[0, 128], [1, 2 * M2]])).then_inc(s_mr, 16)

            @block.tensor
            def _(pe):
                pe.wait_ge(s_ld, 16)
                for j in range(NC4):
                    n = min(512, 2 * M2 - 512 * j)
                    if j >= 2:
                        pe.wait_ge(s_mc4, j - 1)
                    nc.tensor.matmul(pmx[j % 2][:, 0:n], mt[:, :], xt4[:, 512 * j:512 * j + n], start=True, stop=True).then_inc(s_mm4, 1)
                symmetrise(pe, pa, psy, cs, s_sa, s_sbb, s_sc, 1)
                pe.wait_ge(s_y0, 1)
                symmetrise(pe, zp, psy, cs, s_sa, s_sbb, s_sc, 2)
                to_rows_pe(pe, zp, ps, s_zp, s_tr, s_trc)
                for i in range(2):
                    pe.wait_ge(s_dg, i + 1)
                    nc.tensor.matmul(pbc[:, 128 * i:128 * i + 128], ones[:, :], dg[:, :], start=True, stop=True).then_inc(s_bc, 1)

            @block.scalar
            def _(act):
                ch = Chain(act, s_a4)
                act.wait_ge(s_f, 1)
                energy(ch, nc.scalar, mxs, mxs[:, 0], ta, en[:, 0:4])
                energy(ch, nc.scalar, fs, fs[:, 0], ta, en[:, 4:8])
                root.serve(act, nc.scalar, v1("r"))
                root.serve(act, nc.scalar, v1("r"))
                act.wait_ge(s_f, 2)
                energy(ch, nc.scalar, zp, s0[:, :, :], ta, en[:, 8:12])
                root.serve(act, nc.scalar, v1("r"))
                act.wait_ge(s_zp, 1)
                to_rows_copy(act, ps, s_tr, s_trc)

            @block.vector
            def _(dve):
                ch = Chain(dve, s_v4)
                V = nc.vector
                mflat = mxs[:, :, :, :].rearrange("p w r h -> p (w r h)")
                for j in range(NC4):
                    n = min(512, 2 * M2 - 512 * j)
                    dve.wait_ge(s_mm4, j + 1)
                    V.tensor_copy(mflat[:, 512 * j:512 * j + n], pmx[j % 2][:, 0:n]).then_inc(s_mc4, 1)
                dve.wait_ge(s_mc4, NC4)
                ch.link(V.tensor_scalar(mxs[DC], mxs[DC], v1("cbeta"), None, ALU.add))
                dve.wait_ge(s_sa, 1)
                V.tensor_copy(cs[:, :], psy[:, 0:128]).then_inc(s_sbb, 1)
                ch.link(V.tensor_tensor(fs[:, 1:KW], mxs[:, 1:KW], pa[:, 1:KW], ALU.add))
                dve.wait_ge(s_sc, 1)
                V.tensor_tensor(fs[:, 0], mxs[:, 0], psy[:, 128:256].rearrange("p (r h) -> p r h", r=2), ALU.add).then_inc(s_f, 1)
                dve.wait_ge(s_a4, 8)
                e1, e2 = v1("e1"), v1("e2")
                energy_sum(ch, V, e1, en[:, 0:4])
                energy_sum(ch, V, e2, en[:, 4:8])
                var, r, t = v1("var"), v1("r"), v1("t")
                ch.link(V.tensor_tensor(var, e2, e1, ALU.subtract))
                ch.link(V.tensor_tensor(var, var, v1("mixsq"), ALU.add))
                ch.link(V.tensor_copy(v1("mu"), fs[DC]))
                mulv(ch, V, t, v1("mu"), v1("mu"))
                ch.link(V.tensor_tensor(var, var, t, ALU.subtract))
                root.rsqrt(dve, ch, V, r, var)
                mulv(ch, V, v1("g"), r, scalar["attn_w"])
                mulv(ch, V, t, v1("g"), v1("g"))
                mulv(ch, V, t, t, var)
                root.rsqrt(dve, ch, V, r, t)
                mulv(ch, V, v1("kappa"), r, scalar["norm2_w"])
                mulv(ch, V, v1("kg"), v1("kappa"), v1("g"))
                ch.link(V.tensor_scalar(fs[:, :, :, :], fs[:, :, :, :], v1("kg"), None, ALU.mult))
                ch.link(V.tensor_copy(fs[DC], scalar["norm2_b"]))
                dve.wait_ge(s_mr, 16)
                complex_product(ch, V, zp[:, :, 0:2], mraw, fs, t4[:, :].rearrange("p (w h) -> p w h", w=KW))
                ch.link(V.memset(zp[:, 0, 0:2, 0:1], 0.0))
                V.tensor_scalar(t4[:, 0:1], zp[DC], 1.0, None, ALU.mult).then_inc(s_y0, 1)
                dve.wait_ge(s_sa, 2)
                V.tensor_copy(cs[:, :], psy[:, 0:128]).then_inc(s_sbb, 1)
                dve.wait_ge(s_sc, 2)
                V.tensor_copy(s0[:, :, :], psy[:, 128:256].rearrange("p (r h) -> p r h", r=2)).then_inc(s_f, 1)
                dve.wait_ge(s_a4, 12)
                energy_sum(ch, V, e1, en[:, 8:12])
                root.rsqrt(dve, ch, V, r, e1)
                mulv(ch, V, v1("skg"), v1("kg"), scalar["m0sw"])
                ch.link(V.tensor_scalar(zp[:, :, 0:2], zp[:, :, 0:2], r, None, ALU.mult))
                ch.link(V.scalar_tensor_tensor(zp[:, :, 0:2], pa[:, :, :, :], v1("skg"), zp[:, :, 0:2], ALU.mult, ALU.add))
                mulv(ch, V, t, v1("skg"), v1("mu"))
                ch.link(V.tensor_tensor(zp[DC], zp[DC], t, ALU.subtract))
                mulv(ch, V, t, scalar["m0sw"], scalar["norm2_b"])
                ch.link(V.tensor_tensor(zp[DC], zp[DC], t, ALU.add))
                V.tensor_scalar(zp[:, :, 2], zp[:, :, 0], -1.0, None, ALU.mult).then_inc(s_zp, 1)
                for i, (n, dst) in enumerate((("skg", c1b), ("g", c2b))):
                    V.tensor_scalar(dg[:, :], ident[:, :], v1(n), None, ALU.mult).then_inc(s_dg, 1)
                    dve.wait_ge(s_bc, i + 1)
                    ch.link(V.tensor_copy(dst[:, :], pbc[:, 128 * i:128 * i + 128]))

        recycle()

        def lagged(b, u, k, body, *args):
            if k > u:
                if not (isinstance(b, int) and b == 0):
                    body(b - 1, u - k + GPB, *args)
            else:
                body(b, u - k, *args)

        def inverse_h(pe, b, u, ts, pz, s_ts, s_s1, s_z):
            g = GPB * b + u
            pe.wait_ge(s_ts, g + 1)
            wait(pe, s_z, g)
            for i in range(GI):
                m = nc.tensor.matmul(pz[:, 128 * i:128 * i + 128], ts[:, u % 2, :, i], eh[:, :], start=True, stop=True)
            m.then_inc(s_s1, 1)

        def inverse_w(pe, b, u, zs, pi, s_z, s_s2, s_add):
            g = GPB * b + u
            pe.wait_ge(s_z, g + 1)
            wait(pe, s_add, g)
            for i in range(GI):
                m = nc.tensor.matmul(pi[:, 128 * i:128 * i + 128], zs[:, u % 2, i, :], cw[:, :], start=True, stop=True)
            m.then_inc(s_s2, 1)

        with ExitStack() as p5:
            def sb(name, shape):
                return p5.enter_context(nc.sbuf_tensor(name, shape, F32))

            def pb(name, shape):
                return p5.enter_context(nc.psum_tensor(name, shape, F32))

            mg = sb("mg5", [128, GPB, GI, WW])
            ts = sb("ts5", [128, 2, 2 * KW, GI])
            zs = sb("zs5", [2 * KW, 2, GI, 128])
            pre = sb("pre5", [128, 2, GI, WW])
            yst = sb("yst5", [128, 2, GI, WW])
            sq = sb("sq5", [128, 2, GI, WW])
            yf = sb("yf5", [128, 2, 2, GI, KH])
            yo = sb("yo5", [2 * KW, GPB, GI, KH])
            ysq = sb("ysq5", [128, NI])
            pz = pb("pz5", [2 * KW, GI * 128])
            pi = pb("pi5", [128, GI * 128])
            pf = pb("pf5", [128, GI * 128])
            pw = pb("pw5", [2 * KW, GI * KH])
            pq = pb("pq5", [128, 512])
            s_mg = sems("p5_mixed_loaded", GPB)
            s_ts, s_s1, s_z, s_s2 = sem("p5_spectra_staged"), sem("p5_rows_done"), sem("p5_rows_copied_back"), sem("p5_pixels_done")
            s_m5 = sem("p5_mixed_scaled")
            s_add, s_y, s_sqd, s_rd = sem("p5_preactivation_ready"), sem("hidden_ready"), sem("hidden_squared"), sem("hidden_squares_summed")
            s_yd = sems("hidden_kept", 2)
            s_f1, s_e1, s_f2, s_e2, s_yo = sem("p5_h_transform_done"), sem("p5_h_transform_copied"), sem("p5_w_transform_done"), sem("p5_w_transform_copied"), sems("hidden_spectrum_stored", GPB)
            s_q5, s_v5 = sem("hidden_energy_done"), sem("p5_vector_steps")
            block = p5.enter_context(nc.Block())
            mixr = mixd.rearrange("i h w -> h i w")

            @block.sync
            def _(sp):
                def load(b):
                    for u in range(GPB):
                        g = GPB * b + u
                        wait(sp, s_m5, g + 1 - GPB)
                        sp.dma_start(mg[:, u], mixr[:, bass.ds(g * GI, GI), :]).then_inc(s_mg[u], 16)
                per_batch(sp, load)

            @block.gpsimd
            def _(pool):
                def stage(b, u):
                    g = GPB * b + u
                    wait(pool, s_s1, g - 1)
                    nc.gpsimd.tensor_copy(ts[:, u % 2], tt[:, :, bass.ds(g * GI, GI)]).then_inc(s_ts, 1)

                def keep_hidden(b, u):
                    g = GPB * b + u
                    pool.wait_ge(s_y, g + 1)
                    pool.dma_start(yall[:, bass.ds(g * GI, GI), :], yst[:, u % 2]).then_inc(s_yd[u % 2], 16)

                def store(b, u):
                    g = GPB * b + u
                    pool.wait_ge(s_e2, g + 1)
                    pool.dma_start(ys[bass.ds(g * GI, GI)].rearrange("i m k -> m i k"), yo[:, u]).then_inc(s_yo[u], 16)

                def body(b):
                    for u in range(GPB):
                        lagged(b, u, 0, stage)
                        lagged(b, u, 1, keep_hidden)
                        lagged(b, u, 2, store)
                per_batch(pool, body)
                keep_hidden(NB - 1, GPB - 1)
                store(NB - 1, GPB - 2)
                store(NB - 1, GPB - 1)
                for q in s_yo:
                    pool.wait_ge(q, 16 * NGRP // GPB)
                for q in s_yd:
                    pool.wait_ge(q, 16 * NGRP // 2)

            @block.tensor
            def _(pe):
                def forward_h(b, u):
                    g = GPB * b + u
                    pe.wait_ge(s_y, g + 1)
                    wait(pe, s_e1, g)
                    for i in range(GI):
                        m = nc.tensor.matmul(pf[:, 128 * i:128 * i + 128], yst[:, u % 2, i, :], fh[:, :], start=True, stop=True)
                    m.then_inc(s_f1, 1)

                def forward_w(b, u):
                    g = GPB * b + u
                    pe.wait_ge(s_e1, g + 1)
                    wait(pe, s_e2, g)
                    for r, f in enumerate((fw1, fw2)):
                        m = nc.tensor.matmul(pw[:, :], f[:, :], yf[:, u % 2, r].rearrange("w i k -> w (i k)"), start=(r == 0), stop=(r == 1))
                    m.then_inc(s_f2, 1)

                def body(b):
                    for u in range(GPB):
                        lagged(b, u, 0, lambda c_, v: inverse_h(pe, c_, v, ts, pz, s_ts, s_s1, s_z))
                        lagged(b, u, 1, forward_h)
                        lagged(b, u, 0, lambda c_, v: inverse_w(pe, c_, v, zs, pi, s_z, s_s2, s_add))
                        lagged(b, u, 1, forward_w)
                per_batch(pe, body)
                forward_h(NB - 1, GPB - 1)
                forward_w(NB - 1, GPB - 1)
                pe.wait_ge(s_rd, NGRP)
                nc.tensor.matmul(pq[:, 0:1], ysq[:, :], ones[:, 0:1], start=True, stop=True).then_inc(s_q5, 1)

            @block.scalar
            def _(act):
                def rows_back(b, u):
                    g = GPB * b + u
                    act.wait_ge(s_s1, g + 1)
                    wait(act, s_s2, g - 1)
                    act.activation(zs[:, u % 2], pz[:, :].rearrange("m (i h) -> m i h", i=GI), ACT.Copy).then_inc(s_z, 1)

                def forward_copy(b, u):
                    g = GPB * b + u
                    act.wait_ge(s_f1, g + 1)
                    wait(act, s_f2, g - 1)
                    act.activation(yf[:, u % 2], pf[:, :].rearrange("w (i r k) -> w r i k", i=GI, r=2), ACT.Copy).then_inc(s_e1, 1)

                def gelu(b, u):
                    g = GPB * b + u
                    act.wait_ge(s_add, g + 1)
                    wait(act, s_f1, g - 1)
                    wait(act, s_yd[u % 2], 16 * nth(b, u))
                    act.activation(yst[:, u % 2], pre[:, u % 2], ACT.Gelu).then_inc(s_y, 1)
                    act.wait_ge(s_y, g + 1)
                    wait(act, s_rd, g - 1)
                    act.activation(sq[:, u % 2], yst[:, u % 2], ACT.Square).then_inc(s_sqd, 1)

                def body(b):
                    for u in range(GPB):
                        lagged(b, u, 0, rows_back)
                        lagged(b, u, 1, forward_copy)
                        lagged(b, u, 0, gelu)
                per_batch(act, body)
                forward_copy(NB - 1, GPB - 1)

            @block.vector
            def _(dve):
                V = nc.vector

                def scale(b, u):
                    g = GPB * b + u
                    dve.wait_ge(s_mg[u], 16 * (b + 1))
                    wait(dve, s_y, g - 1)
                    V.tensor_tensor(pre[:, u % 2], mg[:, u], bc(c1b[:, bass.ds(g * GI, GI)], 2, WW), ALU.mult).then_inc(s_m5, 1)

                def add(b, u):
                    g = GPB * b + u
                    dve.wait_ge(s_s2, g + 1)
                    dve.wait_ge(s_m5, g + 1)
                    V.tensor_tensor(pre[:, u % 2], pre[:, u % 2], pi[:, :].rearrange("h (i w) -> h i w", i=GI), ALU.add).then_inc(s_add, 1)

                def sum_squares(b, u):
                    g = GPB * b + u
                    dve.wait_ge(s_sqd, g + 1)
                    V.reduce_sum(ysq[:, bass.ds(g * GI, GI)], sq[:, u % 2], axis=AX.X).then_inc(s_rd, 1)

                def copy_out(b, u):
                    g = GPB * b + u
                    dve.wait_ge(s_f2, g + 1)
                    wait(dve, s_yo[u], 16 * b)
                    V.tensor_copy(yo[:, u], pw[:, :].rearrange("m (i k) -> m i k", i=GI)).then_inc(s_e2, 1)

                def body(b):
                    for u in range(GPB):
                        lagged(b, u, 0, scale)
                        lagged(b, u, 1, sum_squares)
                        lagged(b, u, 0, add)
                        lagged(b, u, 1, copy_out)
                per_batch(dve, body)
                sum_squares(NB - 1, GPB - 1)
                copy_out(NB - 1, GPB - 1)
                dve.wait_ge(s_q5, 1)
                ch = Chain(dve, s_v5)
                ch.link(V.tensor_scalar(v1("ysq"), pq[:, 0:1], 1.0 / (HH * WW), None, ALU.mult))

        with ExitStack() as p6:
            def sb(name, shape):
                return p6.enter_context(nc.sbuf_tensor(name, shape, F32))

            def pb(name, shape):
                return p6.enter_context(nc.psum_tensor(name, shape, F32))

            zp = sb("zp6", [128, KW, 3, KH])
            t6 = sb("t6", [128, M2])
            ta = sb("t6a", [128, M2])
            cs = sb("cs6", [128, 128])
            s0 = sb("s06", [128, 2, KH])
            en = sb("en6", [128, 4])
            cr = sb("cr6", [128, 4])
            dg = sb("dg6", [128, NI])
            flat = tt[:, :, :].rearrange("p j i -> p (j i)")
            yt = flat[:, 0:2 * M2].rearrange("p (w z h) -> p w z h", z=2, w=KW)
            mraw = flat[:, 2 * M2:4 * M2].rearrange("p (h w r) -> p h w r", h=KH, w=KW)
            psy = pb("psy6", [128, 512])
            ps = [pb(f"ptr6_{i}", [128, 512]) for i in range(2)]
            pbc = pb("pbc6", [128, 512])
            s_ld = sem("p6_loaded")
            s_y1 = sem("p6_products_ready")
            s_sa, s_sbb, s_sc = sem("p6_column0_transposed"), sem("p6_column0_copied"), sem("p6_column0_symmetrised")
            s_v6, s_a6 = sem("p6_vector_steps"), sem("p6_energy_steps")
            s_f = sem("p6_spectrum_for_energy")
            s_zp, s_tr, s_trc = sem("p6_spectrum_ready"), sem("p6_rows_transposed"), sem("p6_rows_copied")
            s_dg, s_bc = sem("p6_factors_ready"), sem("p6_factors_spread")
            root = Root(sem("p6_root_asked"), sem("p6_root_given"))
            block = p6.enter_context(nc.Block())

            @block.sync
            def _(sp):
                sp.dma_start(flat[:, 0:2 * M2], ys.rearrange("i m k -> i (m k)")).then_inc(s_ld, 16)
                src = a["L0_conv_m1cw"]
                sp.dma_start(mraw.rearrange("p h w r -> p (h w r)"), bass.AP(src.tensor, 0, [[0, 128], [1, 2 * M2]])).then_inc(s_ld, 16)

            @block.tensor
            def _(pe):
                pe.wait_ge(s_y1, 1)
                symmetrise(pe, zp, psy, cs, s_sa, s_sbb, s_sc, 1)
                to_rows_pe(pe, zp, ps, s_zp, s_tr, s_trc)
                pe.wait_ge(s_dg, 1)
                nc.tensor.matmul(pbc[:, 0:128], ones[:, :], dg[:, :], start=True, stop=True).then_inc(s_bc, 1)

            @block.scalar
            def _(act):
                ch = Chain(act, s_a6)
                act.wait_ge(s_f, 1)
                energy(ch, nc.scalar, zp, s0[:, :, :], ta, en[:, 0:4])
                root.serve(act, nc.scalar, v1("r"))
                root.serve(act, nc.scalar, v1("t"))
                act.wait_ge(s_zp, 1)
                to_rows_copy(act, ps, s_tr, s_trc)

            @block.vector
            def _(dve):
                ch = Chain(dve, s_v6)
                V = nc.vector
                r, t, var = v1("r"), v1("t"), v1("var")
                dve.wait_ge(s_ld, 32)
                tv = t6[:, :].rearrange("p (w h) -> p w h", w=KW)
                complex_product(ch, V, zp[:, :, 0:2], mraw, yt, tv)
                ch.link(V.memset(zp[:, 0, 0:2, 0:1], 0.0))
                V.tensor_scalar(t6[:, 0:1], zp[DC], 1.0, None, ALU.mult).then_inc(s_y1, 1)
                dve.wait_ge(s_sa, 1)
                V.tensor_copy(cs[:, :], psy[:, 0:128]).then_inc(s_sbb, 1)
                dve.wait_ge(s_sc, 1)
                V.tensor_copy(s0[:, :, :], psy[:, 128:256].rearrange("p (r h) -> p r h", r=2)).then_inc(s_f, 1)
                for q in range(2):
                    ch.link(V.tensor_tensor(tv, zp[:, :, q], yt[:, :, q], ALU.mult))
                    ch.link(V.reduce_sum(cr[:, 2 * q:2 * q + 1], t6[:, KH:M2], axis=AX.X))
                    ch.link(V.reduce_sum(cr[:, 2 * q + 1:2 * q + 2], t6[:, 0:KH], axis=AX.X))
                cross = v1("cross")
                ch.link(V.tensor_tensor(cross, cr[:, 0:1], cr[:, 2:3], ALU.add))
                ch.link(V.tensor_scalar(cross, cross, 2.0, None, ALU.mult))
                ch.link(V.tensor_tensor(cross, cross, cr[:, 1:2], ALU.add))
                ch.link(V.tensor_tensor(cross, cross, cr[:, 3:4], ALU.add))
                dve.wait_ge(s_a6, 4)
                e1, w1, yb_ = v1("e1"), scalar["m1sw"], v1("ybar")
                energy_sum(ch, V, e1, en[:, 0:4])
                root.rsqrt(dve, ch, V, r, e1)
                mulv(ch, V, var, r, e1)
                mulv(ch, V, t, w1, cross)
                ch.link(V.tensor_scalar(t, t, 2.0, None, ALU.mult))
                ch.link(V.tensor_tensor(var, var, t, ALU.add))
                mulv(ch, V, var, var, r)
                ch.link(V.tensor_copy(yb_, yt[DC]))
                mulv(ch, V, t, yb_, yb_)
                ch.link(V.tensor_tensor(t, v1("ysq"), t, ALU.subtract))
                mulv(ch, V, t, t, w1)
                mulv(ch, V, t, t, w1)
                ch.link(V.tensor_tensor(var, var, t, ALU.add))
                root.rsqrt(dve, ch, V, t, var)
                gm = v1("gm")
                mulv(ch, V, gm, t, scalar["mon_w"])
                mulv(ch, V, r, r, gm)
                ch.link(V.tensor_scalar(zp[:, :, 0:2], zp[:, :, 0:2], r, None, ALU.mult))
                ch.link(V.scalar_tensor_tensor(zp[:, :, 0:2], pa[:, :, :, :], v1("g"), zp[:, :, 0:2], ALU.mult, ALU.add))
                c2 = v1("c2")
                mulv(ch, V, c2, gm, w1)
                mulv(ch, V, t, c2, yb_)
                ch.link(V.tensor_tensor(zp[DC], zp[DC], t, ALU.subtract))
                mulv(ch, V, t, v1("g"), v1("mu"))
                ch.link(V.tensor_tensor(zp[DC], zp[DC], t, ALU.subtract))
                ch.link(V.tensor_tensor(zp[DC], zp[DC], scalar["mon_b"], ALU.add))
                ch.link(V.tensor_tensor(zp[DC], zp[DC], scalar["attn_b"], ALU.add))
                V.tensor_scalar(zp[:, :, 2], zp[:, :, 0], -1.0, None, ALU.mult).then_inc(s_zp, 1)
                V.tensor_scalar(dg[:, :], ident[:, :], c2, None, ALU.mult).then_inc(s_dg, 1)
                dve.wait_ge(s_bc, 1)
                ch.link(V.tensor_copy(c1b[:, :], pbc[:, 0:128]))

        fwd = ExitStack()
        y1 = fwd.enter_context(nc.sbuf_tensor("y1", [128, NI, 130], F32))
        en8 = fwd.enter_context(nc.sbuf_tensor("en8", [128, 2, NGRP], F32))
        spare = pa[:, :, :, :].rearrange("p w r h -> p (w r h)")[:, 0:4 * GI * WW]
        with ExitStack() as p7:
            def sb(name, shape):
                return p7.enter_context(nc.sbuf_tensor(name, shape, F32))

            def pb(name, shape):
                return p7.enter_context(nc.psum_tensor(name, shape, F32))

            mg, xn = (spare[:, v * 2 * GI * WW:(v + 1) * 2 * GI * WW].rearrange("p (u i w) -> p u i w", u=2, i=GI) for v in range(2))
            xg = sb("xg7", [128, 2, GI, WW])
            ts = sb("ts7", [128, 2, 2 * KW, GI])
            zs = sb("zs7", [2 * KW, 2, GI, 128])
            qh = sb("qh", [128, 128])
            pz = pb("pz7", [2 * KW, GI * 128])
            pi = pb("pi7", [128, GI * 128])
            pf = pb("pf7", [128, GI * 128])
            s_qh = sem("p7_matrix_loaded")
            s_mg = sems("p7_images_loaded", 2)
            s_ts, s_s1, s_z, s_s2 = sem("p7_spectra_staged"), sem("p7_rows_done"), sem("p7_rows_copied_back"), sem("p7_pixels_done")
            s_m7, s_p7 = sem("p7_mixed_scaled"), sem("p7_input_added")
            s_h7, s_q7 = sem("p7_hidden_scaled"), sem("p7_parts_added")
            s_add, s_k = sem("layer0_output_ready"), sems("layer0_output_kept", 2)
            s_f1, s_e1, s_sq7 = sem("p7_h_transform_done"), sem("p7_h_transform_copied"), sem("p7_squares_summed")
            sq7 = pb("sq7", [128, 2, GI, 64])
            block = p7.enter_context(nc.Block())
            xr7 = x.rearrange("i h w -> h i w")

            @block.sync
            def _(sp):
                sp.dma_start(qh[:, :], c["qh"]).then_inc(s_qh, 16)

                def load(b, u):
                    g = GPB * b + u
                    wait(sp, s_q7, g - 1)
                    sp.dma_start(mg[:, u % 2], mixr[:, bass.ds(g * GI, GI), :]).then_inc(s_mg[u % 2], 16)
                    sp.dma_start(xg[:, u % 2], xr7[:, bass.ds(g * GI, GI), :]).then_inc(s_mg[u % 2], 16)

                def body(b):
                    for u in range(GPB):
                        load(b, u)
                per_batch(sp, body)

            @block.gpsimd
            def _(pool):
                V = nc.gpsimd

                def scale(b, u):
                    g = GPB * b + u
                    pool.wait_ge(s_mg[u % 2], 32 * (nth(b, u) + 1))
                    V.tensor_tensor(mg[:, u % 2], mg[:, u % 2], bc(c2b[:, bass.ds(g * GI, GI)], 2, WW), ALU.mult).then_inc(s_m7, 1)

                def keep_output(b, u):
                    g = GPB * b + u
                    pool.wait_ge(s_add, g + 1)
                    pool.dma_start(yall[:, bass.ds(g * GI, GI), :], xn[:, u % 2]).then_inc(s_k[u % 2], 16)

                def body(b):
                    for u in range(GPB):
                        lagged(b, u, 0, scale)
                        lagged(b, u, 1, keep_output)
                per_batch(pool, body)
                keep_output(NB - 1, GPB - 1)
                for q in s_k:
                    pool.wait_ge(q, 16 * NGRP // 2)

            @block.tensor
            def _(pe):
                pe.wait_ge(s_qh, 16)

                def forward_h(b, u):
                    g = GPB * b + u
                    pe.wait_ge(s_add, g + 1)
                    wait(pe, s_e1, g)
                    for i in range(GI):
                        m = nc.tensor.matmul(pf[:, 128 * i:128 * i + 128], xn[:, u % 2, i, :], qh[:, :], start=True, stop=True)
                    m.then_inc(s_f1, 1)

                def body(b):
                    for u in range(GPB):
                        lagged(b, u, 0, lambda c_, v: inverse_h(pe, c_, v, ts, pz, s_ts, s_s1, s_z))
                        lagged(b, u, 1, forward_h)
                        lagged(b, u, 0, lambda c_, v: inverse_w(pe, c_, v, zs, pi, s_z, s_s2, s_add))
                per_batch(pe, body)
                forward_h(NB - 1, GPB - 1)

            @block.scalar
            def _(act):
                def stage(b, u):
                    g = GPB * b + u
                    wait(act, s_s1, g - 1)
                    act.activation(ts[:, u % 2], tt[:, :, bass.ds(g * GI, GI)], ACT.Copy).then_inc(s_ts, 1)

                def rows_back(b, u):
                    g = GPB * b + u
                    act.wait_ge(s_s1, g + 1)
                    wait(act, s_s2, g - 1)
                    act.activation(zs[:, u % 2], pz[:, :].rearrange("m (i h) -> m i h", i=GI), ACT.Copy).then_inc(s_z, 1)

                def forward_copy(b, u):
                    g = GPB * b + u
                    act.wait_ge(s_f1, g + 1)
                    v = pf[:, :].rearrange("w (i k) -> w i k", i=GI)
                    act.activation(y1[:, bass.ds(g * GI, GI), 0:65], v[:, :, 0:65], ACT.Copy)
                    act.activation(y1[:, bass.ds(g * GI, GI), 66:129], v[:, :, 65:128], ACT.Copy).then_inc(s_e1, 1)
                    act.wait_ge(s_e1, g + 1)
                    wait(act, s_sq7, g)
                    act.activation(sq7[:, 0], y1[:, bass.ds(g * GI, GI), 0:64], ACT.Square, accum_out=en8[:, 0, bass.ds(g, 1)])
                    act.activation(sq7[:, 1, :, 0:63], y1[:, bass.ds(g * GI, GI), 66:129], ACT.Square, accum_out=en8[:, 1, bass.ds(g, 1)]).then_inc(s_sq7, 1)

                def body(b):
                    for u in range(GPB):
                        lagged(b, u, 1, rows_back)
                        lagged(b, u, 0, stage)
                        lagged(b, u, 2, forward_copy)
                per_batch(act, body)
                rows_back(NB - 1, GPB - 1)
                forward_copy(NB - 1, GPB - 2)
                forward_copy(NB - 1, GPB - 1)
                act.wait_ge(s_sq7, NGRP)

            @block.vector
            def _(dve):
                V = nc.vector
                V.memset(y1[:, :, 65:130:64], 0.0)

                def hidden(b, u):
                    g = GPB * b + u
                    wait(dve, s_f1, g - 1)
                    wait(dve, s_k[u % 2], 16 * nth(b, u))
                    dve.wait_ge(s_mg[u % 2], 32 * (nth(b, u) + 1))
                    V.tensor_tensor(xn[:, u % 2], yall[:, bass.ds(g * GI, GI), :], bc(c1b[:, bass.ds(g * GI, GI)], 2, WW), ALU.mult).then_inc(s_h7, 1)
                    dve.wait_ge(s_h7, g + 1)
                    V.tensor_tensor(xn[:, u % 2], xn[:, u % 2], xg[:, u % 2], ALU.add).then_inc(s_p7, 1)
                    dve.wait_ge(s_p7, g + 1)
                    dve.wait_ge(s_m7, g + 1)
                    V.tensor_tensor(xn[:, u % 2], xn[:, u % 2], mg[:, u % 2], ALU.add).then_inc(s_q7, 1)
                    dve.wait_ge(s_q7, g + 1)
                    dve.wait_ge(s_s2, g + 1)
                    V.tensor_tensor(xn[:, u % 2], xn[:, u % 2], pi[:, :].rearrange("h (i w) -> h i w", i=GI), ALU.add).then_inc(s_add, 1)

                def body(b):
                    for u in range(GPB):
                        hidden(b, u)
                per_batch(dve, body)

        with ExitStack() as p8:
            def sb(name, shape):
                return p8.enter_context(nc.sbuf_tensor(name, shape, F32))

            def pb(name, shape):
                return p8.enter_context(nc.psum_tensor(name, shape, F32))

            yg = spare.rearrange("p (u i k) -> p u i k", u=2, i=GI)
            sq = sb("sq8", [128, NI, 2])
            en2 = sb("en8b", [128, NB, 2])
            enb = sb("en8c", [128, NB])
            mo = sb("mo8", [128, 2, NB])
            gs = sb("gs8", [128, 5, NB])
            xst = sb("xst8", [128, 2, GI, 2 * KWF])
            wa, wb8 = (sb(n, [128, 2 * KWF]) for n in ("wa", "wb8"))
            gmean = sb("gmean", [128, 128])
            px = [pb(f"px8_{i}", [128, 3 * 512]) for i in range(2)]
            pg = pb("pg8", [128, 512])
            s_ld = sem("p8_matrices_loaded")
            s_ws = sems("weight_slab_loaded", 3)
            wsl0 = tt[:, :, :].rearrange("p j i -> p (j i)")[:, 0:NT * SM].rearrange("p (o m) -> p o m", o=NT)

            def load_weights(sp, dst, s, done):
                for p in range(2):
                    row0 = (64 if p == 0 else 0) + SL * s
                    for r, w in enumerate((a["L1_conv_weight_real"], a["L1_conv_weight_imag"])):
                        q = slice(64 * p + 32 * r, 64 * p + 32 * r + 32)
                        sp.dma_start(dst[q], bass.AP(w.tensor, row0 * KWF, [[NT * HH * KWF, NT], [HH * KWF, NT], [1, SM]])).then_inc(done, 16)
            s_v8, s_mo8, s_gm8, s_rt8 = sem("p8_vector_steps"), sem("p8_moments_ready"), sem("p8_group_moments_ready"), sem("p8_scales_ready")
            s_sc8, s_yg = sem("p8_group_scaled"), sem("p8_group_normed")
            root = Root(sem("p8_root_asked"), sem("p8_root_given"))
            s_w8, s_p8, s_st8 = sem("p8_w_transform_done"), sem("p8_spectrum_copied"), sems("layer1_spectrum_stored", 2)
            block = p8.enter_context(nc.Block())

            @block.sync
            def _(sp):
                for t, n in ((wa, "wa"), (wb8, "wb8"), (gmean, "gmean")):
                    sp.dma_start(t[:, :], c[n]).then_inc(s_ld, 16)
                load_weights(sp, wsl0, 0, s_ws[0])

                def store(b):
                    for u in range(GPB):
                        g = GPB * b + u
                        sp.wait_ge(s_p8, g + 1)
                        sp.dma_start(x1s[u * GI:(u + 1) * GI, bass.ds(b, 1)].rearrange("i b s w -> s (i b) w"), xst[:, u % 2]).then_inc(s_st8[u % 2], 16)
                per_batch(sp, store)
                for q in s_st8:
                    sp.wait_ge(q, 16 * NGRP // 2)

            @block.tensor
            def _(pe):
                pe.wait_ge(s_ld, 48)
                pe.wait_ge(s_mo8, 1)
                nc.tensor.matmul(pg[:, 0:2 * NB], gmean[:, :], mo[:, :, :].rearrange("p a b -> p (a b)"), start=True, stop=True).then_inc(s_gm8, 1)

                def transform(b):
                    for u in range(GPB):
                        g = GPB * b + u
                        pe.wait_ge(s_yg, g + 1)
                        wait(pe, s_p8, g - 1)
                        for i in range(GI):
                            o = 512 * (i // 3) + 130 * (i % 3)
                            dst = px[u % 2][:, o:o + 130]
                            src = yg[:, u % 2, i]
                            nc.tensor.matmul(dst, src[:, 0:128], wa[:, :], start=True, stop=False)
                            m = nc.tensor.matmul(dst, src[:, 128:256], wb8[:, :], start=False, stop=True)
                        m.then_inc(s_w8, 1)
                per_batch(pe, transform)

            @block.scalar
            def _(act):
                root.serve(act, nc.scalar, gs[:, 2, :])
                act.wait_ge(s_rt8, 1)

                def norm(b):
                    for u in range(GPB):
                        g = GPB * b + u
                        wait(act, s_w8, g - 1)
                        for at, first, row in ((0, 0, 2), (64, 1, 2), (128, 65, 2), (192, 66, 4)):
                            m = act.activation(yg[:, u % 2, :, at:at + 64], y1[:, bass.ds(g * GI, GI), first:first + 64], ACT.Copy, scale=gs[:, row, b:b + 1])
                        m.then_inc(s_sc8, 1)
                        act.wait_ge(s_sc8, g + 1)
                        act.activation(yg[:, u % 2, :, 0:1], yg[:, u % 2, :, 0:1], ACT.Identity, bias=gs[:, 3, b:b + 1]).then_inc(s_yg, 1)
                for b in range(NB):
                    norm(b)

            @block.vector
            def _(dve):
                ch = Chain(dve, s_v8)
                V = nc.vector
                ch.link(V.reduce_sum(mo[:, 0, :], y1[:, :, 0].rearrange("w (b i) -> w b i", b=NB), axis=AX.X))
                ch.link(V.tensor_tensor(sq[:, :, :], y1[:, :, 0:65:64], y1[:, :, 0:65:64], ALU.mult))
                ch.link(V.reduce_sum(en2[:, :, :], sq[:, :, :].rearrange("w (b i) k -> w b k i", b=NB), axis=AX.X))
                ch.link(V.reduce_sum(mo[:, 1, :], en8[:, 0, :].rearrange("w (b q) -> w b q", b=NB), axis=AX.X))
                ch.link(V.reduce_sum(enb[:, :], en8[:, 1, :].rearrange("w (b q) -> w b q", b=NB), axis=AX.X))
                ch.link(V.tensor_tensor(mo[:, 1, :], mo[:, 1, :], enb[:, :], ALU.add))
                ch.link(V.tensor_scalar(mo[:, 1, :], mo[:, 1, :], 2.0, None, ALU.mult))
                ch.link(V.tensor_tensor(mo[:, 1, :], mo[:, 1, :], en2[:, :, 0], ALU.subtract))
                ch.link(V.tensor_tensor(mo[:, 1, :], mo[:, 1, :], en2[:, :, 1], ALU.add))
                V.tensor_scalar(mo[:, :, :], mo[:, :, :], 1.0 / NT, None, ALU.mult).then_inc(s_mo8, 1)
                dve.wait_ge(s_gm8, 1)
                ch.link(V.tensor_copy(gs[:, 0:2, :], pg[:, 0:2 * NB].rearrange("p (a b) -> p a b", a=2)))
                ch.link(V.tensor_tensor(gs[:, 2, :], gs[:, 0, :], gs[:, 0, :], ALU.mult))
                ch.link(V.tensor_tensor(gs[:, 2, :], gs[:, 1, :], gs[:, 2, :], ALU.subtract))
                root.rsqrt(dve, ch, V, gs[:, 2, :], gs[:, 2, :])
                ch.link(V.tensor_scalar(gs[:, 4, :], gs[:, 2, :], -1.0, None, ALU.mult))
                ch.link(V.tensor_tensor(gs[:, 3, :], gs[:, 0, :], gs[:, 2, :], ALU.mult))
                V.tensor_scalar(gs[:, 3, :], gs[:, 3, :], -1.0, None, ALU.mult).then_inc(s_rt8, 1)

                def copy(b):
                    for u in range(GPB):
                        g = GPB * b + u
                        dve.wait_ge(s_w8, g + 1)
                        wait(dve, s_st8[u % 2], 16 * nth(b, u))
                        for q in range(3):
                            n = min(3, GI - 3 * q)
                            m = V.tensor_copy(xst[:, u % 2, 3 * q:3 * q + n, :],
                                              px[u % 2][:, 512 * q:512 * q + 130 * n].rearrange("s (i w) -> s i w", i=n))
                        m.then_inc(s_p8, 1)
                per_batch(dve, copy)
        fwd.close()
        fac.close()

        with ExitStack() as p9:
            def sb(name, shape):
                return p9.enter_context(nc.sbuf_tensor(name, shape, F32))

            def pb(name, shape):
                return p9.enter_context(nc.psum_tensor(name, shape, F32))

            wsl = [wsl0] + [sb(f"wsl{i}", [128, NT, SM]) for i in (1, 2)]
            xsl1 = pa[:, :, :, :].rearrange("p w r h -> p (w r h)")[:, 0:2 * NB * 2 * SM]
            xsl = [sb("xsl0", [128, 2, NB, SL, 2, KWF]),
                   xsl1.rearrange("p (v b q r w) -> p v b q r w", v=2, b=NB, q=SL, r=2)]
            osl = [sb(f"osl{i}", [128, 2 * NB, 2 * KWF]) for i in range(2)]
            po = [pb(f"po9_{i}", [128, 3 * 512]) for i in range(2)]
            s_xl, s_os = sems("spectrum_slab_loaded", 2), sems("mixed_slab_stored", 2)
            s_ms, s_oc = sem("slab_mixed"), sem("mixed_slab_copied")
            s_sw, s_ng = sem("imaginary_rows_ready"), sem("negative_rows_ready")
            s_free = sem("slab_buffers_cleared")
            block = p9.enter_context(nc.Block())

            def slabs(eng, step):
                with eng.Fori(0, NSLAB // 6) as i:
                    for n in range(6):
                        step(6 * i + n, n, 2 * i + n // 3)
                for n in range(NSLAB // 6 * 6, NSLAB):
                    step(n, n % 6, n // 3)

            @block.sync
            def _(sp):
                def load(s, n):
                    u = n % 2
                    wait(sp, s_ms, s - 1)
                    for p in range(2):
                        slot0 = SL * s if p == 0 else HH - SL - SL * s
                        sp.dma_start(xsl[u][64 * p:64 * p + 32, p].rearrange("i b s r w -> i b (s r w)"),
                                     bass.AP(x1s.tensor, slot0 * 2 * KWF, [[NB * HH * 2 * KWF, NT], [HH * 2 * KWF, NB], [1, 2 * SM]])).then_inc(s_xl[u], 16)

                def load_ahead(s, n):
                    wait(sp, s_ms, s - 1)
                    load_weights(sp, wsl[(n + 1) % 3], s + 1, s_ws[(n + 1) % 3])
                load(0, 0)
                load_weights(sp, wsl[1], 1, s_ws[1])
                load(1, 1)
                load_weights(sp, wsl[2], 2, s_ws[2])
                for s in range(2, 6):
                    load(s, s)
                    load_ahead(s, s)
                with sp.Fori(1, NSLAB // 6) as i:
                    for n in range(6):
                        load(6 * i + n, n)
                        load_ahead(6 * i + n, n)
                for s in range(NSLAB // 6 * 6, NSLAB):
                    load(s, s % 6)
                    if s < NSLAB - 1:
                        load_ahead(s, s % 6)

            @block.gpsimd
            def _(pool):
                nc.gpsimd.memset(xsl[1][0:64, 1], 0.0)
                nc.gpsimd.memset(xsl[1][64:128, 0], 0.0).then_inc(s_free, 1)

            @block.tensor
            def _(pe):
                pe.wait_ge(s_free, 2)
                def mix(s, n, wturn):
                    u = n % 2
                    pe.wait_ge(s_ws[n % 3], 64 * (wturn + 1))
                    pe.wait_ge(s_sw, s + 1)
                    pe.wait_ge(s_ng, s + 1)
                    pe.wait_ge(s_oc, s + 1)
                    for kw in range(KWF):
                        for q in range(SL):
                            v = xsl[u][:, 0, 0, q, 0, kw:kw + 1]
                            mov = bass.AP(v.tensor, v.offset, [list(v.ap[0]), [NB * 2 * SM + (SL - 1 - 2 * q) * 2 * KWF, 2],
                                                               [2 * SM, NB], [KWF, 2]])
                            m = nc.tensor.matmul(po[u][32 * q:32 * q + 32, 16 * kw:16 * kw + 16],
                                                 wsl[n % 3][:, :, q * KWF + KWF - 1 - kw], mov, start=True, stop=True)
                    m.then_inc(s_ms, 1)
                slabs(pe, mix)

            @block.vector
            def _(dve):
                V = nc.vector
                V.memset(xsl[0][0:64, 1], 0.0)
                V.memset(xsl[0][64:128, 0], 0.0).then_inc(s_free, 1)
                V.memset(osl[0][:, :, 0:1], 0.0).then_inc(s_oc, 1)
                V.memset(osl[1][:, :, 0:1], 0.0).then_inc(s_oc, 1)

                def negate(i, u):
                    dve.wait_ge(s_xl[u], 32 * (i + 1))
                    for p in range(2):
                        m = V.tensor_scalar(xsl[u][64 * p + 32:64 * p + 64, p, :, :, 1], xsl[u][64 * p:64 * p + 32, p, :, :, 0], -1.0, None, ALU.mult)
                    m.then_inc(s_ng, 1)

                def copy(i, u):
                    s = 2 * i + u
                    dve.wait_ge(s_ms, s + 1)
                    wait(dve, s_os[u], 16 * 8 * i)
                    v = po[u][:, 0:16 * KWF].rearrange("p (w c z) -> p z c w", w=KWF, z=2)
                    V.tensor_copy(osl[u][:, :, 0:KWF], v[:, 0])
                    V.tensor_copy(osl[u][:, :, KWF:2 * KWF - 1], v[:, 1, :, 1:KWF])
                    V.tensor_copy(osl[u][:, :, 2 * KWF - 1:2 * KWF], v[:, 1, :, 0:1]).then_inc(s_oc, 1)
                negate(0, 0)
                negate(0, 1)
                copy(0, 0)
                with dve.Fori(1, NSLAB // 2) as i:
                    negate(i, 0)
                    copy(i - 1, 1)
                    negate(i, 1)
                    copy(i, 0)
                copy(NSLAB // 2 - 1, 1)

            @block.scalar
            def _(act):
                def imaginary(i, u):
                    act.wait_ge(s_xl[u], 32 * (i + 1))
                    for p in range(2):
                        m = act.activation(xsl[u][64 * p + 32:64 * p + 64, p, :, :, 0], xsl[u][64 * p:64 * p + 32, p, :, :, 1], ACT.Copy)
                    m.then_inc(s_sw, 1)

                def store(i, u):
                    s = 2 * i + u
                    act.wait_ge(s_oc, s + 3)
                    for q in range(SL):
                        for p in range(2):
                            slot = SL * s + q if p == 0 else HH - 1 - SL * s - q
                            act.dma_start(bass.AP(os_.tensor, slot * 2 * KWF, [[NB * HH * 2 * KWF, NT], [HH * 2 * KWF, NB], [1, 2 * KWF]]),
                                          osl[u][32 * q:32 * q + 32, NB * p:NB * p + NB]).then_inc(s_os[u], 16)
                imaginary(0, 0)
                imaginary(0, 1)
                store(0, 0)
                with act.Fori(1, NSLAB // 2) as i:
                    imaginary(i, 0)
                    store(i - 1, 1)
                    imaginary(i, 1)
                    store(i, 0)
                store(NSLAB // 2 - 1, 1)
                for q in s_os:
                    act.wait_ge(q, 16 * 8 * NSLAB // 2)

        spec.close()
        with ExitStack() as p10:
            def sb(name, shape):
                return p10.enter_context(nc.sbuf_tensor(name, shape, F32))

            def pb(name, shape):
                return p10.enter_context(nc.psum_tensor(name, shape, F32))

            od = sb("od", [128, GPB, GI, 2 * KWF])
            ob = sb("ob", [128, 2, GI, 128])
            zz = sb("zz", [128, 2, GI, 128])
            ec, es, cf = sb("ec", [128, 128]), sb("es", [128, 128]), sb("cf", [128, 128])
            pz = [pb(f"pz10_{i}", [128, 1024]) for i in range(2)]
            pi = [pb(f"pi10_{i}", [128, 1024]) for i in range(2)]
            s_cl = sem("p10_matrices_loaded")
            s_od, s_ob, s_h, s_hc = sems("p10_spectra_loaded", GPB), sem("p10_second_parts_ready"), sem("p10_rows_done"), sem("p10_rows_copied")
            s_w, s_fin, s_st = sem("p10_pixels_done"), sem("output_ready"), sem("output_stored")
            block = p10.enter_context(nc.Block())

            @block.sync
            def _(sp):
                def load(b, u):
                    g = GPB * b + u
                    wait(sp, s_h, g + 1 - GPB)
                    sp.dma_start(od[:, u], os_[u * GI:(u + 1) * GI, bass.ds(b, 1)].rearrange("i b s w -> s (i b) w")).then_inc(s_od[u], 16)

                def store(b, u):
                    g = GPB * b + u
                    sp.wait_ge(s_fin, g + 1)
                    sp.dma_start(xo.rearrange("i h w -> h i w")[:, bass.ds(g * GI, GI), :], yall[:, bass.ds(g * GI, GI), :]).then_inc(s_st, 16)

                def body(b):
                    for u in range(GPB):
                        lagged(b, u, 0, load)
                        if isinstance(b, int) and u == 1:
                            for t, n in ((ec, "ec"), (es, "es"), (cf, "cf")):
                                sp.dma_start(t[:, :], c[n]).then_inc(s_cl, 16)
                        lagged(b, u, 3, store)
                per_batch(sp, body)
                for k in (3, 2, 1):
                    store(NB - 1, GPB - k)
                sp.wait_ge(s_st, 16 * NGRP)

            @block.tensor
            def _(pe):
                pe.wait_ge(s_cl, 48)

                def rows_back(b, u):
                    g = GPB * b + u
                    pe.wait_ge(s_od[u], 16 * (b + 1))
                    pe.wait_ge(s_ob, g + 1)
                    wait(pe, s_hc, g - 1)
                    for j in range(GI):
                        nc.tensor.matmul(pz[u % 2][:, 128 * j:128 * j + 128], od[:, u, j, 0:128], ec[:, :], start=True, stop=False)
                        m = nc.tensor.matmul(pz[u % 2][:, 128 * j:128 * j + 128], ob[:, u % 2, j, :], es[:, :], start=False, stop=True)
                    m.then_inc(s_h, 1)

                def pixels(b, u):
                    g = GPB * b + u
                    pe.wait_ge(s_hc, g + 1)
                    wait(pe, s_fin, g - 1)
                    for j in range(GI):
                        m = nc.tensor.matmul(pi[u % 2][:, 128 * j:128 * j + 128], zz[:, u % 2, j, :], cf[:, :], start=True, stop=True)
                    m.then_inc(s_w, 1)

                def body(b):
                    for u in range(GPB):
                        lagged(b, u, 0, rows_back)
                        lagged(b, u, 1, pixels)
                per_batch(pe, body)
                pixels(NB - 1, GPB - 1)

            @block.scalar
            def _(act):
                def second(b, u):
                    g = GPB * b + u
                    act.wait_ge(s_od[u], 16 * (b + 1))
                    wait(act, s_h, g - 1)
                    act.activation(ob[:, u % 2, :, 0:1], od[:, u, :, 129:130], ACT.Copy)
                    act.activation(ob[:, u % 2, :, 1:65], od[:, u, :, 65:129], ACT.Copy)
                    act.activation(ob[:, u % 2, :, 65:128], od[:, u, :, 1:64], ACT.Copy, scale=-1.0).then_inc(s_ob, 1)

                def rows_copy(b, u):
                    g = GPB * b + u
                    act.wait_ge(s_h, g + 1)
                    wait(act, s_w, g - 1)
                    act.activation(zz[:, u % 2], pz[u % 2][:, :].rearrange("k (j e) -> k j e", j=GI), ACT.Copy).then_inc(s_hc, 1)

                def body(b):
                    for u in range(GPB):
                        lagged(b, u, 0, second)
                        lagged(b, u, 1, rows_copy)
                per_batch(act, body)
                rows_copy(NB - 1, GPB - 1)

            @block.vector
            def _(dve):
                V = nc.vector

                def body(b):
                    for u in range(GPB):
                        g = GPB * b + u
                        dve.wait_ge(s_w, g + 1)
                        y = yall[:, bass.ds(g * GI, GI), :]
                        V.tensor_tensor(y, y, pi[u % 2][:, :].rearrange("h (i w) -> h i w", i=GI), ALU.add).then_inc(s_fin, 1)
                per_batch(dve, body)


_INS = ["x"] + ["L0_conv_" + n for n in (
    "norm1_w", "norm1_b", "Kcw", "Ksw", "Qcw", "Qsw", "Vcw", "Vsw", "Pcw", "Psw", "attn_w", "attn_b",
    "norm2_w", "norm2_b", "m0cw", "m0sw", "m1cw", "m1sw", "mon_w", "mon_b")] + ["L1_conv_weight_real", "L1_conv_weight_imag"]


def kernel(**inputs):
    import numpy as _np
    import concourse.bacc as _bacc
    from concourse import mybir as _mybir
    from concourse.bass_utils import run_bass_kernel_spmd as _run

    nc = _bacc.Bacc("TRN2", target_bir_lowering=False, num_devices=1)
    arrays, a, c = {}, {}, {}
    for name in _INS:
        v = _np.ascontiguousarray(inputs[name])
        arrays[f"in_{name}_dram"] = v
        a[name] = nc.dram_tensor(f"in_{name}_dram", v.shape, _mybir.dt.from_np(v.dtype), kind="ExternalInput").ap()
    for name, v in constants().items():
        arrays[f"const_{name}_dram"] = v
        c[name] = nc.dram_tensor(f"const_{name}_dram", v.shape, _mybir.dt.float32, kind="ExternalInput").ap()
    out = nc.dram_tensor("out_0_dram", (NB, NT, HH, WW), _mybir.dt.float32, kind="ExternalOutput").ap()
    build(nc, a, c, out)
    r = _run(nc, [arrays], core_ids=[0])
    return r.results[0]["out_0_dram"]
```
